# Optimizing a Trainium2 kernel written in Bass

```python
import numpy as np
import jax
import jax.numpy as jnp

def _softmax(x, axis=-1):
    return jax.nn.softmax(x, axis=axis)

def _gelu(x):
    return jax.nn.gelu(x, approximate=True)

def _silu(x):
    return jax.nn.silu(x)

def _sigmoid(x):
    return jax.nn.sigmoid(x)

def _layernorm(x, axis=-1, eps=1e-05):
    m = jnp.mean(x, axis=axis, keepdims=True)
    v = jnp.var(x, axis=axis, keepdims=True)
    return (x - m) / jnp.sqrt(v + eps)

def _scatter_add(tgt, idx, src, axis=0):
    return tgt.at[idx].add(src)

def _segment_sum(src, seg, n):
    return jax.ops.segment_sum(src, seg, n)
kernel_name = 'mk_gnn_preln_d4_gnn_r16_e114c2'

def setup_inputs(seed: int=0):
    np.random.seed(seed)
    _w = jnp.asarray

    def _rec_inputs():
        import jax
        import jax.numpy as jnp
        _gk = jax.random.key(seed)
        x = -0.000202 + 1 * jax.random.normal(jax.random.fold_in(_gk, 1), (6250, 128), jnp.float32)
        src = jax.random.randint(jax.random.fold_in(_gk, 2), (100000,), 0, 6250, jnp.int32)
        dst = jax.random.randint(jax.random.fold_in(_gk, 3), (100000,), 0, 6250, jnp.int32)
        _o = jnp.argsort(dst, stable=True)
        src = src[_o]
        dst = dst[_o]
        edge_attr_128 = jax.random.uniform(jax.random.fold_in(_gk, 13), (100000, 128), jnp.float32, 0.0, 1)
        edge_attr_3 = 0.000669165 + 0.999965 * jax.random.normal(jax.random.fold_in(_gk, 14), (100000, 3), jnp.float32)
        edge_weight = jax.random.uniform(jax.random.fold_in(_gk, 16), (100000,), jnp.float32, 0.0, 4.99999)
        return (x, src, dst, edge_attr_128, edge_attr_3, edge_weight)
    x, src, dst, edge_attr_128, edge_attr_3, edge_weight = _rec_inputs()

    def _L0_gnn_setup():
        import jax, jax.numpy as jnp
        import numpy as np
        N_NODES = 3125
        IN_DIM = 128
        OUT_DIM = 128
        N_EDGES = 50000
        key = jax.random.key(seed)
        k_x, k_e, k_ws, k_wn = jax.random.split(key, 4)
        x = jax.random.normal(k_x, (N_NODES, IN_DIM), dtype=jnp.float32)
        edge_index = jax.random.randint(k_e, (2, N_EDGES), 0, N_NODES, dtype=jnp.int64)
        lim = 1.0 / np.sqrt(IN_DIM)
        W_self = jax.random.uniform(k_ws, (OUT_DIM, IN_DIM), jnp.float32, -lim, lim)
        W_neigh = jax.random.uniform(k_wn, (OUT_DIM, IN_DIM), jnp.float32, -lim, lim)
        bias = jnp.zeros((OUT_DIM,), jnp.float32)
        return {'x': x, 'edge_index': edge_index, 'W_self': W_self, 'W_neigh': W_neigh, 'bias': bias}
    _L0_gnn_all = _L0_gnn_setup()
    _L0_gnn_in = {k: v for k, v in _L0_gnn_all.items() if k in ('W_self', 'W_neigh', 'bias')}
    del _L0_gnn_all

    def _L1_gnn_setup():
        import jax, jax.numpy as jnp
        import numpy as np
        IN_FEATS = 128
        OUT_FEATS = 128
        N_NODES = 1250
        N_EDGES = 40000
        R_MIN, R_MAX = (0.0, 5.0)
        LN2 = 0.6931471805599453

        def ssp(x):
            return jax.nn.softplus(x) - LN2
        key = jax.random.key(seed)
        ks = jax.random.split(key, 12)
        h = jax.random.normal(ks[0], (N_NODES, IN_FEATS), dtype=jnp.float32)
        edge_feat = jax.random.uniform(ks[1], (N_EDGES, IN_FEATS), dtype=jnp.float32)
        dist = jax.random.uniform(ks[2], (N_EDGES,), dtype=jnp.float32) * R_MAX
        src = jax.random.randint(ks[3], (N_EDGES,), 0, N_NODES)
        dst = jax.random.randint(ks[4], (N_EDGES,), 0, N_NODES)
        s = 0.1
        W1 = jax.random.normal(ks[5], (IN_FEATS, IN_FEATS), dtype=jnp.float32) * s
        b1 = jnp.zeros((IN_FEATS,), dtype=jnp.float32)
        W2 = jax.random.normal(ks[6], (IN_FEATS, IN_FEATS), dtype=jnp.float32) * s
        b2 = jnp.zeros((IN_FEATS,), dtype=jnp.float32)
        W3 = jax.random.normal(ks[7], (IN_FEATS, OUT_FEATS), dtype=jnp.float32) * s
        b3 = jnp.zeros((OUT_FEATS,), dtype=jnp.float32)
        return {'h': h, 'edge_feat': edge_feat, 'dist': dist, 'src': src, 'dst': dst, 'W1': W1, 'b1': b1, 'W2': W2, 'b2': b2, 'W3': W3, 'b3': b3}
    _L1_gnn_all = _L1_gnn_setup()
    _L1_gnn_in = {k: v for k, v in _L1_gnn_all.items() if k in ('W1', 'b1', 'W2', 'b2', 'W3', 'b3')}
    del _L1_gnn_all

    def _L2_gnn_setup():
        import jax, jax.numpy as jnp
        import numpy as np
        N_NODES = 6250
        N_EDGES = 100000
        D = 128
        N_LAYERS = 3

        def _sage_layer(x, src, dst, Wl, Wr, bias, n_nodes):
            msg_sum = jax.ops.segment_sum(x[src], dst, num_segments=n_nodes)
            cnt = jax.ops.segment_sum(jnp.ones((src.shape[0], 1), x.dtype), dst, num_segments=n_nodes)
            mean = msg_sum / jnp.maximum(cnt, 1.0)
            return mean @ Wl + x @ Wr + bias
        key = jax.random.key(seed)
        k1, k2, k3, k4, k5 = jax.random.split(key, 5)
        scale = 1.0 / np.sqrt(D)
        x = jax.random.normal(k1, (N_NODES, D), dtype=jnp.float32)
        edge_index = jax.random.randint(k2, (2, N_EDGES), 0, N_NODES, dtype=jnp.int64)
        W_agg = jax.random.normal(k3, (N_LAYERS, D, D), dtype=jnp.float32) * scale
        W_root = jax.random.normal(k4, (N_LAYERS, D, D), dtype=jnp.float32) * scale
        b = jax.random.normal(k5, (N_LAYERS, D), dtype=jnp.float32) * scale
        return {'x': x, 'edge_index': edge_index, 'W_agg': W_agg, 'W_root': W_root, 'b': b}
    _L2_gnn_all = _L2_gnn_setup()
    _L2_gnn_in = {k: v for k, v in _L2_gnn_all.items() if k in ('W_agg', 'W_root', 'b')}
    del _L2_gnn_all

    def _L3_gnn_setup():
        import jax, jax.numpy as jnp
        import numpy as np
        N, E, IN, H, ED = (3125, 50000, 128, 128, 3)
        EPS = 1e-05

        def _gat_conv(x, src, dst, ea, W, a_src, a_dst, We, a_edge, bias):
            n = x.shape[0]
            loops = jnp.arange(n, dtype=src.dtype)
            s = jnp.concatenate([src, loops])
            d = jnp.concatenate([dst, loops])
            ea_full = jnp.concatenate([ea, jnp.broadcast_to(ea.mean(0), (n, ea.shape[1]))], 0)
            h = x @ W
            al_s = h @ a_src
            al_d = h @ a_dst
            al_e = ea_full @ We @ a_edge
            alpha = jax.nn.leaky_relu(al_s[s] + al_d[d] + al_e, 0.2)
            amax = jax.ops.segment_max(alpha, d, num_segments=n)
            ex = jnp.exp(alpha - amax[d])
            denom = jax.ops.segment_sum(ex, d, num_segments=n)
            coef = ex / (denom[d] + 1e-16)
            out = jax.ops.segment_sum(h[s] * coef[:, None], d, num_segments=n)
            return out + bias

        def _bn(x, gamma, beta):
            mu = x.mean(0)
            var = ((x - mu) ** 2).mean(0)
            return (x - mu) * jax.lax.rsqrt(var + EPS) * gamma + beta
        key = jax.random.key(seed)
        ks = jax.random.split(key, 40)
        inp = {'x': jax.random.normal(ks[0], (N, IN), jnp.float32), 'edge_index': jax.random.randint(ks[1], (2, E), 0, N, dtype=jnp.int32), 'batch': jnp.zeros((N,), jnp.int32), 'edge_attr': jax.random.normal(ks[2], (E, ED), jnp.float32)}
        i = 3
        for l, cin in ((1, IN), (2, H), (3, H)):
            s = 1.0 / np.sqrt(cin)
            inp[f'W{l}'] = jax.random.normal(ks[i], (cin, H), jnp.float32) * s
            i += 1
            inp[f'as{l}'] = jax.random.normal(ks[i], (H,), jnp.float32) * 0.1
            i += 1
            inp[f'ad{l}'] = jax.random.normal(ks[i], (H,), jnp.float32) * 0.1
            i += 1
            inp[f'We{l}'] = jax.random.normal(ks[i], (ED, H), jnp.float32) * 0.5
            i += 1
            inp[f'ae{l}'] = jax.random.normal(ks[i], (H,), jnp.float32) * 0.1
            i += 1
            inp[f'b{l}'] = jnp.zeros((H,), jnp.float32)
            inp[f'g{l}'] = jnp.ones((H,), jnp.float32)
            inp[f'be{l}'] = jnp.zeros((H,), jnp.float32)
        return inp
    _L3_gnn_all = _L3_gnn_setup()
    _L3_gnn_in = {k: v for k, v in _L3_gnn_all.items() if k in ('W1', 'as1', 'ad1', 'We1', 'ae1', 'b1', 'g1', 'be1', 'W2', 'as2', 'ad2', 'We2', 'ae2', 'b2', 'g2', 'be2', 'W3', 'as3', 'ad3', 'We3', 'ae3', 'b3', 'g3', 'be3')}
    del _L3_gnn_all
    return {'x': x, 'src': src, 'dst': dst, 'edge_attr_128': edge_attr_128, 'edge_attr_3': edge_attr_3, 'edge_weight': edge_weight, 'L0_gnn_W_self': _L0_gnn_in['W_self'], 'L0_gnn_W_neigh': _L0_gnn_in['W_neigh'], 'L0_gnn_bias': _L0_gnn_in['bias'], 'L1_gnn_W1': _L1_gnn_in['W1'], 'L1_gnn_b1': _L1_gnn_in['b1'], 'L1_gnn_W2': _L1_gnn_in['W2'], 'L1_gnn_b2': _L1_gnn_in['b2'], 'L1_gnn_W3': _L1_gnn_in['W3'], 'L1_gnn_b3': _L1_gnn_in['b3'], 'L2_gnn_W_agg': _L2_gnn_in['W_agg'], 'L2_gnn_W_root': _L2_gnn_in['W_root'], 'L2_gnn_b': _L2_gnn_in['b'], 'L3_gnn_W1': _L3_gnn_in['W1'], 'L3_gnn_as1': _L3_gnn_in['as1'], 'L3_gnn_ad1': _L3_gnn_in['ad1'], 'L3_gnn_We1': _L3_gnn_in['We1'], 'L3_gnn_ae1': _L3_gnn_in['ae1'], 'L3_gnn_b1': _L3_gnn_in['b1'], 'L3_gnn_g1': _L3_gnn_in['g1'], 'L3_gnn_be1': _L3_gnn_in['be1'], 'L3_gnn_W2': _L3_gnn_in['W2'], 'L3_gnn_as2': _L3_gnn_in['as2'], 'L3_gnn_ad2': _L3_gnn_in['ad2'], 'L3_gnn_We2': _L3_gnn_in['We2'], 'L3_gnn_ae2': _L3_gnn_in['ae2'], 'L3_gnn_b2': _L3_gnn_in['b2'], 'L3_gnn_g2': _L3_gnn_in['g2'], 'L3_gnn_be2': _L3_gnn_in['be2'], 'L3_gnn_W3': _L3_gnn_in['W3'], 'L3_gnn_as3': _L3_gnn_in['as3'], 'L3_gnn_ad3': _L3_gnn_in['ad3'], 'L3_gnn_We3': _L3_gnn_in['We3'], 'L3_gnn_ae3': _L3_gnn_in['ae3'], 'L3_gnn_b3': _L3_gnn_in['b3'], 'L3_gnn_g3': _L3_gnn_in['g3'], 'L3_gnn_be3': _L3_gnn_in['be3']}

def reference(x, src, dst, edge_attr_128, edge_attr_3, edge_weight, L0_gnn_W_self, L0_gnn_W_neigh, L0_gnn_bias, L1_gnn_W1, L1_gnn_b1, L1_gnn_W2, L1_gnn_b2, L1_gnn_W3, L1_gnn_b3, L2_gnn_W_agg, L2_gnn_W_root, L2_gnn_b, L3_gnn_W1, L3_gnn_as1, L3_gnn_ad1, L3_gnn_We1, L3_gnn_ae1, L3_gnn_b1, L3_gnn_g1, L3_gnn_be1, L3_gnn_W2, L3_gnn_as2, L3_gnn_ad2, L3_gnn_We2, L3_gnn_ae2, L3_gnn_b2, L3_gnn_g2, L3_gnn_be2, L3_gnn_W3, L3_gnn_as3, L3_gnn_ad3, L3_gnn_We3, L3_gnn_ae3, L3_gnn_b3, L3_gnn_g3, L3_gnn_be3):
    import jax
    import jax.numpy as jnp

    def _L0_gnn_ref(x, edge_index, W_self, W_neigh, bias):
        import jax, jax.numpy as jnp
        import numpy as np
        N_NODES = 3125
        IN_DIM = 128
        OUT_DIM = 128
        N_EDGES = 50000
        n_nodes = x.shape[0]
        src, dst = (edge_index[0], edge_index[1])
        agg = jax.ops.segment_sum(x[src], dst, num_segments=n_nodes)
        count = jax.ops.segment_sum(jnp.ones((src.shape[0],), x.dtype), dst, num_segments=n_nodes)
        agg = agg / jnp.maximum(count, 1.0)[:, None]
        h = x @ W_self.T + agg @ W_neigh.T + bias
        return jax.nn.relu(h)

    def _L1_gnn_ref(h, edge_feat, dist, src, dst, W1, b1, W2, b2, W3, b3):
        import jax, jax.numpy as jnp
        import numpy as np
        IN_FEATS = 128
        OUT_FEATS = 128
        N_NODES = 1250
        N_EDGES = 40000
        R_MIN, R_MAX = (0.0, 5.0)
        LN2 = 0.6931471805599453

        def ssp(x):
            return jax.nn.softplus(x) - LN2
        n_nodes = h.shape[0]
        centers = jnp.linspace(R_MIN, R_MAX, IN_FEATS, dtype=jnp.float32)
        delta = (R_MAX - R_MIN) / (IN_FEATS - 1)
        coeff = -0.5 / (delta * delta)
        bf = jnp.exp(coeff * (dist[:, None] - centers[None, :]) ** 2)
        bf = ssp(bf @ W1 + b1)
        bf = ssp(bf @ W2 + b2)
        cut = jnp.where(dist < R_MAX, 0.5 * (jnp.cos(jnp.pi * dist / R_MAX) + 1.0), 0.0)
        msg = h[src] * edge_feat * bf * cut[:, None]
        agg = jax.ops.segment_prod(msg, dst, num_segments=n_nodes)
        out = ssp(agg @ W3 + b3)
        return out

    def _L2_gnn_ref(x, edge_index, W_agg, W_root, b):
        import jax, jax.numpy as jnp
        import numpy as np
        N_NODES = 6250
        N_EDGES = 100000
        D = 128
        N_LAYERS = 3

        def _sage_layer(x, src, dst, Wl, Wr, bias, n_nodes):
            msg_sum = jax.ops.segment_sum(x[src], dst, num_segments=n_nodes)
            cnt = jax.ops.segment_sum(jnp.ones((src.shape[0], 1), x.dtype), dst, num_segments=n_nodes)
            mean = msg_sum / jnp.maximum(cnt, 1.0)
            return mean @ Wl + x @ Wr + bias
        src, dst = (edge_index[0], edge_index[1])
        n = x.shape[0]
        for i in range(N_LAYERS - 1):
            x = _sage_layer(x, src, dst, W_agg[i], W_root[i], b[i], n)
            x = jax.nn.relu(x)
        x = _sage_layer(x, src, dst, W_agg[-1], W_root[-1], b[-1], n)
        return x

    def _L3_gnn_ref(x, edge_index, batch, edge_attr, W1, as1, ad1, We1, ae1, b1, g1, be1, W2, as2, ad2, We2, ae2, b2, g2, be2, W3, as3, ad3, We3, ae3, b3, g3, be3):
        import jax, jax.numpy as jnp
        import numpy as np
        N, E, IN, H, ED = (3125, 50000, 128, 128, 3)
        EPS = 1e-05

        def _gat_conv(x, src, dst, ea, W, a_src, a_dst, We, a_edge, bias):
            n = x.shape[0]
            loops = jnp.arange(n, dtype=src.dtype)
            s = jnp.concatenate([src, loops])
            d = jnp.concatenate([dst, loops])
            ea_full = jnp.concatenate([ea, jnp.broadcast_to(ea.mean(0), (n, ea.shape[1]))], 0)
            h = x @ W
            al_s = h @ a_src
            al_d = h @ a_dst
            al_e = ea_full @ We @ a_edge
            alpha = jax.nn.leaky_relu(al_s[s] + al_d[d] + al_e, 0.2)
            amax = jax.ops.segment_max(alpha, d, num_segments=n)
            ex = jnp.exp(alpha - amax[d])
            denom = jax.ops.segment_sum(ex, d, num_segments=n)
            coef = ex / (denom[d] + 1e-16)
            out = jax.ops.segment_sum(h[s] * coef[:, None], d, num_segments=n)
            return out + bias

        def _bn(x, gamma, beta):
            mu = x.mean(0)
            var = ((x - mu) ** 2).mean(0)
            return (x - mu) * jax.lax.rsqrt(var + EPS) * gamma + beta
        src, dst = (edge_index[0], edge_index[1])
        h = _gat_conv(x, src, dst, edge_attr, W1, as1, ad1, We1, ae1, b1)
        h = _bn(jax.nn.leaky_relu(h, 0.01), g1, be1)
        h = _gat_conv(h, src, dst, edge_attr, W2, as2, ad2, We2, ae2, b2)
        h = _bn(jax.nn.leaky_relu(h, 0.01), g2, be2)
        h = _gat_conv(h, src, dst, edge_attr, W3, as3, ad3, We3, ae3, b3)
        h = _bn(jax.nn.leaky_relu(h, 0.01), g3, be3)
        return h
    edge_index = jnp.stack([src, dst])
    batch0 = jnp.zeros((6250,), jnp.int32)
    h = jnp.maximum(_layernorm(x, axis=-1), 0.0)
    x = x + _L0_gnn_ref(h, edge_index, L0_gnn_W_self, L0_gnn_W_neigh, L0_gnn_bias)
    h = jnp.maximum(_layernorm(x, axis=-1), 0.0)
    x = x + _L1_gnn_ref(h, edge_attr_128, edge_weight, src, dst, L1_gnn_W1, L1_gnn_b1, L1_gnn_W2, L1_gnn_b2, L1_gnn_W3, L1_gnn_b3)
    h = jnp.maximum(_layernorm(x, axis=-1), 0.0)
    x = x + _L2_gnn_ref(h, edge_index, L2_gnn_W_agg, L2_gnn_W_root, L2_gnn_b)
    h = jnp.maximum(_layernorm(x, axis=-1), 0.0)
    x = x + _L3_gnn_ref(h, edge_index, batch0, edge_attr_3, L3_gnn_W1, L3_gnn_as1, L3_gnn_ad1, L3_gnn_We1, L3_gnn_ae1, L3_gnn_b1, L3_gnn_g1, L3_gnn_be1, L3_gnn_W2, L3_gnn_as2, L3_gnn_ad2, L3_gnn_We2, L3_gnn_ae2, L3_gnn_b2, L3_gnn_g2, L3_gnn_be2, L3_gnn_W3, L3_gnn_as3, L3_gnn_ad3, L3_gnn_We3, L3_gnn_ae3, L3_gnn_b3, L3_gnn_g3, L3_gnn_be3)
    return x

_drawn_inputs = setup_inputs


def setup_inputs(seed=0):
    import zlib

    import numpy as np

    out = dict(_drawn_inputs(seed))
    spreads = {'L0_gnn_bias': (0.0, 0.1),
     'L1_gnn_b1': (0.0, 0.8),
     'L1_gnn_b2': (0.0, 0.8),
     'L1_gnn_b3': (0.0, 0.1),
     'L3_gnn_b1': (0.0, 0.1),
     'L3_gnn_g1': (1.0, 0.2),
     'L3_gnn_be1': (0.0, 0.1),
     'L3_gnn_b2': (0.0, 0.1),
     'L3_gnn_g2': (1.0, 0.2),
     'L3_gnn_be2': (0.0, 0.1),
     'L3_gnn_b3': (0.0, 0.1),
     'L3_gnn_g3': (1.0, 0.2),
     'L3_gnn_be3': (0.0, 0.1)}
    factors = {'edge_attr_128': 8.0,
     'edge_weight': 8.0,
     'L1_gnn_W1': 8.0,
     'L1_gnn_W2': 8.0,
     'L1_gnn_W3': 8.0}
    for name, (base, spread) in spreads.items():
        noise = np.random.default_rng([zlib.crc32(name.encode()), seed]).standard_normal(out[name].shape)
        drawn = base * np.exp(spread * noise) if base else spread * noise
        out[name] = jnp.asarray(drawn.astype(out[name].dtype))
    for name, factor in factors.items():
        out[name] = (out[name] * factor).astype(out[name].dtype)
    return out
```

```python
from contextlib import ExitStack

import numpy as np
import concourse.bass as bass
from concourse import mybir

ALU = mybir.AluOpType
ACT = mybir.ActivationFunctionType
F32 = mybir.dt.float32
I32 = mybir.dt.int32
BF16 = mybir.dt.bfloat16
AX = mybir.AxisListType

P = 128
N, E, D = 6250, 100000, 128
NT = -(-N // P)
NPAD = NT * P
NLAST = N - (NT - 1) * P
CH = 7
NCH = NT // CH
CW = CH * D
ET = 784
EPAD = ET * P
HT = 8
BT = 2 * HT
ITERS = ET // BT
BE = BT * P
TB = 112
NB = ET // TB
ACCW = 6400
SROWS = E - (P - 1) * ET
BIGPOS = float(1 << 20)
HUGE = 1.0e30
LN2 = 0.6931471805599453
R_MAX = 5.0
DELTA = R_MAX / (D - 1)
COEFF = -0.5 / (DELTA * DELTA)
EPS = 1e-5
MAGIC = 12582912.0
K = 8
SAGE = (0, 2, 3, 4)
GAT = (5, 6, 7)


def build(nc, a, out):
    ds = bass.ds
    with ExitStack() as ctx:
        def sb(name, shape, dt=F32):
            return ctx.enter_context(nc.sbuf_tensor(name, shape, dt))

        def sem(name):
            return ctx.enter_context(nc.semaphore(name))

        def sems(name, n):
            return [sem(f"{name}{i}") for i in range(n)]

        def dram(name, shape, dt=F32):
            return nc.dram_tensor(name, shape, dt, kind="Internal").ap()

        table = [dram("table0", (NPAD, D)), dram("table1", (NPAD, D))]
        seg_rows = dram("seg_rows", (NPAD, D))
        flats = dram("flats", (5, EPAD))
        flat_bf = dram("flat_bf", (5, EPAD), BF16)
        first_of_tile = dram("first_of_tile", (ET,), I32)
        node_table = dram("node_table", (NPAD, 4))
        at_first = dram("at_first", (EPAD, 2))
        at_last = dram("at_last", (EPAD, 2))
        al_flat = dram("al_flat", (EPAD,))
        ex_flat = dram("ex_flat", (EPAD,))

        X = sb("X", [P, NT * D])
        H = sb("H", [P, ACCW])
        G = sb("G", [P, NT * D])
        T = sb("T", [P, NT * D])
        acc = sb("acc", [P, ACCW])
        rows = sb("rows", [P, BT, D])
        onehot = sb("onehot", [P, BT, D])
        idx_buf = sb("idx_buf", [P, BT], I32)
        meta_buf = sb("meta_buf", [P, BT * 3])
        iota_coli = sb("iota_coli", [P, 1], I32)
        src_t = sb("src_t", [P, ET], I32)
        srchi_t = sb("srchi_t", [P, ET])
        loc_t = sb("loc_t", [P, ET])
        loclast_t = sb("loclast_t", [P, ET])
        cut_t = sb("cut_t", [P, ET])
        ex_t = sb("ex_t", [P, ET])
        als_t = sb("als_t", [P, ET])
        same_s = sb("same_s", [P, ET])
        last_s = sb("last_s", [P, ET])
        seg0_row = sb("seg0_row", [1, ET], I32)
        vecs = sb("vecs", [P, 20 * D])
        mats = sb("mats", [P, 14 * D])
        iota_row = sb("iota_row", [P, D])
        iota_col = sb("iota_col", [P, 1])
        iota_int = sb("iota_int", [P, D], I32)
        ident = sb("ident", [P, P])
        before = sb("before", [P, P])
        ones = sb("ones", [P, P])
        ones_bf = sb("ones_bf", [3, P], BF16)
        rowmask = sb("rowmask", [P, 1])
        node_info = sb("node_info", [P, NT * 4])
        cmap = sb("cmap", [P, NT], I32)
        firstpos = sb("firstpos", [P, NT], I32)
        lastpos = sb("lastpos", [P, NT], I32)
        rcount = sb("rcount", [P, NT])
        small = sb("small", [P, 8 * NT])
        nd = sb("nd", [P, NT * 2])
        cols = sb("cols", [P, 64])
        edge_cols = sb("edge_cols", [P, 2], I32)
        carry_cols = sb("carry_cols", [P, 2])
        carry_row = sb("carry_row", [1, 4 * P])
        carry_in = sb("carry_in", [P, 1])
        bias_cols = sb("bias_cols", [P, 2])
        ids_int = sb("ids_int", [P, NT], I32)
        seg0_blk = sb("seg0_blk", [P, NB], I32)
        PS = ctx.enter_context(nc.psum_tensor("PS", [P, 8 * 512], F32))

        def bank(b, w=512):
            return PS[:, b * 512:b * 512 + w]

        X3 = X[:].rearrange("p (t f) -> p t f", f=D)
        G3 = G[:].rearrange("p (t f) -> p t f", f=D)
        T3 = T[:].rearrange("p (t f) -> p t f", f=D)
        H3 = H[:, 0:NT * D].rearrange("p (t f) -> p t f", f=D)
        stage = onehot[:].rearrange("p a b -> p (a b)")
        stage_in, stage_mid = stage[:, 0:CW], stage[:, 1024:1024 + CW]
        stage_out = rows[:].rearrange("p a b -> p (a b)")[:, 0:CW]
        macc = H[0:3, :]
        meta_t = G[:, 0:3 * ET]

        def scan_tmp(buf, i):
            return buf[:, i * ET:(i + 1) * ET]

        def vec(i):
            return vecs[:, i * D:(i + 1) * D]

        def vec_nodes(i, tiles=NT):
            return vec(i).unsqueeze(1).broadcast_to([P, tiles, D])

        def mat(i):
            return mats[:, i * D:(i + 1) * D]

        VEC = ["L0_gnn_bias", "L1_gnn_b3", "L2_0", "L2_1", "L2_2"]
        for l in (1, 2, 3):
            VEC += [f"L3_gnn_as{l}", f"L3_gnn_ad{l}", f"L3_gnn_b{l}", f"L3_gnn_g{l}", f"L3_gnn_be{l}"]
        vsrc = {n: a[n] for n in VEC if not n.startswith("L2_")}
        for l in range(3):
            vsrc[f"L2_{l}"] = a["L2_gnn_b"][l, :]
        MAT = ["ws_raw", "wn_raw", "ws", "wn", "W1", "W2", "W3", "agg0", "agg1", "agg2",
               "root0", "root1", "root2"]
        msrc = {"ws_raw": a["L0_gnn_W_self"], "wn_raw": a["L0_gnn_W_neigh"], "W1": a["L1_gnn_W1"],
                "W2": a["L1_gnn_W2"], "W3": a["L1_gnn_W3"]}
        for l in range(3):
            msrc[f"agg{l}"] = a["L2_gnn_W_agg"][l, :, :]
            msrc[f"root{l}"] = a["L2_gnn_W_root"][l, :, :]
        gat_w = sb("gat_w", [P, 3 * D])
        V = {n: i for i, n in enumerate(VEC)}
        M = {n: i for i, n in enumerate(MAT)}
        row_matrix = {0: mat(M["ws"]), 2: mat(M["root0"]), 3: mat(M["root1"]), 4: mat(M["root2"]),
                      5: gat_w[:, 0:D], 6: gat_w[:, D:2 * D], 7: gat_w[:, 2 * D:3 * D]}
        seg_matrix = {0: mat(M["wn"]), 1: mat(M["W3"]), 2: mat(M["agg0"]), 3: mat(M["agg1"]),
                      4: mat(M["agg2"]), 5: ident[:], 6: ident[:], 7: ident[:]}
        bias_vec = {0: V["L0_gnn_bias"], 1: V["L1_gnn_b3"], 2: V["L2_0"], 3: V["L2_1"], 4: V["L2_2"],
                    5: V["L3_gnn_b1"], 6: V["L3_gnn_b2"], 7: V["L3_gnn_b3"]}

        def wide(buf, i):
            return buf[:, i * BE:(i + 1) * BE]
        rbf, lnp = wide(H, 0), wide(H, 1)
        attr = wide(G, 1)
        msg0 = wide(G, 2)
        msgf = wide(T, 0)
        keep = wide(T, 1)
        prod = wide(T, 2)
        filt = wide(H, 2)
        dist_row = sb("dist_row", [3, BE], BF16)
        flag_row = sb("flag_row", [1, BE], BF16)

        dst_i, src_i, ew = scan_tmp(T, 0).bitcast(I32), scan_tmp(T, 1).bitcast(I32), scan_tmp(T, 2)
        dst_f, src_f, seg_s = scan_tmp(T, 3), scan_tmp(T, 4), scan_tmp(T, 5)
        cut_s, w0, w1, w2 = scan_tmp(T, 6), scan_tmp(T, 7), scan_tmp(H, 0), scan_tmp(H, 1)
        first_s, ones_s = scan_tmp(H, 2), scan_tmp(H, 3)
        bf = H[:, 4 * ET:7 * ET].bitcast(BF16).rearrange("p (q e) -> p q e", q=6)
        blocks = acc[0:TB, 0:5 * NB * P].rearrange("p (q b c) -> p q b c", q=5, c=P)
        pos_i = acc[:, 5600:5600 + ET].bitcast(I32)
        dst_t, last_t, srcf_t = scan_tmp(T, 0), scan_tmp(T, 1), scan_tmp(T, 2)
        we_bc = G[:, 3 * ET:3 * ET + 9 * D]
        ae_bc = G[:, 3 * ET + 9 * D:3 * ET + 12 * D]
        wprod = G[:, 3 * ET + 12 * D:3 * ET + 21 * D]
        HALF_PI, NEGC, ASUM, VV, AMEAN, ALLSAME, NOLAST, PENALL, EPSC, TOTAL = 0, 1, 2, 5, 14, 17, 18, 19, 20, 21
        AMN, EDGE, NCOLS = 22, 25, 64

        def col(i, n=1):
            return cols[:, i:i + n]

        Gs = [scan_tmp(G, i) for i in range(8)]
        Hs = [scan_tmp(H, i) for i in range(4)]
        turned = H[0:TB, 4 * ET:4 * ET + NB * P]
        at_f = G[:, ET:3 * ET].rearrange("p (j c) -> p j c", c=2)
        at_l = H[:, 0:2 * ET].rearrange("p (j c) -> p j c", c=2)
        nd3 = nd[:].rearrange("p (t c) -> p t c", c=2)
        attr_pre = G[:, 0:3 * ET]
        attr_att = acc[:, 0:3 * ET]
        attr3 = attr_att.rearrange("p (j c) -> p j c", c=3)
        info3 = node_info[:].rearrange("p (t c) -> p t c", c=4)
        als_n, ald_n, self_n, amax_n, exs_n, rden_n = (small[:, i * NT:(i + 1) * NT] for i in range(6))
        stat0, stat1 = small[:, 6 * NT:7 * NT], small[:, 7 * NT:8 * NT]

        consts = sem("consts")
        pads_set = sem("pads_set")
        loads = sem("loads")
        dve = sem("dve")
        act = sem("act")
        pre_in = sem("pre_in")
        pre_out = sem("pre_out")
        cut_in = sem("cut_in")
        cut_out = sem("cut_out")
        zeros_ready = sem("zeros_ready")
        zeros_stored = sem("zeros_stored")
        flats_ready = sem("flats_ready")
        flats_stored = sem("flats_stored")
        blocks_loaded = sem("blocks_loaded")
        seg0_ready = sem("seg0_ready")
        seg0_stored = sem("seg0_stored")
        seg0_loaded = sem("seg0_loaded")
        loc_ready = sem("loc_ready")
        tiles_turned = sem("tiles_turned")
        tiles_copied = sem("tiles_copied")
        tiles_ready = sem("tiles_ready")
        info_turned = sem("info_turned")
        info_ready = sem("info_ready")
        info_scattered = sem("info_scattered")
        info_loaded = sem("info_loaded")
        info_cols = sem("info_cols")
        h_ready = sem("h_ready")
        table_stored = sem("table_stored")
        p_staged = sem("p_staged")
        p_turned = sem("p_turned")
        p_copied = sem("p_copied")
        p_product = sem("p_product")
        p_done = sem("p_done")
        idx_loaded = sems("idx_loaded", 2)
        gathered = sems("gathered", 2)
        onehot_ready = sems("onehot_ready", 2)
        multiplied = sems("multiplied", 2)
        added = sems("added", 2)
        meta_staged = sems("meta_staged", 2)
        meta_added = sems("meta_added", 2)
        c_staged = sem("c_staged")
        c_product = sem("c_product")
        c_copied = sem("c_copied")
        c_stored = sem("c_stored")
        node_rows = sems("node_rows", NCH)
        dist_in = sem("dist_in")
        flag_in = sem("flag_in")
        attr_in = sem("attr_in")
        dist_bc = sem("dist_bc")
        squared = sem("squared")
        rbf_ready = sem("rbf_ready")
        z_ready = sems("z_ready", 2)
        clamped = sems("clamped", 2)
        exp_done = sems("exp_done", 2)
        ln_done = sems("ln_done", 2)
        soft_ready = sems("soft_ready", 2)
        msg_ready = sems("msg_ready", 2)
        msg_turned = sem("msg_turned")
        msgf_ready = sem("msgf_ready")
        flag_bc = sem("flag_bc")
        keep_ready = sem("keep_ready")
        start_ready = sem("start_ready")
        scanned = sem("scanned")
        scan_turned = sem("scan_turned")
        scan_copied = sem("scan_copied")
        win_ready = sem("win_ready")
        ln_in = sem("ln_in")
        ln_out = sem("ln_out")
        var_ready = sem("var_ready")
        std_ready = sem("std_ready")
        sum_in = sem("sum_in")
        sum_out = sem("sum_out")
        attr_space = sem("attr_space")
        attr_again = sem("attr_again")
        lo_in = sems("lo_in", 3)
        lo_bc = sems("lo_bc", 3)
        lo_hot = sems("lo_hot", 3)
        al_rows = sems("al_rows", 3)
        al_mask = sems("al_mask", 3)
        al_pick = sems("al_pick", 3)
        al_done = sems("al_done", 3)
        turn_in = sem("turn_in")
        turn_out = sem("turn_out")
        turn_blk = sem("turn_blk")
        al_stored = sem("al_stored")
        al_loaded = sem("al_loaded")
        first_in = sem("first_in")
        first_sc = sem("first_sc")
        first_ld = sem("first_ld")
        last_in = sem("last_in")
        last_st = sem("last_st")
        last_fill = sem("last_fill")
        last_ga = sem("last_ga")
        exp_in = sem("exp_in")
        exp_out = sem("exp_out")
        ex_stored = sem("ex_stored")
        ex_loaded = sem("ex_loaded")
        ex_turned = sem("ex_turned")
        self_in = sem("self_in")
        self_out = sem("self_out")
        carry_in_ready = sem("carry_in_ready")
        carry_rows = sem("carry_rows")
        carry_scanned = sem("carry_scanned")
        carry_cols_out = sem("carry_cols_out")
        out_ready = sem("out_ready")
        out_stored = sem("out_stored")

        turn = {k: k - (k > 1) for k in range(K)}

        def hold(eng):
            eng.nop(nofuse=True)

        def stepper(eng, own):
            count = {}

            def step(ins, s=own):
                count[s] = count.get(s, 0) + 1
                ins.then_inc(s, 1)
                eng.wait_ge(s, count[s])
            return step

        ctx.enter_context(nc.allow_non_contiguous_dma(reason="a few hundred single words at the start"))
        block = ctx.enter_context(nc.Block())

        @block.sync
        def _(sp):
            sp.wait_ge(pads_set, 1)
            sent = []

            def load(dst, src):
                sp.dma_start(dst, src).then_inc(loads, 16)
                sent.append(1)

            head_e = (P - 1) * ET
            for dst, name in ((dst_i, "dst"), (src_i, "src"), (ew, "edge_weight")):
                load(dst[0:P - 1, :], a[name][0:head_e].rearrange("(p j) -> p j", j=ET))
                load(dst[P - 1:P, 0:SROWS], a[name][head_e:E].unsqueeze(0))
            load(edge_cols[1:P, 0:1], a["dst"][ET - 1:ET + (P - 2) * ET:ET].unsqueeze(1))
            load(edge_cols[0:P - 1, 1:2], a["dst"][ET:ET + (P - 2) * ET + 1:ET].unsqueeze(1))
            attr_head = a["edge_attr_3"][0:head_e, :].rearrange("(p j) c -> p (j c)", j=ET)
            attr_rest = a["edge_attr_3"][head_e:E, :].rearrange("(o j) c -> o (j c)", o=1)
            load(attr_pre[0:P - 1, :], attr_head)
            load(attr_pre[P - 1:P, 0:3 * SROWS], attr_rest)
            load(X3[:, 0:NT - 1, :], a["x"][0:(NT - 1) * P, :].rearrange("(t p) f -> p t f", p=P))
            load(X3[0:NLAST, NT - 1, :], a["x"][(NT - 1) * P:N, :])
            for n, i in V.items():
                load(vec(i), vsrc[n].unsqueeze(0).broadcast_to([P, D]))
            for n in msrc:
                load(mat(M[n]), msrc[n])
            for l in range(3):
                load(gat_w[:, l * D:(l + 1) * D], a[f"L3_gnn_W{l + 1}"])
                load(we_bc[:, l * 3 * D:(l + 1) * 3 * D],
                     a[f"L3_gnn_We{l + 1}"].rearrange("(o c) f -> o (c f)", o=1).broadcast_to([P, 3 * D]))
                load(ae_bc[:, l * D:(l + 1) * D], a[f"L3_gnn_ae{l + 1}"].unsqueeze(0).broadcast_to([P, D]))
            load(bias_cols[:, 0:1], a["L1_gnn_b1"].unsqueeze(1))
            load(bias_cols[:, 1:2], a["L1_gnn_b2"].unsqueeze(1))
            assert len(sent) == LOADS

            sp.wait_ge(zeros_ready, 1)
            sp.dma_start(at_first.rearrange("(p j) c -> p (j c)", p=P), acc[:, 0:2 * ET]).then_inc(zeros_stored, 16)
            sp.dma_start(node_table.rearrange("(t p) c -> p t c", p=P), info3).then_inc(zeros_stored, 16)

            sp.wait_ge(flats_ready, 1)
            for q, t in enumerate((seg_s, dst_f, last_s[:], src_f, cut_s)):
                sp.dma_start(flats[q, :].rearrange("(p j) -> p j", p=P), t).then_inc(flats_stored, 16)
            for q in range(5):
                sp.dma_start(flat_bf[q, :].rearrange("(p j) -> p j", p=P), bf[:, q, :]).then_inc(flats_stored, 16)
            sp.wait_ge(flats_stored, 160)
            sp.wait_ge(zeros_stored, 32)
            for q in range(5):
                sp.dma_start(blocks[:, q, :, :], flats[q, :].rearrange("(b t c) -> t b c", t=TB, c=P))\
                    .then_inc(blocks_loaded, 16)
            sp.wait_ge(seg0_ready, 1)
            sp.dma_start(first_of_tile.rearrange("(b t) -> t b", t=TB), seg0_blk[0:TB, :]).then_inc(seg0_stored, 16)
            sp.wait_ge(seg0_stored, 16)
            sp.dma_start(seg0_row[:], first_of_tile.unsqueeze(0)).then_inc(seg0_loaded, 16)

            def index_load(k, i, h):
                sp.wait_ge(gathered[h], i * (16 * HT) + k * (ITERS * 16 * HT))
                sp.dma_start(idx_buf[:, h * HT:(h + 1) * HT], src_t[:, ds(i * BT + h * HT, HT)])\
                    .then_inc(idx_loaded[h], 16)

            def product_loads(i):
                sp.wait_ge(dist_bc, i * 4)
                sp.dma_start(dist_row[:], flat_bf[0:3, ds(i * BE, BE)]).then_inc(dist_in, 16)
                for h in range(2):
                    sp.wait_ge(msg_ready[h], i * HT)
                if isinstance(i, int):
                    full = (E - i * BE) // P
                    sp.dma_start(attr[:, 0:full * D].rearrange("p (t f) -> p t f", f=D),
                                 a["edge_attr_128"][i * BE:i * BE + full * P, :].rearrange("(t p) f -> p t f", p=P))\
                        .then_inc(attr_in, 16)
                    sp.dma_start(attr[0:E - i * BE - full * P, full * D:(full + 1) * D],
                                 a["edge_attr_128"][i * BE + full * P:E, :]).then_inc(attr_in, 16)
                else:
                    for q in range(4):
                        sp.dma_start(attr[:, q * 512:(q + 1) * 512].rearrange("p (t f) -> p t f", f=D),
                                     a["edge_attr_128"][ds(i * BE + q * 512, 512), :].rearrange("(t p) f -> p t f", p=P))\
                            .then_inc(attr_in, 16)
                for h in range(2):
                    index_load(1, i, h)
                sp.wait_ge(flag_bc, i * 4)
                sp.dma_start(flag_row[:], flat_bf[3:4, ds(i * BE, BE)]).then_inc(flag_in, 16)

            for k in range(K):
                if k in GAT:
                    l = k - 5
                    sp.wait_ge(attr_space, l + 1)
                    sp.dma_start(attr_att[0:P - 1, :], attr_head).then_inc(attr_again, 16)
                    sp.dma_start(attr_att[P - 1:P, 0:3 * SROWS], attr_rest).then_inc(attr_again, 16)
                    sp.wait_ge(p_done, NCH + turn[k] * NCH)
                    sp.dma_start(table[k % 2].rearrange("(t p) f -> p t f", p=P), T3).then_inc(table_stored, 16)
                    with sp.Fori(0, ITERS) as i:
                        sp.wait_ge(lo_bc[l], i * 4)
                        sp.dma_start(flag_row[:], flat_bf[4:5, ds(i * BE, BE)]).then_inc(lo_in[l], 16)
                    sp.wait_ge(turn_blk, l + 1)
                    sp.dma_start(al_flat.rearrange("(b t c) -> t b c", t=TB, c=P),
                                 turned.rearrange("p (b c) -> p b c", c=P)).then_inc(al_stored, 16)
                    sp.wait_ge(al_stored, 16 * (l + 1))
                    sp.dma_start(Gs[0], al_flat.rearrange("(p j) -> p j", p=P)).then_inc(al_loaded, 16)
                    sp.wait_ge(first_sc, 16 * NT * (l + 1))
                    sp.dma_start(G[:, ET:3 * ET], at_first.rearrange("(p j) c -> p (j c)", p=P)).then_inc(first_ld, 16)
                    sp.wait_ge(exp_out, l + 1)
                    sp.dma_start(ex_flat.rearrange("(p j) -> p j", p=P), Gs[6]).then_inc(ex_stored, 16)
                    sp.wait_ge(ex_stored, 16 * (l + 1))
                    sp.dma_start(turned.rearrange("p (b c) -> p b c", c=P),
                                 ex_flat.rearrange("(b t c) -> t b c", t=TB, c=P)).then_inc(ex_loaded, 16)
                    sp.wait_ge(last_in, l + 1)
                    sp.dma_start(at_last.rearrange("(p j) c -> p (j c)", p=P), H[:, 0:2 * ET]).then_inc(last_st, 16)
                else:
                    sp.wait_ge(h_ready, 1 + k)
                    sp.dma_start(table[k % 2].rearrange("(t p) f -> p t f", p=P), H3).then_inc(table_stored, 16)
                if k == 0:
                    sp.wait_ge(tiles_ready, 1)
                if k == 1:
                    with sp.Fori(0, ITERS - 1) as i:
                        product_loads(i)
                    product_loads(ITERS - 1)
                else:
                    with sp.Fori(0, ITERS) as i:
                        for h in range(2):
                            index_load(k, i, h)
                with sp.Fori(0, NCH) as i:
                    sp.wait_ge(c_copied, i + 1 + k * NCH)
                    sp.dma_start(seg_rows[ds(i * (CH * P), CH * P), :].rearrange("(t p) f -> p t f", p=P),
                                 stage_out.rearrange("p (t f) -> p t f", f=D)).then_inc(c_stored, 16)
                if k == 0:
                    sp.wait_ge(info_scattered, 16 * NT)
                    sp.dma_start(info3, node_table.rearrange("(t p) c -> p t c", p=P)).then_inc(info_loaded, 16)
            sp.wait_ge(out_ready, 1)
            sp.dma_start(out[0:(NT - 1) * P, :].rearrange("(t p) f -> p t f", p=P), X3[:, 0:NT - 1, :]).then_inc(out_stored, 16)
            sp.dma_start(out[(NT - 1) * P:N, :], X3[0:NLAST, NT - 1, :]).then_inc(out_stored, 16)
            sp.wait_ge(out_stored, 32)

        @block.gpsimd
        def _(pool):
            step = stepper(pool, consts)
            step(pool.iota(iota_int[:], pattern=[[1, D]], base=0, channel_multiplier=0))
            step(pool.iota(iota_coli[:], pattern=[[0, 1]], base=0, channel_multiplier=1))
            step(pool.iota(ids_int[:], pattern=[[P, NT]], base=0, channel_multiplier=1))
            step(pool.iota(pos_i, pattern=[[P, ET]], base=0, channel_multiplier=1))
            step(pool.memset(ones[:], 1.0))
            step(pool.memset(ident[:], 0.0))
            step(pool.affine_select(out=ident[:], in_=ident[:], compare_op=ALU.not_equal, fill=1.0, base=0,
                                    pattern=[[-1, P]], channel_multiplier=1))
            step(pool.affine_select(out=before[:], in_=ones[:], compare_op=ALU.is_gt, fill=0.0, base=0,
                                    pattern=[[1, P]], channel_multiplier=-1))
            step(pool.affine_select(out=rowmask[:], in_=ones[:, 0:1], compare_op=ALU.is_gt, fill=0.0, base=NLAST,
                                    pattern=[[0, 1]], channel_multiplier=-1))

            def at(idx):
                return bass.IndirectOffsetOnAxis(idx, 0)

            for k in range(K):
                if k in GAT:
                    l = k - 5
                    pool.wait_ge(first_in, l + 1)
                    for t in range(NT):
                        pool.indirect_dma_start(at_first, at(firstpos[:, t:t + 1]), nd[:, 2 * t:2 * t + 2], None,
                                                bounds_check=EPAD - 1, oob_is_err=False).then_inc(first_sc, 16)
                pool.wait_ge(table_stored, 16 + k * 16)
                with pool.Fori(0, ITERS) as i:
                    for h in range(2):
                        pool.wait_ge(idx_loaded[h], 16 * (i + 1) + k * (ITERS * 16))
                        if k == 1:
                            pool.wait_ge(msg_ready[h], i * HT)
                        else:
                            pool.wait_ge(multiplied[h], i + turn[k] * ITERS)
                        hold(pool)
                        for j in range(h * HT, (h + 1) * HT):
                            pool.indirect_dma_start(rows[:, j, :], None, table[k % 2], at(idx_buf[:, j:j + 1]))\
                                .then_inc(gathered[h], 16)
                if k == 0:
                    pool.wait_ge(info_ready, 1)
                    for t in range(NT):
                        pool.indirect_dma_start(node_table, at(cmap[:, t:t + 1]), node_info[:, 4 * t:4 * t + 4], None,
                                                bounds_check=NPAD - 1, oob_is_err=False).then_inc(info_scattered, 16)
                    pool.wait_ge(info_cols, 1)
                if k in GAT:
                    pool.wait_ge(last_st, 16 * (l + 1))
                    pool.wait_ge(last_fill, l + 1)
                    for t in range(NT):
                        pool.indirect_dma_start(nd[:, 2 * t:2 * t + 2], None, at_last, at(lastpos[:, t:t + 1]),
                                                bounds_check=EPAD - 1, oob_is_err=False).then_inc(last_ga, 16)
                for t in range(NT):
                    if t == 0 or (t + 1) % CH == 0:
                        pool.wait_ge(c_stored, 16 * min(NCH, (t + 1) // CH + 1) + k * (NCH * 16))
                    pool.indirect_dma_start(G3[:, t, :], None, seg_rows, at(cmap[:, t:t + 1])).then_inc(node_rows[t // CH], 16)

        @block.scalar
        def _(s):
            step = stepper(s, act)
            s.wait_ge(cut_in, 1)
            step(nc.scalar.activation(w0, w0, ACT.Abs))
            nc.scalar.activation(w1, w0, ACT.Sin, bias=col(HALF_PI), scale=-2.0 * np.pi).then_inc(cut_out, 1)
            n_sqrt = 0

            def sqrt(scale, src, dst):
                nonlocal n_sqrt
                n_sqrt += 1
                s.wait_ge(var_ready, n_sqrt)
                nc.scalar.activation(dst, src, ACT.Sqrt, bias=col(EPSC), scale=scale).then_inc(std_ready, 1)

            def stage_rows(k):
                s.wait_ge(h_ready, 1 + k)
                with s.Fori(0, NCH) as i:
                    s.wait_ge(p_turned, i + turn[k] * NCH)
                    hold(s)
                    nc.scalar.activation(stage_in, H[:, ds(i * CW, CW)], ACT.Copy).then_inc(p_staged, 1)

            def stage_segments(k):
                for h in range(2):
                    s.wait_ge(added[h], ITERS * HT + k * (ITERS * HT))
                with s.Fori(0, NCH) as i:
                    s.wait_ge(c_product, i + k * NCH)
                    hold(s)
                    nc.scalar.activation(stage_in, acc[:, ds(i * CW, CW)], ACT.Copy).then_inc(c_staged, 1)

            def rbf_steps(i):
                for q in range(4):
                    w = slice(q * 512, (q + 1) * 512)
                    s.wait_ge(dist_bc, i * 4 + q + 1)
                    s.wait_ge(z_ready[1], i * 4)
                    hold(s)
                    nc.scalar.activation(rbf[:, w], bank(q), ACT.Square, bias=col(NEGC)).then_inc(squared, 1)
                    s.wait_ge(squared, i * 4 + q + 1)
                    nc.scalar.activation(rbf[:, w], rbf[:, w], ACT.Exp, scale=COEFF).then_inc(rbf_ready, 1)

            def soft_steps(i, n):
                for q in range(4):
                    w = slice(q * 512, (q + 1) * 512)
                    s.wait_ge(clamped[n], i * 4 + q + 1)
                    nc.scalar.activation(lnp[:, w], lnp[:, w], ACT.Exp).then_inc(exp_done[n], 1)
                    s.wait_ge(exp_done[n], i * 4 + q + 1)
                    nc.scalar.activation(lnp[:, w], lnp[:, w], ACT.Ln, bias=1.0).then_inc(ln_done[n], 1)

            def scan_copies(i):
                for q in range(4):
                    s.wait_ge(scan_turned, i * 4 + q + 1)
                    nc.scalar.activation(msg0[:, q * 512:(q + 1) * 512], bank(4 + q), ACT.Copy).then_inc(scan_copied, 1)

            for k in range(K):
                if k in (0, 1, 2, 5):
                    sqrt(1.0 / D, stat1, stat1)
                if k != 1:
                    stage_rows(k)
                if k == 0:
                    s.wait_ge(tiles_ready, 1)
                    with s.Fori(0, ITERS) as i:
                        for h in range(2):
                            s.wait_ge(multiplied[h], i + turn[0] * ITERS)
                            hold(s)
                            nc.scalar.activation(meta_buf[:, h * HT * 3:(h + 1) * HT * 3],
                                                 meta_t[:, ds(i * (BT * 3) + h * HT * 3, HT * 3)],
                                                 ACT.Copy).then_inc(meta_staged[h], 1)
                if k == 1:
                    s.preload_act_table_set("natural_log_exp_and_others")
                    s.wait_ge(table_stored, 32)
                    rbf_steps(0)
                    soft_steps(0, 0)
                    soft_steps(0, 1)
                    with s.Fori(0, ITERS - 1) as i:
                        rbf_steps(i + 1)
                        soft_steps(i + 1, 0)
                        scan_copies(i)
                        soft_steps(i + 1, 1)
                    scan_copies(ITERS - 1)
                if k in GAT:
                    s.wait_ge(exp_in, k - 4)
                    nc.scalar.activation(Gs[6], Gs[5], ACT.Exp).then_inc(exp_out, 1)
                stage_segments(k)
                if k == 1:
                    s.wait_ge(ln_in, 1)
                    step(nc.scalar.activation(T[:], T[:], ACT.Exp))
                    nc.scalar.activation(T[:], T[:], ACT.Ln, bias=1.0).then_inc(ln_out, 1)
                if k in GAT:
                    s.wait_ge(self_in, k - 4)
                    nc.scalar.activation(exs_n, exs_n, ACT.Exp).then_inc(self_out, 1)
                    sqrt(1.0 / N, acc[:, 2 * D:3 * D], acc[:, 3 * D:4 * D])

        @block.tensor
        def _(pe):
            mm, tr = nc.tensor.matmul, nc.tensor.transpose
            pe.wait_ge(consts, CONSTS)
            pe.wait_ge(loads, 16 * LOADS)
            pe.wait_ge(pre_in, 1)
            tr(PS[:, 0:D], mat(M["ws_raw"]), ident[:])
            tr(PS[:, D:2 * D], mat(M["wn_raw"]), ident[:])
            mm(PS[:, 512:513], mat(M["W2"]), ones[:, 0:1], start=True, stop=True)
            mm(PS[:, 1024:1025], before[:], col(TOTAL), start=True, stop=True)
            mm(PS[:, 1536:1539], ones[:], col(ASUM, 3), start=True, stop=True).then_inc(pre_out, 1)
            pe.wait_ge(blocks_loaded, 80)
            pe.wait_ge(loc_ready, 1)
            for q in range(5):
                base = 2048 + (q % 2) * 1024
                if q >= 2:
                    pe.wait_ge(tiles_copied, q - 1)
                for b in range(NB):
                    o = base + (b // 4) * 512 + (b % 4) * TB
                    last = tr(PS[:, o:o + TB], blocks[:, q, b, :], ident[0:TB, 0:TB])
                last.then_inc(tiles_turned, 1)

            def rows_product(k):
                with pe.Fori(0, NCH) as i:
                    pe.wait_ge(p_staged, i + 1 + turn[k] * NCH)
                    pe.wait_ge(p_copied, i + turn[k] * NCH)
                    for j in range(CH):
                        last = tr(PS[:, j * D:(j + 1) * D], stage_in[:, j * D:(j + 1) * D], ident[:])
                    last.then_inc(p_turned, 1)
                    pe.wait_ge(p_copied, i + 1 + turn[k] * NCH)
                    pe.wait_ge(p_done, i + turn[k] * NCH)
                    for j in range(CH):
                        last = mm(PS[:, 1024 + j * D:1024 + (j + 1) * D], stage_mid[:, j * D:(j + 1) * D],
                                  row_matrix[k], start=True, stop=True)
                    last.then_inc(p_product, 1)

            def segment_product(k):
                with pe.Fori(0, NCH) as i:
                    pe.wait_ge(c_staged, i + 1 + k * NCH)
                    pe.wait_ge(c_copied, i + k * NCH)
                    for j in range(CH):
                        last = mm(PS[:, 1024 + j * D:1024 + (j + 1) * D], stage_in[:, j * D:(j + 1) * D],
                                  seg_matrix[k], start=True, stop=True)
                    last.then_inc(c_product, 1)

            def edge_pass(k):
                with pe.Fori(0, ITERS) as i:
                    for h in range(2):
                        pe.wait_ge(gathered[h], (i + 1) * (16 * HT) + k * (ITERS * 16 * HT))
                        pe.wait_ge(onehot_ready[h], i + 1 + k * ITERS)
                        pe.wait_ge(added[h], i * HT + k * (ITERS * HT))
                        if k == 0:
                            pe.wait_ge(meta_staged[h], i + 1)
                            pe.wait_ge(meta_added[h], i * HT)
                        for j in range(HT):
                            o, r = h * 1024 + j * D, h * HT + j
                            last = mm(PS[:, o:o + D], rows[:, r, :], onehot[:, r, :], start=True, stop=True)
                            if k == 0:
                                last = mm(PS[0:3, 2048 + o:2048 + o + D], meta_buf[:, 3 * r:3 * r + 3],
                                          onehot[:, r, :], start=True, stop=True)
                        last.then_inc(multiplied[h], 1)

            def filter_step(i, n):
                for q in range(4):
                    pe.wait_ge(soft_ready[0] if n else rbf_ready, i * 4 + q + 1)
                    mm(bank(q), mat(M["W2" if n else "W1"]), rbf[:, q * 512:(q + 1) * 512],
                       start=True, stop=True).then_inc(z_ready[n], 1)

            def spread_distances(i):
                pe.wait_ge(dist_in, (i + 1) * 16)
                pe.wait_ge(soft_ready[1], i * 4)
                for q in range(4):
                    mm(bank(q), ones_bf[:], dist_row[:, q * 512:(q + 1) * 512], start=True, stop=True)\
                        .then_inc(dist_bc, 1)

            def turn_messages(i):
                for q in range(4):
                    h = q // 2
                    pe.wait_ge(msg_ready[h], i * HT + (q % 2 + 1) * 4)
                    pe.wait_ge(added[h], i * HT + 1 * (ITERS * HT))
                    for j in range(4 * q, 4 * q + 4):
                        o = 2048 + j * D
                        last = tr(PS[:, o:o + D], msg0[:, j * D:(j + 1) * D], ident[:])
                    last.then_inc(msg_turned, 1)

            def spread_flags(i):
                pe.wait_ge(flag_in, (i + 1) * 16)
                for q in range(4):
                    pe.wait_ge(msgf_ready, i * 4 + q + 1)
                    mm(bank(4 + q), ones_bf[0:1, :], flag_row[:, q * 512:(q + 1) * 512], start=True, stop=True)\
                        .then_inc(flag_bc, 1)

            def turn_scans(i):
                for q in range(4):
                    pe.wait_ge(scanned, i * 4 + q + 1)
                    for j in range(4 * q, 4 * q + 4):
                        o = 2048 + j * D
                        last = tr(PS[:, o:o + D], prod[:, j * D:(j + 1) * D], ident[:])
                    last.then_inc(scan_turned, 1)

            def last_windows(i):
                for q in range(4):
                    pe.wait_ge(scan_copied, i * 4 + q + 1)
                    if q % 2 == 0:
                        pe.wait_ge(onehot_ready[q // 2], i + 1 + 1 * ITERS)
                    for j in range(4 * q, 4 * q + 4):
                        o = 2048 + j * D
                        last = mm(PS[:, o:o + D], msg0[:, j * D:(j + 1) * D], onehot[:, j, :], start=True, stop=True)
                    last.then_inc(win_ready, 1)

            n_carry = 0

            def carries(n):
                nonlocal n_carry
                for _ in range(n):
                    n_carry += 1
                    pe.wait_ge(carry_in_ready, n_carry)
                    tr(PS[0:1, 3072:3072 + P], carry_cols[:, 0:1], ident[:])
                    tr(PS[0:1, 3072 + P:3072 + 2 * P], carry_cols[:, 1:2], ident[:]).then_inc(carry_rows, 1)
                    pe.wait_ge(carry_scanned, n_carry)
                    tr(PS[:, 3584:3585], carry_row[0:1, 3 * P:4 * P], ident[0:1, 0:1]).then_inc(carry_cols_out, 1)

            def attention(l):
                with pe.Fori(0, ITERS) as i:
                    pe.wait_ge(lo_in[l], (i + 1) * 16)
                    pe.wait_ge(lo_hot[l], i)
                    for q in range(4):
                        mm(bank(q), ones_bf[0:1, :], flag_row[:, q * 512:(q + 1) * 512], start=True, stop=True)\
                            .then_inc(lo_bc[l], 1)
                    pe.wait_ge(lo_hot[l], i + 1)
                    pe.wait_ge(al_pick[l], i)
                    for j in range(BT):
                        o = 2048 + (j // HT) * 512 + (j % HT) * NT
                        last = mm(PS[:, o:o + NT], onehot[:, j, :], als_n, start=True, stop=True)
                    last.then_inc(al_rows[l], 1)
                pe.wait_ge(al_done[l], ITERS)
                for b in range(NB):
                    last = tr(PS[0:TB, 3072 + b * P:3072 + (b + 1) * P], als_t[:, b * TB:(b + 1) * TB], ident[:])
                last.then_inc(turn_out, 1)
                pe.wait_ge(turn_blk, l + 1)
                carries(5)
                pe.wait_ge(ex_loaded, 16 * (l + 1))
                for b in range(NB):
                    o = 2048 + (b // 4) * 512 + (b % 4) * TB
                    last = tr(PS[:, o:o + TB], turned[:, b * P:(b + 1) * P], ident[0:TB, 0:TB])
                last.then_inc(ex_turned, 1)

            def statistics(l):
                for n in range(2):
                    pe.wait_ge(sum_in, 2 * l + n + 1)
                    mm(PS[:, 0:D], ones[:], acc[:, 2 * n * D:(2 * n + 1) * D], start=True, stop=True).then_inc(sum_out, 1)

            for k in range(K):
                if k != 1:
                    rows_product(k)
                if k == 1:
                    spread_distances(0)
                    filter_step(0, 0)
                    filter_step(0, 1)
                    with pe.Fori(0, ITERS - 1) as i:
                        spread_distances(i + 1)
                        turn_messages(i)
                        filter_step(i + 1, 0)
                        spread_flags(i)
                        filter_step(i + 1, 1)
                        turn_scans(i)
                        last_windows(i)
                    turn_messages(ITERS - 1)
                    spread_flags(ITERS - 1)
                    turn_scans(ITERS - 1)
                    last_windows(ITERS - 1)
                else:
                    if k in GAT:
                        attention(k - 5)
                    edge_pass(k)
                if k == 0:
                    for h in range(2):
                        pe.wait_ge(meta_added[h], ITERS * HT)
                    for t in range(NT):
                        last = tr(PS[:, 2560 + 3 * t:2563 + 3 * t], macc[:, t * P:(t + 1) * P], ident[0:3, 0:3])
                    last.then_inc(info_turned, 1)
                segment_product(k)
                if k in GAT:
                    statistics(k - 5)

        @block.vector
        def _(v):
            tt, ts, stt = nc.vector.tensor_tensor, nc.vector.tensor_scalar, nc.vector.scalar_tensor_tensor
            copy, memset, reduce = nc.vector.tensor_copy, nc.vector.memset, nc.vector.tensor_reduce
            scan, recip = nc.vector.tensor_tensor_scan, nc.vector.reciprocal
            step = stepper(v, dve)

            step(memset(dst_i, N))
            step(memset(src_i, 0))
            step(memset(ew, R_MAX))
            step(memset(edge_cols[:], -1))
            step(memset(X3[:, NT - 1, :], 0.0))
            memset(attr_pre, 0.0).then_inc(pads_set, 1)
            step(memset(acc[:, 0:2 * ET], 0.0))
            step(memset(col(HALF_PI), float(np.pi / 2)))
            step(memset(col(EPSC), EPS))
            step(memset(ones_bf[:], 1.0))
            step(memset(ones_s, 1.0))
            step(memset(info3[:, :, 0:1], 0.0))
            step(memset(info3[:, :, 1:3], BIGPOS))
            memset(info3[:, :, 3:4], 0.0).then_inc(zeros_ready, 1)
            v.wait_ge(consts, CONSTS)
            step(copy(iota_row[:], iota_int[:]))
            step(copy(iota_col[:], iota_coli[:]))
            step(ts(col(NEGC), iota_col[:], -DELTA, None, ALU.mult))
            v.wait_ge(loads, 16 * LOADS)
            step(copy(dst_f, dst_i))
            step(copy(src_f, src_i))
            step(copy(col(EDGE, 2), edge_cols[:]))
            step(tt(first_s[:, 1:ET], dst_f[:, 1:ET], dst_f[:, 0:ET - 1], ALU.not_equal))
            step(tt(first_s[:, 0:1], dst_f[:, 0:1], col(EDGE), ALU.not_equal))
            step(copy(last_s[:, 0:ET - 1], first_s[:, 1:ET]))
            step(tt(last_s[:, ET - 1:ET], dst_f[:, ET - 1:ET], col(EDGE + 1), ALU.not_equal))
            step(ts(same_s[:], first_s, -1.0, 1.0, ALU.mult, ALU.add))
            step(reduce(col(ALLSAME), same_s[:], AX.X, ALU.min))
            step(ts(col(PENALL), col(ALLSAME), -1.0, HUGE, ALU.add, ALU.mult))
            step(reduce(col(NOLAST), last_s[:], AX.X, ALU.max))
            step(ts(col(NOLAST), col(NOLAST), -1.0, 1.0, ALU.mult, ALU.add))
            step(scan(seg_s, ones_s, first_s, 0.0, ALU.mult, ALU.add))
            step(copy(col(TOTAL), seg_s[:, ET - 1:ET]))
            reduce(col(ASUM, 3), attr_pre.rearrange("p (j c) -> p c j", c=3), AX.X, ALU.add).then_inc(pre_in, 1)
            step(ts(w0, ew, 0.1, MAGIC, ALU.mult, ALU.add))
            step(ts(w0, w0, -MAGIC, None, ALU.add))
            stt(w0, ew, 0.1, w0, ALU.mult, ALU.subtract).then_inc(cut_in, 1)
            step(copy(bf[:, 0, :], ew))
            step(tt(cut_s, ew, bf[:, 0, :], ALU.subtract))
            step(copy(bf[:, 1, :], cut_s))
            step(tt(cut_s, cut_s, bf[:, 1, :], ALU.subtract))
            step(copy(bf[:, 2, :], cut_s))
            step(copy(bf[:, 3, :], same_s[:]))
            step(ts(w2.bitcast(I32), src_i, P - 1, None, ALU.bitwise_and))
            step(copy(bf[:, 4, :], w2.bitcast(I32)))
            v.wait_ge(cut_out, 1)
            step(ts(cut_s, w1, 0.5, 0.5, ALU.mult, ALU.add))
            step(ts(w2, ew, R_MAX, None, ALU.is_lt))
            step(tt(cut_s, cut_s, w2, ALU.mult))
            for l in range(3):
                step(tt(wprod[:, 3 * l * D:3 * (l + 1) * D].rearrange("p (c f) -> p c f", c=3),
                        we_bc[:, 3 * l * D:3 * (l + 1) * D].rearrange("p (c f) -> p c f", c=3),
                        ae_bc[:, l * D:(l + 1) * D].unsqueeze(1).broadcast_to([P, 3, D]), ALU.mult))
            step(reduce(col(VV, 9), wprod.rearrange("p (c f) -> p c f", f=D), AX.X, ALU.add))
            v.wait_ge(pre_out, 1)
            step(ts(col(AMN, 3), PS[:, 1536:1539], 1.0 / E, None, ALU.mult))
            for l in range(3):
                step(tt(col(EDGE + 2, 3), col(AMN, 3), col(VV + 3 * l, 3), ALU.mult))
                step(reduce(col(AMEAN + l), col(EDGE + 2, 3), AX.X, ALU.add))
            step(copy(mats[:, M["ws"] * D:(M["wn"] + 1) * D], PS[:, 0:2 * D]))
            step(stt(bias_cols[:, 1:2], PS[:, 512:513], -LN2, bias_cols[:, 1:2], ALU.mult, ALU.add))
            step(copy(col(TOTAL), PS[:, 1024:1025]))
            step(ts(seg_s, seg_s, col(TOTAL), None, ALU.add), flats_ready)
            v.wait_ge(blocks_loaded, 80)
            step(copy(small[0:TB, 0:NB], blocks[:, 0, :, 0]))
            copy(seg0_blk[0:TB, :], small[0:TB, 0:NB]).then_inc(seg0_ready, 1)
            tt(blocks[:, 0, :, :], blocks[:, 0, :, :], small[0:TB, 0:NB].unsqueeze(2).broadcast_to([TB, NB, P]),
               ALU.subtract).then_inc(loc_ready, 1)
            for q, dst in enumerate((loc_t[:], dst_t, last_t, srcf_t, cut_t[:])):
                base = 2048 + (q % 2) * 1024
                v.wait_ge(tiles_turned, q + 1)
                step(copy(dst[:, 0:4 * TB], PS[:, base:base + 4 * TB]))
                step(copy(dst[:, 4 * TB:ET], PS[:, base + 512:base + 512 + 3 * TB]), tiles_copied)
            step(stt(loclast_t[:], loc_t[:], 1.0, last_t, ALU.add, ALU.mult))
            step(ts(loclast_t[:], loclast_t[:], -1.0, None, ALU.add))
            step(copy(src_t[:], srcf_t))
            step(ts(srcf_t.bitcast(I32), src_t[:], 7, None, ALU.arith_shift_right))
            step(copy(srchi_t[:], srcf_t.bitcast(I32)))
            meta3 = meta_t.rearrange("p (e c) -> p e c", c=3)
            step(tt(meta3[:, :, 0], dst_t, last_t, ALU.mult))
            step(copy(srcf_t, pos_i))
            step(tt(meta3[:, :, 1], srcf_t, last_t, ALU.mult))
            step(memset(meta3[:, :, 2:3], 1.0), tiles_ready)

            def layer_input(k):
                step(reduce(stat0, X3, AX.X, ALU.add))
                step(ts(stat0, stat0, -1.0 / D, None, ALU.mult))
                step(tt(H3, X3, stat0.unsqueeze(2).broadcast_to([P, NT, D]), ALU.add))
                sq = acc[:, 0:NT * D]
                step(tt(sq, H[:, 0:NT * D], H[:, 0:NT * D], ALU.mult))
                reduce(stat1, sq.rearrange("p (t f) -> p t f", f=D), AX.X, ALU.add).then_inc(var_ready, 1)
                v.wait_ge(std_ready, vars_done(1))
                step(recip(stat1, stat1))
                step(stt(H3, H3, 0.0, stat1.unsqueeze(2).broadcast_to([P, NT, D]), ALU.max, ALU.mult), h_ready)

            n_vars = 0

            def vars_done(n):
                nonlocal n_vars
                n_vars += n
                return n_vars

            def rows_product(k):
                with v.Fori(0, NCH) as i:
                    v.wait_ge(p_turned, i + 1 + turn[k] * NCH)
                    copy(stage_mid, PS[:, 0:CW]).then_inc(p_copied, 1)
                    v.wait_ge(p_product, i + 1 + turn[k] * NCH)
                    hold(v)
                    copy(T[:, ds(i * CW, CW)], PS[:, 1024:1024 + CW]).then_inc(p_done, 1)
                v.wait_ge(p_done, NCH + turn[k] * NCH)

            def zero_acc(k):
                step(memset(acc[:], 0.0))
                if k == 1:
                    step(memset(acc[:, 0:1], 1.0))

            def make_onehot(k, i, h, loc, used, used_at):
                v.wait_ge(used, used_at)
                half = onehot[:, h * HT:(h + 1) * HT, :]
                if k in GAT:
                    hold(v)
                    for j in range(HT):
                        e = i * BT + (h * HT + j)
                        last = ts(onehot[:, h * HT + j, :], iota_row[:], loc[:, ds(e, 1)], ex_t[:, ds(e, 1)],
                                  ALU.is_equal, ALU.mult)
                else:
                    last = tt(half, iota_row[:].unsqueeze(1).broadcast_to([P, HT, D]),
                              loc[:, ds(i * BT + h * HT, HT)].unsqueeze(2).broadcast_to([P, HT, D]), ALU.is_equal)
                last.then_inc(onehot_ready[h], 1)

            def add_windows(i, h, windows, dst, done, after, first, before_pass):
                for j in range(HT):
                    at = dst[:, ds(first[j], D)]
                    if j in after:
                        v.wait_ge(*after[j])
                    if j == 0:
                        v.wait_ge(done[1 - h], (i + h) * HT + before_pass)
                    else:
                        v.wait_ge(done[h], i * HT + j + before_pass)
                    tt(at, at, windows[:, j * D:(j + 1) * D], ALU.add).then_inc(done[h], 1)

            def tile_segments(i, h):
                return [v.value_load(seg0_row[0:1, ds(i * BT + (h * HT + j), 1)], min_val=0, max_val=ACCW - D)
                        for j in range(HT)]

            def edge_pass(k):
                with v.Fori(0, ITERS) as i:
                    for h in range(2):
                        make_onehot(k, i, h, loc_t, multiplied[h], i + turn[k] * ITERS)
                    for h in range(2):
                        first = tile_segments(i, h)
                        ready = {0: (multiplied[h], i + 1 + turn[k] * ITERS)}
                        add_windows(i, h, PS[:, h * 1024:(h + 1) * 1024], acc, added, ready, first, k * ITERS * HT)
                        if k == 0:
                            add_windows(i, h, PS[0:3, 2048 + h * 1024:2048 + (h + 1) * 1024], macc, meta_added, ready,
                                        first, 0)

            def messages(i, attrs):
                v.wait_ge(attr_in, attrs)
                v.wait_ge(win_ready, i * 4)
                hold(v)
                for h in range(2):
                    v.wait_ge(gathered[h], (i + 1) * (16 * HT) + 1 * (ITERS * 16 * HT))
                    hold(v)
                    for j in range(h * HT, (h + 1) * HT):
                        w = slice(j * D, (j + 1) * D)
                        stt(msg0[:, w], attr[:, w], cut_t[:, ds(i * BT + j, 1)], rows[:, j, :], ALU.mult, ALU.mult)\
                            .then_inc(msg_ready[h], 1)

            def clamp(i, n):
                for q in range(4):
                    v.wait_ge(z_ready[n], i * 4 + q + 1)
                    v.wait_ge(soft_ready[1 - n], (i + n) * 4)
                    ts(lnp[:, q * 512:(q + 1) * 512], bank(q), bias_cols[:, n:n + 1], 30.0, ALU.add, ALU.min)\
                        .then_inc(clamped[n], 1)

            def softplus(i, n):
                for q in range(4):
                    w = slice(q * 512, (q + 1) * 512)
                    v.wait_ge(ln_done[n], i * 4 + q + 1)
                    stt(filt[:, w] if n else rbf[:, w], bank(q), bias_cols[:, n:n + 1], lnp[:, w], ALU.add, ALU.max)\
                        .then_inc(soft_ready[n], 1)

            def feature_messages(i):
                for q in range(4):
                    w = slice(q * 512, (q + 1) * 512)
                    v.wait_ge(msg_turned, i * 4 + q + 1)
                    v.wait_ge(soft_ready[1], (i + 1) * 4)
                    v.wait_ge(scanned, i * 4)
                    stt(msgf[:, w], filt[:, w], -LN2, bank(4 + q), ALU.add, ALU.mult).then_inc(msgf_ready, 1)

            def scans(i):
                for q in range(4):
                    w = slice(q * 512, (q + 1) * 512)
                    v.wait_ge(flag_bc, i * 4 + q + 1)
                    tt(keep[:, w], msgf[:, w], bank(4 + q), ALU.mult).then_inc(keep_ready, 1)
                    v.wait_ge(keep_ready, i * 4 + q + 1)
                    tt(msgf[:, w], msgf[:, w], keep[:, w], ALU.subtract).then_inc(start_ready, 1)
                    v.wait_ge(start_ready, i * 4 + q + 1)
                    v.wait_ge(scan_turned, i * 4)
                    v.wait_ge(scanned, i * 4 + q)
                    hold(v)
                    e = (q * 512 - 1) % BE
                    scan(prod[:, w], keep[:, w], msgf[:, w], prod[:, e:e + 1], ALU.mult, ALU.add).then_inc(scanned, 1)

            def product_windows(i):
                for h in range(2):
                    first = tile_segments(i, h)
                    ready = {4 * (q % 2): (win_ready, i * 4 + q + 1) for q in (2 * h, 2 * h + 1)}
                    add_windows(i, h, PS[:, 2048 + h * 1024:2048 + (h + 1) * 1024], acc, added, ready, first, ITERS * HT)

            def product_pass():
                step(memset(prod, 0.0))
                clamp(0, 0)
                softplus(0, 0)
                clamp(0, 1)
                softplus(0, 1)
                with v.Fori(0, ITERS - 1) as i:
                    for h in range(2):
                        make_onehot(1, i, h, loclast_t, win_ready, i * 4)
                    messages(i, (i + 1) * 64)
                    clamp(i + 1, 0)
                    feature_messages(i)
                    softplus(i + 1, 0)
                    scans(i)
                    clamp(i + 1, 1)
                    softplus(i + 1, 1)
                    product_windows(i)
                i = ITERS - 1
                for h in range(2):
                    make_onehot(1, i, h, loclast_t, win_ready, i * 4)
                messages(i, i * 64 + 32)
                feature_messages(i)
                scans(i)
                product_windows(i)

            def segments_out(k):
                with v.Fori(0, NCH) as i:
                    v.wait_ge(c_product, i + 1 + k * NCH)
                    v.wait_ge(c_stored, i * 16 + k * (NCH * 16))
                    copy(stage_out, PS[:, 1024:1024 + CW]).then_inc(c_copied, 1)

            def segment_facts():
                v.wait_ge(info_turned, 1)
                facts = PS[:, 2560:2560 + 3 * NT].rearrange("p (t c) -> p t c", c=3)
                step(copy(info3[:, :, 2:4], facts[:, :, 1:3]))
                step(copy(info3[:, :, 0], ids_int[:]))
                step(stt(info3[:, :, 1], info3[:, :, 2], 1.0, info3[:, :, 3], ALU.add, ALU.subtract))
                step(ts(stat0, info3[:, :, 3], 0.0, BIGPOS, ALU.is_equal, ALU.mult))
                step(tt(stat0, stat0, facts[:, :, 0], ALU.add))
                step(copy(cmap[:], stat0), info_ready)

            def node_facts():
                v.wait_ge(info_loaded, 16)
                step(copy(firstpos[:], info3[:, :, 1]))
                step(copy(lastpos[:], info3[:, :, 2]))
                step(ts(rcount[:], info3[:, :, 3], 1.0, None, ALU.max))
                step(recip(rcount[:], rcount[:]))
                step(copy(cmap[:], info3[:, :, 0]), info_cols)

            def chunk(buf3, c):
                return buf3[:, c * CH:(c + 1) * CH, :]

            def mean_layer(k):
                for c in range(NCH):
                    g = chunk(G3, c)
                    v.wait_ge(node_rows[c], (k + 1) * CH * 16)
                    step(tt(g, g, rcount[:, c * CH:(c + 1) * CH].unsqueeze(2).broadcast_to([P, CH, D]), ALU.mult))
                    step(tt(g, g, chunk(T3, c), ALU.add))
                    step(tt(g, g, vec_nodes(bias_vec[k], CH), ALU.add))
                    x = chunk(X3, c)
                    if k == 0:
                        step(stt(x, g, 0.0, x, ALU.max, ALU.add))
                    elif k == 4:
                        step(tt(x, g, x, ALU.add))
                    else:
                        step(ts(chunk(H3, c), g, 0.0, None, ALU.max), h_ready if c == NCH - 1 else dve)

            def product_layer():
                for c in range(NCH):
                    v.wait_ge(node_rows[c], 2 * CH * 16)
                step(tt(G3, G3, vec_nodes(bias_vec[1]), ALU.add))
                ts(T[:], G[:], 30.0, None, ALU.min).then_inc(ln_in, 1)
                v.wait_ge(ln_out, 1)
                step(tt(G[:], G[:], T[:], ALU.max))
                step(stt(X[:], G[:], -LN2, X[:], ALU.add, ALU.add))

            n_carry = 0

            def linked_scan(dst, d0, d1, ops, whole, start, backward=False):
                nonlocal n_carry
                n_carry += 1
                r = (lambda x: x[:, ::-1]) if backward else (lambda x: x)
                end = dst[:, 0:1] if backward else dst[:, ET - 1:ET]
                step(scan(r(dst), r(d0), r(d1), start, *ops))
                step(copy(carry_cols[:, 0:1], end))
                copy(carry_cols[:, 1:2], whole).then_inc(carry_in_ready, 1)
                v.wait_ge(carry_rows, n_carry)
                step(copy(carry_row[:, 0:2 * P], PS[0:1, 3072:3072 + 2 * P]))
                f, w, o, z = (carry_row[:, i * P:(i + 1) * P] for i in range(4))
                step(scan(r(o), r(w), r(f), start, *ops))
                step(memset(z[:, P - 1:P] if backward else z[:, 0:1], start))
                if backward:
                    step(copy(z[:, 0:P - 1], o[:, 1:P]), carry_scanned)
                else:
                    step(copy(z[:, 1:P], o[:, 0:P - 1]), carry_scanned)
                v.wait_ge(carry_cols_out, n_carry)
                step(copy(carry_in[:], PS[:, 3584:3585]))
                return r(dst), r(d0), r(d1), carry_in[:], *ops

            def attention(k):
                l = k - 5
                step(memset(attr_att, 0.0), attr_space)
                for dst, w in ((als_n, f"L3_gnn_as{l + 1}"), (ald_n, f"L3_gnn_ad{l + 1}")):
                    step(tt(G3, T3, vec_nodes(V[w]), ALU.mult))
                    step(reduce(dst, G3, AX.X, ALU.add))
                step(tt(self_n, als_n, ald_n, ALU.add))
                step(ts(self_n, self_n, col(AMEAN + l), None, ALU.add))
                step(stt(self_n, self_n, 0.2, self_n, ALU.mult, ALU.max))
                step(copy(nd3[:, :, 0], ald_n))
                step(copy(nd3[:, :, 1], self_n), first_in)
                mask, pick = Hs[0].rearrange("p (t c) -> p t c", c=NT), Hs[1].rearrange("p (t c) -> p t c", c=NT)
                cand = PS[:, 2048:3072].rearrange("p (a c) -> p a c", a=2)[:, :, 0:HT * NT]
                with v.Fori(0, ITERS) as i:
                    v.wait_ge(lo_bc[l], (i + 1) * 4)
                    v.wait_ge(al_rows[l], i)
                    hold(v)
                    ts(onehot[:].rearrange("p a b -> p (a b)"), PS[:, 0:BE], iota_col[:], None, ALU.is_equal)\
                        .then_inc(lo_hot[l], 1)
                    v.wait_ge(al_pick[l], i)
                    tt(mask, iota_row[:, 0:NT].unsqueeze(1).broadcast_to([P, BT, NT]),
                       srchi_t[:, ds(i * BT, BT)].unsqueeze(2).broadcast_to([P, BT, NT]), ALU.is_equal)\
                        .then_inc(al_mask[l], 1)
                    v.wait_ge(al_mask[l], i + 1)
                    v.wait_ge(al_rows[l], i + 1)
                    v.wait_ge(al_done[l], i)
                    hold(v)
                    tt(Hs[1].rearrange("p (a c) -> p a c", a=2), Hs[0].rearrange("p (a c) -> p a c", a=2), cand,
                       ALU.mult).then_inc(al_pick[l], 1)
                    v.wait_ge(al_pick[l], i + 1)
                    hold(v)
                    reduce(als_t[:, ds(i * BT, BT)], pick, AX.X, ALU.add).then_inc(al_done[l], 1)
                v.wait_ge(turn_out, l + 1)
                step(copy(turned, PS[0:TB, 3072:3072 + NB * P]), turn_blk)
                v.wait_ge(attr_again, 32 * (l + 1))
                step(ts(Gs[5], attr3[:, :, 0], col(VV + 3 * l), None, ALU.mult))
                for c in (1, 2):
                    step(stt(Gs[5], attr3[:, :, c], col(VV + 3 * l + c), Gs[5], ALU.mult, ALU.add))
                v.wait_ge(first_ld, 16 * (l + 1))
                add, spread = (ALU.add, ALU.max), (ALU.mult, ALU.add)
                step(scan(*linked_scan(Gs[3], same_s[:], at_f[:, :, 0], spread, col(ALLSAME), 0.0)))
                step(scan(*linked_scan(Gs[4], same_s[:], at_f[:, :, 1], spread, col(ALLSAME), 0.0)))
                v.wait_ge(al_loaded, 16 * (l + 1))
                step(tt(Gs[0], Gs[0], Gs[3], ALU.add))
                step(tt(Gs[0], Gs[0], Gs[5], ALU.add))
                step(stt(Gs[0], Gs[0], 0.2, Gs[0], ALU.mult, ALU.max))
                step(ts(Gs[5], same_s[:], -1.0, HUGE, ALU.add, ALU.mult))
                step(scan(*linked_scan(Gs[6], Gs[5], Gs[0], add, col(PENALL), -HUGE)))
                step(tt(Gs[6], Gs[6], last_s[:], ALU.mult))
                step(ts(Gs[5], last_s[:], -1.0, 1.0, ALU.mult, ALU.add))
                step(scan(*linked_scan(Gs[7], Gs[5], Gs[6], spread, col(NOLAST), 0.0, backward=True)))
                step(tt(at_l[:, :, 1], Gs[7], Gs[4], ALU.max))
                step(tt(Gs[5], Gs[0], at_l[:, :, 1], ALU.subtract), exp_in)
                v.wait_ge(exp_out, l + 1)
                step(scan(*linked_scan(at_l[:, :, 0], same_s[:], Gs[6], spread, col(ALLSAME), 0.0)), last_in)
                v.wait_ge(ex_turned, l + 1)
                step(copy(ex_t[:, 0:4 * TB], PS[:, 2048:2048 + 4 * TB]))
                step(copy(ex_t[:, 4 * TB:ET], PS[:, 2560:2560 + 3 * TB]))
                step(memset(nd3[:, :, 0:1], 0.0))
                step(memset(nd3[:, :, 1:2], -HUGE), last_fill)

            def attention_layer(k):
                l = k - 5
                v.wait_ge(last_ga, 16 * NT * (l + 1))
                step(tt(amax_n, nd3[:, :, 1], self_n, ALU.max))
                step(tt(exs_n, self_n, amax_n, ALU.subtract), self_in)
                v.wait_ge(self_out, l + 1)
                step(tt(rden_n, nd3[:, :, 0], exs_n, ALU.add))
                step(ts(rden_n, rden_n, 1e-16, None, ALU.add))
                step(recip(rden_n, rden_n))
                step(tt(T3, T3, exs_n.unsqueeze(2).broadcast_to([P, NT, D]), ALU.mult))
                for c in range(NCH):
                    g = chunk(G3, c)
                    v.wait_ge(node_rows[c], (k + 1) * CH * 16)
                    step(tt(g, g, chunk(T3, c), ALU.add))
                    step(tt(g, g, rden_n[:, c * CH:(c + 1) * CH].unsqueeze(2).broadcast_to([P, CH, D]), ALU.mult))
                    step(tt(g, g, vec_nodes(bias_vec[k], CH), ALU.add))
                    step(stt(chunk(H3, c), g, 0.01, g, ALU.mult, ALU.max))
                s0, nm, s1, sd = (acc[:, i * D:(i + 1) * D] for i in range(4))
                lastt = H3[:, NT - 1, :]
                step(ts(lastt, lastt, rowmask[:], None, ALU.mult))
                step(reduce(s0, H3.rearrange("p t f -> p f t"), AX.X, ALU.add), sum_in)
                v.wait_ge(sum_out, 2 * l + 1)
                step(ts(nm, PS[:, 0:D], -1.0 / N, None, ALU.mult))
                step(tt(H3, H3, nm.unsqueeze(1).broadcast_to([P, NT, D]), ALU.add))
                step(ts(lastt, lastt, rowmask[:], None, ALU.mult))
                step(tt(G[:], H[:, 0:NT * D], H[:, 0:NT * D], ALU.mult))
                step(reduce(s1, G3.rearrange("p t f -> p f t"), AX.X, ALU.add), sum_in)
                v.wait_ge(sum_out, 2 * l + 2)
                step(copy(s1, PS[:, 0:D]), var_ready)
                v.wait_ge(std_ready, vars_done(1))
                step(recip(sd, sd))
                step(tt(sd, sd, vec(V[f"L3_gnn_g{l + 1}"]), ALU.mult))
                step(tt(H3, H3, sd.unsqueeze(1).broadcast_to([P, NT, D]), ALU.mult))
                if k < K - 1:
                    step(tt(H3, H3, vec_nodes(V[f"L3_gnn_be{l + 1}"]), ALU.add), h_ready)
                else:
                    step(tt(H3, H3, vec_nodes(V[f"L3_gnn_be{l + 1}"]), ALU.add))
                    step(tt(X[:], X[:], H[:, 0:NT * D], ALU.add), out_ready)

            v.wait_ge(seg0_loaded, 16)
            for k in range(K):
                if k in (0, 1, 2, 5):
                    layer_input(k)
                if k != 1:
                    rows_product(k)
                if k in GAT:
                    attention(k)
                zero_acc(k)
                v.wait_ge(table_stored, 16 + k * 16)
                if k == 0:
                    step(memset(macc, 0.0))
                if k == 1:
                    product_pass()
                else:
                    edge_pass(k)
                if k == 0:
                    segment_facts()
                segments_out(k)
                if k == 0:
                    node_facts()
                if k == 1:
                    product_layer()
                elif k in SAGE:
                    mean_layer(k)
                else:
                    attention_layer(k)


CONSTS = 9
LOADS = 12 + 20 + 11 + 9 + 2
_NAMES = ["x", "src", "dst", "edge_attr_128", "edge_attr_3", "edge_weight", "L0_gnn_W_self", "L0_gnn_W_neigh",
          "L0_gnn_bias", "L1_gnn_W1", "L1_gnn_b1", "L1_gnn_W2", "L1_gnn_b2", "L1_gnn_W3", "L1_gnn_b3",
          "L2_gnn_W_agg", "L2_gnn_W_root", "L2_gnn_b"]
_NAMES += [f"L3_gnn_{n}{l}" for l in (1, 2, 3) for n in ("W", "as", "ad", "We", "ae", "b", "g", "be")]


def kernel(**inputs):
    import concourse.bacc as _bacc
    from concourse.bass_utils import run_bass_kernel_spmd as _run

    nc = _bacc.Bacc("TRN2", target_bir_lowering=False, num_devices=1)
    arrays, aps = {}, {}
    for name in _NAMES:
        x = np.ascontiguousarray(inputs[name])
        arrays[f"in_{name}"] = x
        aps[name] = nc.dram_tensor(f"in_{name}", x.shape, mybir.dt.from_np(x.dtype), kind="ExternalInput").ap()
    out = nc.dram_tensor("out_x", (N, D), F32, kind="ExternalOutput").ap()
    build(nc, aps, out)
    r = _run(nc, [arrays], core_ids=[0])
    return r.results[0]["out_x"]
```

```python
from contextlib import ExitStack

import numpy as np
import concourse.bass as bass
from concourse import mybir

ALU = mybir.AluOpType
ACT = mybir.ActivationFunctionType
F32 = mybir.dt.float32
I32 = mybir.dt.int32
BF16 = mybir.dt.bfloat16
AX = mybir.AxisListType

P = 128
N, E, D = 6250, 100000, 128
NT = -(-N // P)
NPAD = NT * P
NLAST = N - (NT - 1) * P
CH = 7
NCH = NT // CH
CW = CH * D
ET = 784
EPAD = ET * P
HT = 8
BT = 2 * HT
ITERS = ET // BT
BE = BT * P
TB = 112
NB = ET // TB
ACCW = 6400
SROWS = E - (P - 1) * ET
BIGPOS = float(1 << 20)
HUGE = 1.0e30
LN2 = 0.6931471805599453
R_MAX = 5.0
DELTA = R_MAX / (D - 1)
COEFF = -0.5 / (DELTA * DELTA)
EPS = 1e-5
MAGIC = 12582912.0
K = 8
SAGE = (0, 2, 3, 4)
GAT = (5, 6, 7)


def build(nc, a, out):
    ds = bass.ds
    with ExitStack() as ctx:
        def sb(name, shape, dt=F32):
            return ctx.enter_context(nc.sbuf_tensor(name, shape, dt))

        def sem(name):
            return ctx.enter_context(nc.semaphore(name))

        def sems(name, n):
            return [sem(f"{name}{i}") for i in range(n)]

        def dram(name, shape, dt=F32):
            return nc.dram_tensor(name, shape, dt, kind="Internal").ap()

        table = [dram("table0", (NPAD, D)), dram("table1", (NPAD, D))]
        seg_rows = dram("seg_rows", (NPAD, D))
        flats = dram("flats", (4, EPAD))
        flat_bf = dram("flat_bf", (10, EPAD), BF16)
        first_of_tile = dram("first_of_tile", (ET,), I32)
        node_table = dram("node_table", (NPAD, 4))
        at_first = dram("at_first", (EPAD, 2))
        at_last = dram("at_last", (EPAD, 2))
        al_flat = dram("al_flat", (EPAD,))
        ex_flat = dram("ex_flat", (EPAD,))

        X = sb("X", [P, NT * D])
        H = sb("H", [P, ACCW])
        G = sb("G", [P, NT * D])
        T = sb("T", [P, NT * D])
        acc = sb("acc", [P, ACCW])
        rows = sb("rows", [P, BT, D])
        onehot = sb("onehot", [P, BT, D])
        idx_buf = sb("idx_buf", [P, BT], I32)
        meta_buf = sb("meta_buf", [P, BT * 3])
        iota_coli = sb("iota_coli", [P, 1], I32)
        src_t = sb("src_t", [P, ET], I32)
        srchi_t = sb("srchi_t", [P, ET])
        loc_t = sb("loc_t", [P, ET])
        loclast_t = sb("loclast_t", [P, ET])
        als_bf = sb("als_bf", [P, 3 * NT], BF16)
        ex_t = sb("ex_t", [P, ET])
        als_t = sb("als_t", [P, ET])
        same_s = sb("same_s", [P, ET])
        last_s = sb("last_s", [P, ET])
        seg0_row = sb("seg0_row", [1, ET], I32)
        vecs = sb("vecs", [P, 20 * D])
        mats = sb("mats", [P, 14 * D])
        iota_row = sb("iota_row", [P, D])
        iota_col = sb("iota_col", [P, 1])
        iota_int = sb("iota_int", [P, D], I32)
        ident = sb("ident", [P, P])
        before = sb("before", [P, P])
        ones = sb("ones", [P, P])
        ones_bf = sb("ones_bf", [3, P], BF16)
        pick_keep = sb("pick_keep", [6, P], BF16)
        pick_start = sb("pick_start", [6, P], BF16)
        rowmask = sb("rowmask", [P, 1])
        node_info = sb("node_info", [P, NT * 4])
        cmap = sb("cmap", [P, NT], I32)
        firstpos = sb("firstpos", [P, NT], I32)
        lastpos = sb("lastpos", [P, NT], I32)
        rcount = sb("rcount", [P, NT])
        small = sb("small", [P, 8 * NT])
        nd = sb("nd", [P, NT * 2])
        cols = sb("cols", [P, 64])
        edge_cols = sb("edge_cols", [P, 2], I32)
        carry_cols = sb("carry_cols", [P, 2])
        carry_row = sb("carry_row", [1, 4 * P])
        carry_in = sb("carry_in", [P, 1])
        bias_cols = sb("bias_cols", [P, 4])
        ids_int = sb("ids_int", [P, NT], I32)
        seg0_blk = sb("seg0_blk", [P, NB], I32)
        PS = ctx.enter_context(nc.psum_tensor("PS", [P, 8 * 512], F32))

        def bank(b, w=512):
            return PS[:, b * 512:b * 512 + w]

        X3 = X[:].rearrange("p (t f) -> p t f", f=D)
        G3 = G[:].rearrange("p (t f) -> p t f", f=D)
        T3 = T[:].rearrange("p (t f) -> p t f", f=D)
        H3 = H[:, 0:NT * D].rearrange("p (t f) -> p t f", f=D)
        stage = onehot[:].rearrange("p a b -> p (a b)")
        stage_in, stage_mid = stage[:, 0:CW], stage[:, 1024:1024 + CW]
        stage_out = rows[:].rearrange("p a b -> p (a b)")[:, 0:CW]
        macc = H[0:3, :]
        meta_t = G[:, 0:3 * ET]

        def scan_tmp(buf, i):
            return buf[:, i * ET:(i + 1) * ET]

        def vec(i):
            return vecs[:, i * D:(i + 1) * D]

        def vec_nodes(i, tiles=NT):
            return vec(i).unsqueeze(1).broadcast_to([P, tiles, D])

        def mat(i):
            return mats[:, i * D:(i + 1) * D]

        VEC = ["L0_gnn_bias", "L1_gnn_b3", "L2_0", "L2_1", "L2_2"]
        for l in (1, 2, 3):
            VEC += [f"L3_gnn_as{l}", f"L3_gnn_ad{l}", f"L3_gnn_b{l}", f"L3_gnn_g{l}", f"L3_gnn_be{l}"]
        vsrc = {n: a[n] for n in VEC if not n.startswith("L2_")}
        for l in range(3):
            vsrc[f"L2_{l}"] = a["L2_gnn_b"][l, :]
        MAT = ["ws_raw", "wn_raw", "ws", "wn", "W1", "W2", "W3", "agg0", "agg1", "agg2",
               "root0", "root1", "root2"]
        msrc = {"ws_raw": a["L0_gnn_W_self"], "wn_raw": a["L0_gnn_W_neigh"], "W1": a["L1_gnn_W1"],
                "W2": a["L1_gnn_W2"], "W3": a["L1_gnn_W3"]}
        for l in range(3):
            msrc[f"agg{l}"] = a["L2_gnn_W_agg"][l, :, :]
            msrc[f"root{l}"] = a["L2_gnn_W_root"][l, :, :]
        gat_w = sb("gat_w", [P, 3 * D])
        V = {n: i for i, n in enumerate(VEC)}
        M = {n: i for i, n in enumerate(MAT)}
        row_matrix = {0: mat(M["ws"]), 2: mat(M["root0"]), 3: mat(M["root1"]), 4: mat(M["root2"]),
                      5: gat_w[:, 0:D], 6: gat_w[:, D:2 * D], 7: gat_w[:, 2 * D:3 * D]}
        seg_matrix = {0: mat(M["wn"]), 1: mat(M["W3"]), 2: mat(M["agg0"]), 3: mat(M["agg1"]),
                      4: mat(M["agg2"]), 5: ident[:], 6: ident[:], 7: ident[:]}
        bias_vec = {0: V["L0_gnn_bias"], 1: V["L1_gnn_b3"], 2: V["L2_0"], 3: V["L2_1"], 4: V["L2_2"],
                    5: V["L3_gnn_b1"], 6: V["L3_gnn_b2"], 7: V["L3_gnn_b3"]}

        def wide(buf, i):
            return buf[:, i * BE:(i + 1) * BE]
        rbf, lnp = wide(H, 0), wide(H, 1)
        attr = wide(G, 1)
        msg0 = wide(G, 2)
        msgf = wide(T, 0)
        keep = wide(T, 1)
        prod = wide(T, 2)
        filt = wide(H, 2)
        dist_row = sb("dist_row", [3, BE], BF16)
        cut_row = sb("cut_row", [6, BE], BF16)
        lo_row = cut_row[0:1, :]

        dst_i, src_i, ew = scan_tmp(T, 0).bitcast(I32), scan_tmp(T, 1).bitcast(I32), scan_tmp(T, 2)
        dst_f, src_f, seg_s = scan_tmp(T, 3), scan_tmp(T, 4), scan_tmp(T, 5)
        cut_s, w0, w1, w2 = scan_tmp(T, 6), scan_tmp(T, 7), scan_tmp(H, 0), scan_tmp(H, 1)
        first_s, ones_s = scan_tmp(H, 2), scan_tmp(acc, 2)
        bf = H[:, 3 * ET:8 * ET].bitcast(BF16).rearrange("p (q e) -> p q e", q=10)
        blocks = acc[0:TB, 0:4 * NB * P].rearrange("p (q b c) -> p q b c", q=4, c=P)
        pos_i = acc[:, 5600:5600 + ET].bitcast(I32)
        dst_t, last_t, srcf_t = scan_tmp(T, 0), scan_tmp(T, 1), scan_tmp(T, 2)
        we_bc = G[:, 3 * ET:3 * ET + 9 * D]
        ae_bc = G[:, 3 * ET + 9 * D:3 * ET + 12 * D]
        wprod = G[:, 3 * ET + 12 * D:3 * ET + 21 * D]
        HALF_PI, NEGC, ASUM, VV, AMEAN, ALLSAME, NOLAST, PENALL, EPSC, TOTAL = 0, 1, 2, 5, 14, 17, 18, 19, 20, 21
        AMN, EDGE, THIRTY = 22, 25, 40

        def col(i, n=1):
            return cols[:, i:i + n]

        Gs = [scan_tmp(G, i) for i in range(8)]
        Hs = [scan_tmp(H, i) for i in range(4)]
        turned = H[0:TB, 4 * ET:4 * ET + NB * P]
        at_f = G[:, ET:3 * ET].rearrange("p (j c) -> p j c", c=2)
        at_l = H[:, 0:2 * ET].rearrange("p (j c) -> p j c", c=2)
        hot_bf = onehot[:].rearrange("p a b -> p (a b)")[:, 0:BE // 2].bitcast(BF16)\
            .rearrange("p (h a b) -> p h a b", h=2, b=D)
        nd3 = nd[:].rearrange("p (t c) -> p t c", c=2)
        attr_pre = G[:, 0:3 * ET]
        attr_att = acc[:, 0:3 * ET]
        attr3 = attr_att.rearrange("p (j c) -> p j c", c=3)
        info3 = node_info[:].rearrange("p (t c) -> p t c", c=4)
        als_n, ald_n, self_n, amax_n, exs_n, rden_n = (small[:, i * NT:(i + 1) * NT] for i in range(6))
        stat0, stat1 = small[:, 6 * NT:7 * NT], small[:, 7 * NT:8 * NT]

        consts = sem("consts")
        pads_set = sem("pads_set")
        loads = sem("loads")
        dve = sem("dve")
        act = sem("act")
        pre_in = sem("pre_in")
        pre_out = sem("pre_out")
        cut_in = sem("cut_in")
        cut_out = sem("cut_out")
        zeros_ready = sem("zeros_ready")
        zeros_stored = sem("zeros_stored")
        flats_ready = sem("flats_ready")
        flats_stored = sem("flats_stored")
        blocks_loaded = sem("blocks_loaded")
        seg0_ready = sem("seg0_ready")
        seg0_stored = sem("seg0_stored")
        seg0_loaded = sem("seg0_loaded")
        loc_ready = sem("loc_ready")
        tiles_turned = sem("tiles_turned")
        tiles_copied = sem("tiles_copied")
        tiles_ready = sem("tiles_ready")
        info_turned = sem("info_turned")
        info_ready = sem("info_ready")
        info_scattered = sem("info_scattered")
        info_loaded = sem("info_loaded")
        info_cols = sem("info_cols")
        h_ready = sem("h_ready")
        table_stored = sem("table_stored")
        p_staged = sem("p_staged")
        p_turned = sem("p_turned")
        p_copied = sem("p_copied")
        p_product = sem("p_product")
        p_done = sem("p_done")
        idx_loaded = sems("idx_loaded", 2)
        gathered = sems("gathered", 2)
        onehot_ready = sems("onehot_ready", 2)
        multiplied = sems("multiplied", 2)
        added = sems("added", 2)
        meta_staged = sems("meta_staged", 2)
        meta_added = sems("meta_added", 2)
        c_staged = sem("c_staged")
        c_product = sem("c_product")
        c_copied = sem("c_copied")
        c_stored = sem("c_stored")
        node_rows = sems("node_rows", NCH)
        dist_in = sem("dist_in")
        cut_in_row = sem("cut_in_row")
        attr_in = sem("attr_in")
        dist_bc = sem("dist_bc")
        squared = sem("squared")
        rbf_ready = sem("rbf_ready")
        z_ready = sems("z_ready", 2)
        clamped = sems("clamped", 2)
        exp_done = sems("exp_done", 2)
        ln_done = sems("ln_done", 2)
        soft_ready = sems("soft_ready", 2)
        msg_ready = sems("msg_ready", 2)
        msg_turned = sem("msg_turned")
        msgf_ready = sem("msgf_ready")
        keep_bc = sem("keep_bc")
        start_bc = sem("start_bc")
        keep_ready = sem("keep_ready")
        start_ready = sem("start_ready")
        scanned = sem("scanned")
        scan_turned = sem("scan_turned")
        scan_copied = sem("scan_copied")
        win_ready = sem("win_ready")
        ln_in = sem("ln_in")
        ln_out = sem("ln_out")
        var_ready = sem("var_ready")
        std_ready = sem("std_ready")
        sum_in = sem("sum_in")
        sum_out = sem("sum_out")
        attr_space = sem("attr_space")
        attr_again = sem("attr_again")
        lo_in = sems("lo_in", 2)
        lo_bc = sems("lo_bc", 2)
        lo_hot = sems("lo_hot", 2)
        al_rows = sems("al_rows", 2)
        al_mask = sems("al_mask", 2)
        al_pick = sems("al_pick", 2)
        al_done = sems("al_done", 2)
        turn_in = sem("turn_in")
        turn_out = sem("turn_out")
        turn_blk = sem("turn_blk")
        al_stored = sem("al_stored")
        al_loaded = sem("al_loaded")
        first_in = sem("first_in")
        first_sc = sem("first_sc")
        first_ld = sem("first_ld")
        last_in = sem("last_in")
        last_st = sem("last_st")
        last_fill = sem("last_fill")
        last_ga = sem("last_ga")
        exp_in = sem("exp_in")
        exp_out = sem("exp_out")
        ex_stored = sem("ex_stored")
        ex_loaded = sem("ex_loaded")
        ex_turned = sem("ex_turned")
        self_in = sem("self_in")
        self_out = sem("self_out")
        carry_in_ready = sem("carry_in_ready")
        carry_rows = sem("carry_rows")
        carry_scanned = sem("carry_scanned")
        carry_cols_out = sem("carry_cols_out")
        out_ready = sem("out_ready")
        out_stored = sem("out_stored")

        turn = {k: k - (k > 1) for k in range(K)}

        def hold(eng):
            eng.nop(nofuse=True)

        def stepper(eng, own):
            count = {}

            def step(ins, s=own):
                count[s] = count.get(s, 0) + 1
                ins.then_inc(s, 1)
                eng.wait_ge(s, count[s])
            return step

        ctx.enter_context(nc.allow_non_contiguous_dma(reason="a few hundred single words at the start"))
        block = ctx.enter_context(nc.Block())

        @block.sync
        def _(sp):
            sp.wait_ge(pads_set, 1)
            sent = []

            def load(dst, src):
                sp.dma_start(dst, src).then_inc(loads, 16)
                sent.append(1)

            head_e = (P - 1) * ET
            for dst, name in ((dst_i, "dst"), (src_i, "src"), (ew, "edge_weight")):
                load(dst[0:P - 1, :], a[name][0:head_e].rearrange("(p j) -> p j", j=ET))
                load(dst[P - 1:P, 0:SROWS], a[name][head_e:E].unsqueeze(0))
            load(edge_cols[1:P, 0:1], a["dst"][ET - 1:ET + (P - 2) * ET:ET].unsqueeze(1))
            load(edge_cols[0:P - 1, 1:2], a["dst"][ET:ET + (P - 2) * ET + 1:ET].unsqueeze(1))
            attr_head = a["edge_attr_3"][0:head_e, :].rearrange("(p j) c -> p (j c)", j=ET)
            attr_rest = a["edge_attr_3"][head_e:E, :].rearrange("(o j) c -> o (j c)", o=1)
            load(attr_pre[0:P - 1, :], attr_head)
            load(attr_pre[P - 1:P, 0:3 * SROWS], attr_rest)
            load(X3[:, 0:NT - 1, :], a["x"][0:(NT - 1) * P, :].rearrange("(t p) f -> p t f", p=P))
            load(X3[0:NLAST, NT - 1, :], a["x"][(NT - 1) * P:N, :])
            for n, i in V.items():
                load(vec(i), vsrc[n].unsqueeze(0).broadcast_to([P, D]))
            for n in msrc:
                load(mat(M[n]), msrc[n])
            for l in range(3):
                load(gat_w[:, l * D:(l + 1) * D], a[f"L3_gnn_W{l + 1}"])
                load(we_bc[:, l * 3 * D:(l + 1) * 3 * D],
                     a[f"L3_gnn_We{l + 1}"].rearrange("(o c) f -> o (c f)", o=1).broadcast_to([P, 3 * D]))
                load(ae_bc[:, l * D:(l + 1) * D], a[f"L3_gnn_ae{l + 1}"].unsqueeze(0).broadcast_to([P, D]))
            load(bias_cols[:, 0:1], a["L1_gnn_b1"].unsqueeze(1))
            load(bias_cols[:, 1:2], a["L1_gnn_b2"].unsqueeze(1))
            assert len(sent) == LOADS

            sp.wait_ge(zeros_ready, 1)
            sp.dma_start(at_first.rearrange("(p j) c -> p (j c)", p=P), acc[:, 0:2 * ET]).then_inc(zeros_stored, 16)
            sp.dma_start(node_table.rearrange("(t p) c -> p t c", p=P), info3).then_inc(zeros_stored, 16)

            sp.wait_ge(flats_ready, 1)
            for q, t in enumerate((seg_s, dst_f, last_s[:], src_f)):
                sp.dma_start(flats[q, :].rearrange("(p j) -> p j", p=P), t).then_inc(flats_stored, 16)
            for q in range(10):
                sp.dma_start(flat_bf[q, :].rearrange("(p j) -> p j", p=P), bf[:, q, :]).then_inc(flats_stored, 16)
            sp.wait_ge(flats_stored, 16 * 14)
            sp.wait_ge(zeros_stored, 32)
            for q in range(4):
                sp.dma_start(blocks[:, q, :, :], flats[q, :].rearrange("(b t c) -> t b c", t=TB, c=P))\
                    .then_inc(blocks_loaded, 16)
            sp.wait_ge(seg0_ready, 1)
            sp.dma_start(first_of_tile.rearrange("(b t) -> t b", t=TB), seg0_blk[0:TB, :]).then_inc(seg0_stored, 16)
            sp.wait_ge(seg0_stored, 16)
            sp.dma_start(seg0_row[:], first_of_tile.unsqueeze(0)).then_inc(seg0_loaded, 16)

            def index_load(k, i, h):
                sp.wait_ge(gathered[h], i * (16 * HT) + k * (ITERS * 16 * HT))
                sp.dma_start(idx_buf[:, h * HT:(h + 1) * HT], src_t[:, ds(i * BT + h * HT, HT)])\
                    .then_inc(idx_loaded[h], 16)

            def product_loads(i):
                sp.wait_ge(dist_bc, i * 4)
                sp.dma_start(dist_row[:], flat_bf[0:3, ds(i * BE, BE)]).then_inc(dist_in, 16)
                for h in range(2):
                    sp.wait_ge(msg_ready[h], i * 2)
                if isinstance(i, int):
                    full = (E - i * BE) // P
                    sp.dma_start(attr[:, 0:full * D].rearrange("p (t f) -> p t f", f=D),
                                 a["edge_attr_128"][i * BE:i * BE + full * P, :].rearrange("(t p) f -> p t f", p=P))\
                        .then_inc(attr_in, 16)
                    sp.dma_start(attr[0:E - i * BE - full * P, full * D:(full + 1) * D],
                                 a["edge_attr_128"][i * BE + full * P:E, :]).then_inc(attr_in, 16)
                else:
                    for q in range(4):
                        sp.dma_start(attr[:, q * 512:(q + 1) * 512].rearrange("p (t f) -> p t f", f=D),
                                     a["edge_attr_128"][ds(i * BE + q * 512, 512), :].rearrange("(t p) f -> p t f", p=P))\
                            .then_inc(attr_in, 16)
                for h in range(2):
                    index_load(1, i, h)
                sp.wait_ge(start_bc, i * 4)
                sp.dma_start(cut_row[:], flat_bf[3:9, ds(i * BE, BE)]).then_inc(cut_in_row, 16)

            for k in range(K):
                if k in GAT:
                    l = k - 5
                    sp.wait_ge(attr_space, l + 1)
                    sp.dma_start(attr_att[0:P - 1, :], attr_head).then_inc(attr_again, 16)
                    sp.dma_start(attr_att[P - 1:P, 0:3 * SROWS], attr_rest).then_inc(attr_again, 16)
                    sp.wait_ge(p_done, NCH + turn[k] * NCH)
                    sp.dma_start(table[k % 2].rearrange("(t p) f -> p t f", p=P), T3).then_inc(table_stored, 16)
                    with sp.Fori(0, ITERS) as i:
                        for h in range(2):
                            sp.wait_ge(lo_bc[h], i + l * ITERS)
                            sp.dma_start(lo_row[:, h * 1024:(h + 1) * 1024], flat_bf[9:10, ds(i * BE + h * 1024, 1024)])\
                                .then_inc(lo_in[h], 16)
                    sp.wait_ge(turn_blk, l + 1)
                    sp.dma_start(al_flat.rearrange("(b t c) -> t b c", t=TB, c=P),
                                 turned.rearrange("p (b c) -> p b c", c=P)).then_inc(al_stored, 16)
                    sp.wait_ge(al_stored, 16 * (l + 1))
                    sp.dma_start(Gs[0], al_flat.rearrange("(p j) -> p j", p=P)).then_inc(al_loaded, 16)
                    sp.wait_ge(first_sc, 16 * NT * (l + 1))
                    sp.dma_start(G[:, ET:3 * ET], at_first.rearrange("(p j) c -> p (j c)", p=P)).then_inc(first_ld, 16)
                    sp.wait_ge(exp_out, l + 1)
                    sp.dma_start(ex_flat.rearrange("(p j) -> p j", p=P), Gs[6]).then_inc(ex_stored, 16)
                    sp.wait_ge(ex_stored, 16 * (l + 1))
                    sp.dma_start(turned.rearrange("p (b c) -> p b c", c=P),
                                 ex_flat.rearrange("(b t c) -> t b c", t=TB, c=P)).then_inc(ex_loaded, 16)
                    sp.wait_ge(last_in, l + 1)
                    sp.dma_start(at_last.rearrange("(p j) c -> p (j c)", p=P), H[:, 0:2 * ET]).then_inc(last_st, 16)
                else:
                    sp.wait_ge(h_ready, 1 + k)
                    sp.dma_start(table[k % 2].rearrange("(t p) f -> p t f", p=P), H3).then_inc(table_stored, 16)
                if k == 0:
                    sp.wait_ge(tiles_ready, 1)
                if k == 1:
                    with sp.Fori(0, ITERS - 1) as i:
                        product_loads(i)
                    product_loads(ITERS - 1)
                else:
                    with sp.Fori(0, ITERS) as i:
                        for h in range(2):
                            index_load(k, i, h)
                with sp.Fori(0, NCH) as i:
                    sp.wait_ge(c_copied, i + 1 + k * NCH)
                    sp.dma_start(seg_rows[ds(i * (CH * P), CH * P), :].rearrange("(t p) f -> p t f", p=P),
                                 stage_out.rearrange("p (t f) -> p t f", f=D)).then_inc(c_stored, 16)
                if k == 0:
                    sp.wait_ge(info_scattered, 16 * NT)
                    sp.dma_start(info3, node_table.rearrange("(t p) c -> p t c", p=P)).then_inc(info_loaded, 16)
            sp.wait_ge(out_ready, 1)
            sp.dma_start(out[0:(NT - 1) * P, :].rearrange("(t p) f -> p t f", p=P), X3[:, 0:NT - 1, :]).then_inc(out_stored, 16)
            sp.dma_start(out[(NT - 1) * P:N, :], X3[0:NLAST, NT - 1, :]).then_inc(out_stored, 16)
            sp.wait_ge(out_stored, 32)

        @block.gpsimd
        def _(pool):
            step = stepper(pool, consts)
            step(pool.iota(iota_int[:], pattern=[[1, D]], base=0, channel_multiplier=0))
            step(pool.iota(iota_coli[:], pattern=[[0, 1]], base=0, channel_multiplier=1))
            step(pool.iota(ids_int[:], pattern=[[P, NT]], base=0, channel_multiplier=1))
            step(pool.iota(pos_i, pattern=[[P, ET]], base=0, channel_multiplier=1))
            step(pool.memset(ones[:], 1.0))
            step(pool.memset(ident[:], 0.0))
            step(pool.affine_select(out=ident[:], in_=ident[:], compare_op=ALU.not_equal, fill=1.0, base=0,
                                    pattern=[[-1, P]], channel_multiplier=1))
            step(pool.affine_select(out=before[:], in_=ones[:], compare_op=ALU.is_gt, fill=0.0, base=0,
                                    pattern=[[1, P]], channel_multiplier=-1))
            step(pool.affine_select(out=rowmask[:], in_=ones[:, 0:1], compare_op=ALU.is_gt, fill=0.0, base=NLAST,
                                    pattern=[[0, 1]], channel_multiplier=-1))

            def at(idx):
                return bass.IndirectOffsetOnAxis(idx, 0)

            for k in range(K):
                if k in GAT:
                    l = k - 5
                    pool.wait_ge(first_in, l + 1)
                    for t in range(NT):
                        pool.indirect_dma_start(at_first, at(firstpos[:, t:t + 1]), nd[:, 2 * t:2 * t + 2], None,
                                                bounds_check=EPAD - 1, oob_is_err=False).then_inc(first_sc, 16)
                pool.wait_ge(table_stored, 16 + k * 16)
                with pool.Fori(0, ITERS) as i:
                    for h in range(2):
                        pool.wait_ge(idx_loaded[h], 16 * (i + 1) + k * (ITERS * 16))
                        if k == 1:
                            pool.wait_ge(msg_ready[h], i * 2)
                        else:
                            pool.wait_ge(multiplied[h], i + turn[k] * ITERS)
                        hold(pool)
                        for j in range(h * HT, (h + 1) * HT):
                            pool.indirect_dma_start(rows[:, j, :], None, table[k % 2], at(idx_buf[:, j:j + 1]))\
                                .then_inc(gathered[h], 16)
                if k == 0:
                    pool.wait_ge(info_ready, 1)
                    for t in range(NT):
                        pool.indirect_dma_start(node_table, at(cmap[:, t:t + 1]), node_info[:, 4 * t:4 * t + 4], None,
                                                bounds_check=NPAD - 1, oob_is_err=False).then_inc(info_scattered, 16)
                    pool.wait_ge(info_cols, 1)
                if k in GAT:
                    pool.wait_ge(last_st, 16 * (l + 1))
                    pool.wait_ge(last_fill, l + 1)
                    for t in range(NT):
                        pool.indirect_dma_start(nd[:, 2 * t:2 * t + 2], None, at_last, at(lastpos[:, t:t + 1]),
                                                bounds_check=EPAD - 1, oob_is_err=False).then_inc(last_ga, 16)
                for t in range(NT):
                    if t == 0 or (t + 1) % CH == 0:
                        pool.wait_ge(c_stored, 16 * min(NCH, (t + 1) // CH + 1) + k * (NCH * 16))
                    pool.indirect_dma_start(G3[:, t, :], None, seg_rows, at(cmap[:, t:t + 1])).then_inc(node_rows[t // CH], 16)

        @block.scalar
        def _(s):
            step = stepper(s, act)
            s.wait_ge(cut_in, 1)
            step(nc.scalar.activation(w0, w0, ACT.Abs))
            nc.scalar.activation(w1, w0, ACT.Sin, bias=col(HALF_PI), scale=-2.0 * np.pi).then_inc(cut_out, 1)
            n_sqrt = 0

            def sqrt(scale, src, dst):
                nonlocal n_sqrt
                n_sqrt += 1
                s.wait_ge(var_ready, n_sqrt)
                nc.scalar.activation(dst, src, ACT.Sqrt, bias=col(EPSC), scale=scale).then_inc(std_ready, 1)

            def stage_rows(k):
                s.wait_ge(h_ready, 1 + k)
                with s.Fori(0, NCH) as i:
                    s.wait_ge(p_turned, i + turn[k] * NCH)
                    hold(s)
                    nc.scalar.activation(stage_in, H[:, ds(i * CW, CW)], ACT.Copy).then_inc(p_staged, 1)

            def stage_segments(k):
                for h in range(2):
                    s.wait_ge(added[h], ITERS * HT + k * (ITERS * HT))
                with s.Fori(0, NCH) as i:
                    s.wait_ge(c_product, i + k * NCH)
                    hold(s)
                    nc.scalar.activation(stage_in, acc[:, ds(i * CW, CW)], ACT.Copy).then_inc(c_staged, 1)

            def rbf_steps(i):
                for q in range(4):
                    w = slice(q * 512, (q + 1) * 512)
                    s.wait_ge(dist_bc, i * 4 + q + 1)
                    s.wait_ge(z_ready[1], i * 4)
                    hold(s)
                    nc.scalar.activation(rbf[:, w], bank(q), ACT.Square, bias=col(NEGC)).then_inc(squared, 1)
                    s.wait_ge(squared, i * 4 + q + 1)
                    nc.scalar.activation(rbf[:, w], rbf[:, w], ACT.Exp, scale=COEFF).then_inc(rbf_ready, 1)

            def soft_steps(i, n):
                for q in range(4):
                    w = slice(q * 512, (q + 1) * 512)
                    s.wait_ge(z_ready[n], i * 4 + q + 1)
                    s.wait_ge(soft_ready[1 - n], (i + n) * 4)
                    hold(s)
                    nc.scalar.activation(lnp[:, w], bank(q), ACT.Relu, bias=bias_cols[:, 2 + n:3 + n], scale=-1.0)\
                        .then_inc(clamped[n], 1)
                    s.wait_ge(clamped[n], i * 4 + q + 1)
                    nc.scalar.activation(lnp[:, w], lnp[:, w], ACT.Exp, bias=col(THIRTY), scale=-1.0).then_inc(exp_done[n], 1)
                    s.wait_ge(exp_done[n], i * 4 + q + 1)
                    nc.scalar.activation(lnp[:, w], lnp[:, w], ACT.Ln, bias=1.0).then_inc(ln_done[n], 1)

            def scan_copies(i):
                for q in range(4):
                    s.wait_ge(scan_turned, i * 4 + q + 1)
                    nc.scalar.activation(msg0[:, q * 512:(q + 1) * 512], bank(4 + q), ACT.Copy).then_inc(scan_copied, 1)

            for k in range(K):
                if k in (0, 1, 2, 5):
                    sqrt(1.0 / D, stat1, stat1)
                if k != 1:
                    stage_rows(k)
                if k == 0:
                    s.wait_ge(tiles_ready, 1)
                    with s.Fori(0, ITERS) as i:
                        for h in range(2):
                            s.wait_ge(multiplied[h], i + turn[0] * ITERS)
                            hold(s)
                            nc.scalar.activation(meta_buf[:, h * HT * 3:(h + 1) * HT * 3],
                                                 meta_t[:, ds(i * (BT * 3) + h * HT * 3, HT * 3)],
                                                 ACT.Copy).then_inc(meta_staged[h], 1)
                if k == 1:
                    s.preload_act_table_set("natural_log_exp_and_others")
                    s.wait_ge(table_stored, 32)
                    rbf_steps(0)
                    soft_steps(0, 0)
                    soft_steps(0, 1)
                    with s.Fori(0, ITERS - 1) as i:
                        rbf_steps(i + 1)
                        soft_steps(i + 1, 0)
                        scan_copies(i)
                        soft_steps(i + 1, 1)
                    scan_copies(ITERS - 1)
                if k in GAT:
                    s.wait_ge(exp_in, k - 4)
                    nc.scalar.activation(Gs[6], Gs[5], ACT.Exp).then_inc(exp_out, 1)
                stage_segments(k)
                if k == 1:
                    s.wait_ge(ln_in, 1)
                    step(nc.scalar.activation(T[:], T[:], ACT.Exp))
                    nc.scalar.activation(T[:], T[:], ACT.Ln, bias=1.0).then_inc(ln_out, 1)
                if k in GAT:
                    s.wait_ge(self_in, k - 4)
                    nc.scalar.activation(exs_n, exs_n, ACT.Exp).then_inc(self_out, 1)
                    sqrt(1.0 / N, acc[:, 2 * D:3 * D], acc[:, 3 * D:4 * D])

        @block.tensor
        def _(pe):
            mm, tr = nc.tensor.matmul, nc.tensor.transpose
            pe.wait_ge(consts, CONSTS)
            pe.wait_ge(loads, 16 * LOADS)
            pe.wait_ge(pre_in, 1)
            tr(PS[:, 0:D], mat(M["ws_raw"]), ident[:])
            tr(PS[:, D:2 * D], mat(M["wn_raw"]), ident[:])
            mm(PS[:, 512:513], mat(M["W2"]), ones[:, 0:1], start=True, stop=True)
            mm(PS[:, 1024:1025], before[:], col(TOTAL), start=True, stop=True)
            mm(PS[:, 1536:1539], ones[:], col(ASUM, 3), start=True, stop=True).then_inc(pre_out, 1)
            pe.wait_ge(blocks_loaded, 64)
            pe.wait_ge(loc_ready, 1)
            for q in range(4):
                base = 2048 + (q % 2) * 1024
                if q >= 2:
                    pe.wait_ge(tiles_copied, q - 1)
                for b in range(NB):
                    o = base + (b // 4) * 512 + (b % 4) * TB
                    last = tr(PS[:, o:o + TB], blocks[:, q, b, :], ident[0:TB, 0:TB])
                last.then_inc(tiles_turned, 1)

            def rows_product(k):
                with pe.Fori(0, NCH) as i:
                    pe.wait_ge(p_staged, i + 1 + turn[k] * NCH)
                    pe.wait_ge(p_copied, i + turn[k] * NCH)
                    for j in range(CH):
                        last = tr(PS[:, j * D:(j + 1) * D], stage_in[:, j * D:(j + 1) * D], ident[:])
                    last.then_inc(p_turned, 1)
                    pe.wait_ge(p_copied, i + 1 + turn[k] * NCH)
                    pe.wait_ge(p_done, i + turn[k] * NCH)
                    for j in range(CH):
                        last = mm(PS[:, 1024 + j * D:1024 + (j + 1) * D], stage_mid[:, j * D:(j + 1) * D],
                                  row_matrix[k], start=True, stop=True)
                    last.then_inc(p_product, 1)

            def segment_product(k):
                with pe.Fori(0, NCH) as i:
                    pe.wait_ge(c_staged, i + 1 + k * NCH)
                    pe.wait_ge(c_copied, i + k * NCH)
                    for j in range(CH):
                        last = mm(PS[:, 1024 + j * D:1024 + (j + 1) * D], stage_in[:, j * D:(j + 1) * D],
                                  seg_matrix[k], start=True, stop=True)
                    last.then_inc(c_product, 1)

            def edge_pass(k):
                with pe.Fori(0, ITERS) as i:
                    for h in range(2):
                        pe.wait_ge(gathered[h], (i + 1) * (16 * HT) + k * (ITERS * 16 * HT))
                        pe.wait_ge(onehot_ready[h], i + 1 + k * ITERS)
                        pe.wait_ge(added[h], i * HT + k * (ITERS * HT))
                        if k == 0:
                            pe.wait_ge(meta_staged[h], i + 1)
                            pe.wait_ge(meta_added[h], i * HT)
                        for j in range(HT):
                            o, r = h * 1024 + j * D, h * HT + j
                            last = mm(PS[:, o:o + D], rows[:, r, :], onehot[:, r, :], start=True, stop=True)
                            if k == 0:
                                last = mm(PS[0:3, 2048 + o:2048 + o + D], meta_buf[:, 3 * r:3 * r + 3],
                                          onehot[:, r, :], start=True, stop=True)
                        last.then_inc(multiplied[h], 1)

            def filter_step(i, n):
                for q in range(4):
                    pe.wait_ge(soft_ready[0] if n else rbf_ready, i * 4 + q + 1)
                    mm(bank(q), mat(M["W2" if n else "W1"]), rbf[:, q * 512:(q + 1) * 512],
                       start=True, stop=True).then_inc(z_ready[n], 1)

            def spread_distances(i):
                pe.wait_ge(dist_in, (i + 1) * 16)
                pe.wait_ge(soft_ready[1], i * 4)
                for q in range(4):
                    mm(bank(q), ones_bf[:], dist_row[:, q * 512:(q + 1) * 512], start=True, stop=True)\
                        .then_inc(dist_bc, 1)

            def turn_messages(i):
                for q in range(4):
                    h = q // 2
                    pe.wait_ge(msg_ready[h], i * 2 + q % 2 + 1)
                    pe.wait_ge(added[h], i * HT + 1 * (ITERS * HT))
                    for j in range(4 * q, 4 * q + 4):
                        o = 2048 + j * D
                        last = tr(PS[:, o:o + D], msg0[:, j * D:(j + 1) * D], ident[:])
                    last.then_inc(msg_turned, 1)

            def spread_cutoffs(i, pick, after, done):
                pe.wait_ge(cut_in_row, (i + 1) * 16)
                for q in range(4):
                    pe.wait_ge(after, i * 4 + q + 1)
                    mm(bank(4 + q), pick[:], cut_row[:, q * 512:(q + 1) * 512], start=True, stop=True).then_inc(done, 1)

            def turn_scans(i):
                for q in range(4):
                    pe.wait_ge(scanned, i * 4 + q + 1)
                    for j in range(4 * q, 4 * q + 4):
                        o = 2048 + j * D
                        last = tr(PS[:, o:o + D], prod[:, j * D:(j + 1) * D], ident[:])
                    last.then_inc(scan_turned, 1)

            def last_windows(i):
                for q in range(4):
                    pe.wait_ge(scan_copied, i * 4 + q + 1)
                    if q % 2 == 0:
                        pe.wait_ge(onehot_ready[q // 2], i + 1 + 1 * ITERS)
                    for j in range(4 * q, 4 * q + 4):
                        o = 2048 + j * D
                        last = mm(PS[:, o:o + D], msg0[:, j * D:(j + 1) * D], onehot[:, j, :], start=True, stop=True)
                    last.then_inc(win_ready, 1)

            n_carry = 0

            def carries(n):
                nonlocal n_carry
                for _ in range(n):
                    n_carry += 1
                    pe.wait_ge(carry_in_ready, n_carry)
                    tr(PS[0:1, 3072:3072 + P], carry_cols[:, 0:1], ident[:])
                    tr(PS[0:1, 3072 + P:3072 + 2 * P], carry_cols[:, 1:2], ident[:]).then_inc(carry_rows, 1)
                    pe.wait_ge(carry_scanned, n_carry)
                    tr(PS[:, 3584:3585], carry_row[0:1, 3 * P:4 * P], ident[0:1, 0:1]).then_inc(carry_cols_out, 1)

            def attention(l):
                def spread(i, h):
                    pe.wait_ge(lo_in[h], (i + 1 + l * ITERS) * 16)
                    pe.wait_ge(lo_hot[h], i + l * ITERS)
                    for q in (2 * h, 2 * h + 1):
                        last = mm(bank(q), ones_bf[0:1, :], lo_row[:, q * 512:(q + 1) * 512], start=True, stop=True)
                    last.then_inc(lo_bc[h], 1)

                def candidates(i, h):
                    pe.wait_ge(lo_hot[h], i + 1 + l * ITERS)
                    pe.wait_ge(al_pick[h], i + l * ITERS)
                    for j in range(HT):
                        o = (4 + h) * 512 + j * NT
                        for part in range(3):
                            last = mm(PS[:, o:o + NT], hot_bf[:, h, j, :], als_bf[:, part * NT:(part + 1) * NT],
                                      start=(part == 0), stop=(part == 2))
                    last.then_inc(al_rows[h], 1)

                pe.wait_ge(first_in, l + 1)
                for h in range(2):
                    spread(0, h)
                with pe.Fori(0, ITERS - 1) as i:
                    for h in range(2):
                        candidates(i, h)
                        spread(i + 1, h)
                for h in range(2):
                    candidates(ITERS - 1, h)
                    pe.wait_ge(al_done[h], ITERS + l * ITERS)
                for b in range(NB):
                    last = tr(PS[0:TB, 3072 + b * P:3072 + (b + 1) * P], als_t[:, b * TB:(b + 1) * TB], ident[:])
                last.then_inc(turn_out, 1)
                pe.wait_ge(turn_blk, l + 1)
                carries(5)
                pe.wait_ge(ex_loaded, 16 * (l + 1))
                for b in range(NB):
                    o = 2048 + (b // 4) * 512 + (b % 4) * TB
                    last = tr(PS[:, o:o + TB], turned[:, b * P:(b + 1) * P], ident[0:TB, 0:TB])
                last.then_inc(ex_turned, 1)

            def statistics(l):
                for n in range(2):
                    pe.wait_ge(sum_in, 2 * l + n + 1)
                    mm(PS[:, 0:D], ones[:], acc[:, 2 * n * D:(2 * n + 1) * D], start=True, stop=True).then_inc(sum_out, 1)

            for k in range(K):
                if k != 1:
                    rows_product(k)
                if k == 1:
                    spread_distances(0)
                    filter_step(0, 0)
                    filter_step(0, 1)
                    with pe.Fori(0, ITERS - 1) as i:
                        spread_distances(i + 1)
                        turn_messages(i)
                        filter_step(i + 1, 0)
                        spread_cutoffs(i, pick_keep, msgf_ready, keep_bc)
                        filter_step(i + 1, 1)
                        spread_cutoffs(i, pick_start, keep_ready, start_bc)
                        turn_scans(i)
                        last_windows(i)
                    turn_messages(ITERS - 1)
                    spread_cutoffs(ITERS - 1, pick_keep, msgf_ready, keep_bc)
                    spread_cutoffs(ITERS - 1, pick_start, keep_ready, start_bc)
                    turn_scans(ITERS - 1)
                    last_windows(ITERS - 1)
                else:
                    if k in GAT:
                        attention(k - 5)
                    edge_pass(k)
                if k == 0:
                    for h in range(2):
                        pe.wait_ge(meta_added[h], ITERS * HT)
                    for t in range(NT):
                        last = tr(PS[:, 2560 + 3 * t:2563 + 3 * t], macc[:, t * P:(t + 1) * P], ident[0:3, 0:3])
                    last.then_inc(info_turned, 1)
                segment_product(k)
                if k in GAT:
                    statistics(k - 5)

        @block.vector
        def _(v):
            tt, ts, stt = nc.vector.tensor_tensor, nc.vector.tensor_scalar, nc.vector.scalar_tensor_tensor
            copy, memset, reduce = nc.vector.tensor_copy, nc.vector.memset, nc.vector.tensor_reduce
            scan, recip = nc.vector.tensor_tensor_scan, nc.vector.reciprocal
            step = stepper(v, dve)

            step(memset(dst_i, N))
            step(memset(src_i, 0))
            step(memset(ew, R_MAX))
            step(memset(edge_cols[:], -1))
            step(memset(X3[:, NT - 1, :], 0.0))
            memset(attr_pre, 0.0).then_inc(pads_set, 1)
            step(memset(acc[:, 0:2 * ET], 0.0))
            step(memset(col(HALF_PI), float(np.pi / 2)))
            step(memset(col(EPSC), EPS))
            step(memset(ones_bf[:], 1.0))
            step(memset(ones_s, 1.0))
            step(memset(col(THIRTY), 30.0))
            step(memset(pick_start[:], 1.0))
            step(memset(pick_start[0:3, :], 0.0))
            step(memset(pick_keep[:], 0.0))
            step(memset(pick_keep[0:3, :], 1.0))
            step(memset(info3[:, :, 0:1], 0.0))
            step(memset(info3[:, :, 1:3], BIGPOS))
            memset(info3[:, :, 3:4], 0.0).then_inc(zeros_ready, 1)
            v.wait_ge(consts, CONSTS)
            step(copy(iota_row[:], iota_int[:]))
            step(copy(iota_col[:], iota_coli[:]))
            step(ts(col(NEGC), iota_col[:], -DELTA, None, ALU.mult))
            v.wait_ge(loads, 16 * LOADS)
            step(copy(dst_f, dst_i))
            step(copy(src_f, src_i))
            step(copy(col(EDGE, 2), edge_cols[:]))
            step(tt(first_s[:, 1:ET], dst_f[:, 1:ET], dst_f[:, 0:ET - 1], ALU.not_equal))
            step(tt(first_s[:, 0:1], dst_f[:, 0:1], col(EDGE), ALU.not_equal))
            step(copy(last_s[:, 0:ET - 1], first_s[:, 1:ET]))
            step(tt(last_s[:, ET - 1:ET], dst_f[:, ET - 1:ET], col(EDGE + 1), ALU.not_equal))
            step(ts(same_s[:], first_s, -1.0, 1.0, ALU.mult, ALU.add))
            step(reduce(col(ALLSAME), same_s[:], AX.X, ALU.min))
            step(ts(col(PENALL), col(ALLSAME), -1.0, HUGE, ALU.add, ALU.mult))
            step(reduce(col(NOLAST), last_s[:], AX.X, ALU.max))
            step(ts(col(NOLAST), col(NOLAST), -1.0, 1.0, ALU.mult, ALU.add))
            step(scan(seg_s, ones_s, first_s, 0.0, ALU.mult, ALU.add))
            step(copy(col(TOTAL), seg_s[:, ET - 1:ET]))
            reduce(col(ASUM, 3), attr_pre.rearrange("p (j c) -> p c j", c=3), AX.X, ALU.add).then_inc(pre_in, 1)
            step(ts(w0, ew, 0.1, MAGIC, ALU.mult, ALU.add))
            step(ts(w0, w0, -MAGIC, None, ALU.add))
            stt(w0, ew, 0.1, w0, ALU.mult, ALU.subtract).then_inc(cut_in, 1)
            def in_parts(parts, x):
                step(copy(parts[0], x))
                step(tt(x, x, parts[0], ALU.subtract))
                step(copy(parts[1], x))
                step(tt(x, x, parts[1], ALU.subtract))
                step(copy(parts[2], x))

            step(ts(w2.bitcast(I32), src_i, P - 1, None, ALU.bitwise_and))
            step(copy(bf[:, 9, :], w2.bitcast(I32)))
            v.wait_ge(cut_out, 1)
            step(ts(cut_s, w1, 0.5, 0.5, ALU.mult, ALU.add))
            step(ts(w2, ew, R_MAX, None, ALU.is_lt))
            step(tt(cut_s, cut_s, w2, ALU.mult))
            step(tt(w2, cut_s, same_s[:], ALU.mult))
            step(tt(cut_s, cut_s, first_s, ALU.mult))
            in_parts([bf[:, q, :] for q in (0, 1, 2)], ew)
            in_parts([bf[:, q, :] for q in (3, 4, 5)], w2)
            in_parts([bf[:, q, :] for q in (6, 7, 8)], cut_s)
            for l in range(3):
                step(tt(wprod[:, 3 * l * D:3 * (l + 1) * D].rearrange("p (c f) -> p c f", c=3),
                        we_bc[:, 3 * l * D:3 * (l + 1) * D].rearrange("p (c f) -> p c f", c=3),
                        ae_bc[:, l * D:(l + 1) * D].unsqueeze(1).broadcast_to([P, 3, D]), ALU.mult))
            step(reduce(col(VV, 9), wprod.rearrange("p (c f) -> p c f", f=D), AX.X, ALU.add))
            v.wait_ge(pre_out, 1)
            step(ts(col(AMN, 3), PS[:, 1536:1539], 1.0 / E, None, ALU.mult))
            for l in range(3):
                step(tt(col(EDGE + 2, 3), col(AMN, 3), col(VV + 3 * l, 3), ALU.mult))
                step(reduce(col(AMEAN + l), col(EDGE + 2, 3), AX.X, ALU.add))
            step(copy(mats[:, M["ws"] * D:(M["wn"] + 1) * D], PS[:, 0:2 * D]))
            step(stt(bias_cols[:, 1:2], PS[:, 512:513], -LN2, bias_cols[:, 1:2], ALU.mult, ALU.add))
            step(ts(bias_cols[:, 2:4], bias_cols[:, 0:2], -1.0, 30.0, ALU.mult, ALU.add))
            step(copy(col(TOTAL), PS[:, 1024:1025]))
            step(ts(seg_s, seg_s, col(TOTAL), None, ALU.add), flats_ready)
            v.wait_ge(blocks_loaded, 64)
            step(copy(small[0:TB, 0:NB], blocks[:, 0, :, 0]))
            copy(seg0_blk[0:TB, :], small[0:TB, 0:NB]).then_inc(seg0_ready, 1)
            tt(blocks[:, 0, :, :], blocks[:, 0, :, :], small[0:TB, 0:NB].unsqueeze(2).broadcast_to([TB, NB, P]),
               ALU.subtract).then_inc(loc_ready, 1)
            for q, dst in enumerate((loc_t[:], dst_t, last_t, srcf_t)):
                base = 2048 + (q % 2) * 1024
                v.wait_ge(tiles_turned, q + 1)
                step(copy(dst[:, 0:4 * TB], PS[:, base:base + 4 * TB]))
                step(copy(dst[:, 4 * TB:ET], PS[:, base + 512:base + 512 + 3 * TB]), tiles_copied)
            step(stt(loclast_t[:], loc_t[:], 1.0, last_t, ALU.add, ALU.mult))
            step(ts(loclast_t[:], loclast_t[:], -1.0, None, ALU.add))
            step(copy(src_t[:], srcf_t))
            step(ts(srcf_t.bitcast(I32), src_t[:], 7, None, ALU.arith_shift_right))
            step(copy(srchi_t[:], srcf_t.bitcast(I32)))
            meta3 = meta_t.rearrange("p (e c) -> p e c", c=3)
            step(tt(meta3[:, :, 0], dst_t, last_t, ALU.mult))
            step(copy(srcf_t, pos_i))
            step(tt(meta3[:, :, 1], srcf_t, last_t, ALU.mult))
            step(memset(meta3[:, :, 2:3], 1.0), tiles_ready)

            def layer_input(k):
                step(reduce(stat0, X3, AX.X, ALU.add))
                step(ts(stat0, stat0, -1.0 / D, None, ALU.mult))
                step(tt(H3, X3, stat0.unsqueeze(2).broadcast_to([P, NT, D]), ALU.add))
                sq = acc[:, 0:NT * D]
                step(tt(sq, H[:, 0:NT * D], H[:, 0:NT * D], ALU.mult))
                reduce(stat1, sq.rearrange("p (t f) -> p t f", f=D), AX.X, ALU.add).then_inc(var_ready, 1)
                v.wait_ge(std_ready, vars_done(1))
                step(recip(stat1, stat1))
                step(stt(H3, H3, 0.0, stat1.unsqueeze(2).broadcast_to([P, NT, D]), ALU.max, ALU.mult), h_ready)

            n_vars = 0

            def vars_done(n):
                nonlocal n_vars
                n_vars += n
                return n_vars

            def rows_product(k):
                with v.Fori(0, NCH) as i:
                    v.wait_ge(p_turned, i + 1 + turn[k] * NCH)
                    copy(stage_mid, PS[:, 0:CW]).then_inc(p_copied, 1)
                    v.wait_ge(p_product, i + 1 + turn[k] * NCH)
                    hold(v)
                    copy(T[:, ds(i * CW, CW)], PS[:, 1024:1024 + CW]).then_inc(p_done, 1)
                v.wait_ge(p_done, NCH + turn[k] * NCH)

            def zero_acc(k):
                step(memset(acc[:], 0.0))
                if k == 1:
                    step(memset(acc[:, 0:1], 1.0))

            def make_onehot(k, i, h, loc):
                half = onehot[:, h * HT:(h + 1) * HT, :]
                if k in GAT:
                    hold(v)
                    for j in range(HT):
                        e = i * BT + (h * HT + j)
                        last = ts(onehot[:, h * HT + j, :], iota_row[:], loc[:, ds(e, 1)], ex_t[:, ds(e, 1)],
                                  ALU.is_equal, ALU.mult)
                else:
                    last = tt(half, iota_row[:].unsqueeze(1).broadcast_to([P, HT, D]),
                              loc[:, ds(i * BT + h * HT, HT)].unsqueeze(2).broadcast_to([P, HT, D]), ALU.is_equal)
                last.then_inc(onehot_ready[h], 1)

            def add_windows(i, h, sums, after, first, between=()):
                between = list(between)
                for j in range(HT):
                    for windows, dst, done, before_pass in sums:
                        at = dst[:, ds(first[j], D)]
                        if j in after:
                            v.wait_ge(*after[j])
                        if j == 0:
                            v.wait_ge(done[1 - h], (i + h) * HT + before_pass)
                        else:
                            v.wait_ge(done[h], i * HT + j + before_pass)
                        tt(at, at, windows[:, j * D:(j + 1) * D], ALU.add).then_inc(done[h], 1)
                    if j < len(between):
                        between[j]()

            seg_regs = [v.alloc_register(f"segment{j}") for j in range(HT)]

            def tile_segments(i, h):
                v.load(seg_regs, seg0_row[0:1, ds(i * BT + h * HT, HT)])
                return [v.snap(r, min_val=0, max_val=ACCW - D) for r in seg_regs]

            def edge_pass(k):
                def half(i, h):
                    first = tile_segments(i, h)
                    ready = {0: (multiplied[h], i + 1 + turn[k] * ITERS)}
                    sums = [(PS[:, h * 1024:(h + 1) * 1024], acc, added, k * ITERS * HT)]
                    if k == 0:
                        sums.append((PS[0:3, 2048 + h * 1024:2048 + (h + 1) * 1024], macc, meta_added, 0))
                    add_windows(i, h, sums, ready, first)

                for h in range(2):
                    make_onehot(k, 0, h, loc_t)
                with v.Fori(0, ITERS - 1) as i:
                    for h in range(2):
                        half(i, h)
                        v.wait_ge(multiplied[h], i + 1 + turn[k] * ITERS)
                        make_onehot(k, i + 1, h, loc_t)
                for h in range(2):
                    half(ITERS - 1, h)

            def messages(i, attrs):
                v.wait_ge(attr_in, attrs)
                for h in range(2):
                    v.wait_ge(gathered[h], (i + 1) * (16 * HT) + 1 * (ITERS * 16 * HT))
                    for q in (2 * h, 2 * h + 1):
                        w = slice(q * 512, (q + 1) * 512)
                        tt(msg0[:, w], attr[:, w], rows[:, 4 * q:4 * q + 4, :].rearrange("p a b -> p (a b)"), ALU.mult)\
                            .then_inc(msg_ready[h], 1)

            def softplus(i, n, quarters=range(4)):
                for q in quarters:
                    w = slice(q * 512, (q + 1) * 512)
                    v.wait_ge(ln_done[n], i * 4 + q + 1)
                    stt(filt[:, w] if n else rbf[:, w], bank(q), bias_cols[:, n:n + 1], lnp[:, w], ALU.add, ALU.max)\
                        .then_inc(soft_ready[n], 1)

            def feature_messages(i):
                for q in range(4):
                    w = slice(q * 512, (q + 1) * 512)
                    v.wait_ge(msg_turned, i * 4 + q + 1)
                    v.wait_ge(soft_ready[1], (i + 1) * 4)
                    v.wait_ge(scanned, i * 4)
                    stt(msgf[:, w], filt[:, w], -LN2, bank(4 + q), ALU.add, ALU.mult).then_inc(msgf_ready, 1)

            def scans(i):
                for q in range(4):
                    w = slice(q * 512, (q + 1) * 512)
                    v.wait_ge(keep_bc, i * 4 + q + 1)
                    tt(keep[:, w], msgf[:, w], bank(4 + q), ALU.mult).then_inc(keep_ready, 1)
                for q in range(4):
                    w = slice(q * 512, (q + 1) * 512)
                    v.wait_ge(start_bc, i * 4 + q + 1)
                    tt(msgf[:, w], msgf[:, w], bank(4 + q), ALU.mult).then_inc(start_ready, 1)
                v.wait_ge(scan_turned, i * 4)
                for q in range(4):
                    w = slice(q * 512, (q + 1) * 512)
                    v.wait_ge(start_ready, i * 4 + q + 1)
                    v.wait_ge(scanned, i * 4 + q)
                    hold(v)
                    e = (q * 512 - 1) % BE
                    scan(prod[:, w], keep[:, w], msgf[:, w], prod[:, e:e + 1], ALU.mult, ALU.add).then_inc(scanned, 1)

            def product_windows(i, between):
                for h in range(2):
                    first = tile_segments(i, h)
                    ready = {4 * (q % 2): (win_ready, i * 4 + q + 1) for q in (2 * h, 2 * h + 1)}
                    add_windows(i, h, [(PS[:, 2048 + h * 1024:2048 + (h + 1) * 1024], acc, added, ITERS * HT)],
                                ready, first, between[h])

            def product_pass():
                step(memset(prod, 0.0))
                softplus(0, 0)
                softplus(0, 1)
                for h in range(2):
                    make_onehot(1, 0, h, loclast_t)
                nothing = [lambda: None] * 4
                with v.Fori(0, ITERS - 1) as i:
                    messages(i, (i + 1) * 64)
                    feature_messages(i)
                    softplus(i + 1, 0)
                    scans(i)
                    product_windows(i, [[lambda q=q: softplus(i + 1, 1, (q,)) for q in range(4)],
                                        nothing + nothing[0:1] + [lambda h=h: make_onehot(1, i + 1, h, loclast_t)
                                                                  for h in range(2)]])
                i = ITERS - 1
                messages(i, i * 64 + 32)
                feature_messages(i)
                scans(i)
                product_windows(i, [[], []])

            def segments_out(k):
                with v.Fori(0, NCH) as i:
                    v.wait_ge(c_product, i + 1 + k * NCH)
                    v.wait_ge(c_stored, i * 16 + k * (NCH * 16))
                    copy(stage_out, PS[:, 1024:1024 + CW]).then_inc(c_copied, 1)

            def segment_facts():
                v.wait_ge(info_turned, 1)
                facts = PS[:, 2560:2560 + 3 * NT].rearrange("p (t c) -> p t c", c=3)
                step(copy(info3[:, :, 2:4], facts[:, :, 1:3]))
                step(copy(info3[:, :, 0], ids_int[:]))
                step(stt(info3[:, :, 1], info3[:, :, 2], 1.0, info3[:, :, 3], ALU.add, ALU.subtract))
                step(ts(stat0, info3[:, :, 3], 0.0, BIGPOS, ALU.is_equal, ALU.mult))
                step(tt(stat0, stat0, facts[:, :, 0], ALU.add))
                step(copy(cmap[:], stat0), info_ready)

            def node_facts():
                v.wait_ge(info_loaded, 16)
                step(copy(firstpos[:], info3[:, :, 1]))
                step(copy(lastpos[:], info3[:, :, 2]))
                step(ts(rcount[:], info3[:, :, 3], 1.0, None, ALU.max))
                step(recip(rcount[:], rcount[:]))
                step(copy(cmap[:], info3[:, :, 0]), info_cols)

            def chunk(buf3, c):
                return buf3[:, c * CH:(c + 1) * CH, :]

            def mean_layer(k):
                for c in range(NCH):
                    g = chunk(G3, c)
                    v.wait_ge(node_rows[c], (k + 1) * CH * 16)
                    step(tt(g, g, rcount[:, c * CH:(c + 1) * CH].unsqueeze(2).broadcast_to([P, CH, D]), ALU.mult))
                    step(tt(g, g, chunk(T3, c), ALU.add))
                    step(tt(g, g, vec_nodes(bias_vec[k], CH), ALU.add))
                    x = chunk(X3, c)
                    if k == 0:
                        step(stt(x, g, 0.0, x, ALU.max, ALU.add))
                    elif k == 4:
                        step(tt(x, g, x, ALU.add))
                    else:
                        step(ts(chunk(H3, c), g, 0.0, None, ALU.max), h_ready if c == NCH - 1 else dve)

            def product_layer():
                for c in range(NCH):
                    v.wait_ge(node_rows[c], 2 * CH * 16)
                step(tt(G3, G3, vec_nodes(bias_vec[1]), ALU.add))
                ts(T[:], G[:], 30.0, None, ALU.min).then_inc(ln_in, 1)
                v.wait_ge(ln_out, 1)
                step(tt(G[:], G[:], T[:], ALU.max))
                step(stt(X[:], G[:], -LN2, X[:], ALU.add, ALU.add))

            n_carry = 0

            def linked_scan(dst, d0, d1, ops, whole, start, backward=False):
                nonlocal n_carry
                n_carry += 1
                r = (lambda x: x[:, ::-1]) if backward else (lambda x: x)
                end = dst[:, 0:1] if backward else dst[:, ET - 1:ET]
                step(scan(r(dst), r(d0), r(d1), start, *ops))
                step(copy(carry_cols[:, 0:1], end))
                copy(carry_cols[:, 1:2], whole).then_inc(carry_in_ready, 1)
                v.wait_ge(carry_rows, n_carry)
                step(copy(carry_row[:, 0:2 * P], PS[0:1, 3072:3072 + 2 * P]))
                f, w, o, z = (carry_row[:, i * P:(i + 1) * P] for i in range(4))
                step(scan(r(o), r(w), r(f), start, *ops))
                step(memset(z[:, P - 1:P] if backward else z[:, 0:1], start))
                if backward:
                    step(copy(z[:, 0:P - 1], o[:, 1:P]), carry_scanned)
                else:
                    step(copy(z[:, 1:P], o[:, 0:P - 1]), carry_scanned)
                v.wait_ge(carry_cols_out, n_carry)
                step(copy(carry_in[:], PS[:, 3584:3585]))
                return r(dst), r(d0), r(d1), carry_in[:], *ops

            def attention(k):
                l = k - 5
                step(memset(attr_att, 0.0), attr_space)
                for dst, w in ((als_n, f"L3_gnn_as{l + 1}"), (ald_n, f"L3_gnn_ad{l + 1}")):
                    step(tt(G3, T3, vec_nodes(V[w]), ALU.mult))
                    step(reduce(dst, G3, AX.X, ALU.add))
                step(tt(self_n, als_n, ald_n, ALU.add))
                step(ts(self_n, self_n, col(AMEAN + l), None, ALU.add))
                step(stt(self_n, self_n, 0.2, self_n, ALU.mult, ALU.max))
                step(copy(stat0, als_n))
                in_parts([als_bf[:, q * NT:(q + 1) * NT] for q in range(3)], stat0)
                step(copy(nd3[:, :, 0], ald_n))
                step(copy(nd3[:, :, 1], self_n), first_in)
                def make_lo(i, h):
                    v.wait_ge(lo_bc[h], i + 1 + l * ITERS)
                    v.wait_ge(al_rows[h], i + l * ITERS)
                    hold(v)
                    ts(hot_bf[:, h, :, :].rearrange("p a b -> p (a b)"), PS[:, h * 1024:(h + 1) * 1024], iota_col[:],
                       None, ALU.is_equal).then_inc(lo_hot[h], 1)

                def pick(i, h):
                    at = l * ITERS + i
                    mask = Hs[h][:, 0:HT * NT].rearrange("p (t c) -> p t c", c=NT)
                    cand = PS[:, (4 + h) * 512:(4 + h) * 512 + HT * NT].rearrange("p (t c) -> p t c", c=NT)
                    v.wait_ge(al_done[h], at)
                    tt(mask, iota_row[:, 0:NT].unsqueeze(1).broadcast_to([P, HT, NT]),
                       srchi_t[:, ds(i * BT + h * HT, HT)].unsqueeze(2).broadcast_to([P, HT, NT]), ALU.is_equal)\
                        .then_inc(al_mask[h], 1)
                    v.wait_ge(al_mask[h], at + 1)
                    v.wait_ge(al_rows[h], at + 1)
                    hold(v)
                    tt(mask, mask, cand, ALU.mult).then_inc(al_pick[h], 1)
                    v.wait_ge(al_pick[h], at + 1)
                    hold(v)
                    reduce(als_t[:, ds(i * BT + h * HT, HT)], mask, AX.X, ALU.add).then_inc(al_done[h], 1)

                make_lo(0, 0)
                with v.Fori(0, ITERS - 1) as i:
                    make_lo(i, 1)
                    pick(i, 0)
                    make_lo(i + 1, 0)
                    pick(i, 1)
                make_lo(ITERS - 1, 1)
                pick(ITERS - 1, 0)
                pick(ITERS - 1, 1)
                v.wait_ge(turn_out, l + 1)
                step(copy(turned, PS[0:TB, 3072:3072 + NB * P]), turn_blk)
                v.wait_ge(attr_again, 32 * (l + 1))
                step(ts(Gs[5], attr3[:, :, 0], col(VV + 3 * l), None, ALU.mult))
                for c in (1, 2):
                    step(stt(Gs[5], attr3[:, :, c], col(VV + 3 * l + c), Gs[5], ALU.mult, ALU.add))
                v.wait_ge(first_ld, 16 * (l + 1))
                add, spread = (ALU.add, ALU.max), (ALU.mult, ALU.add)
                step(scan(*linked_scan(Gs[3], same_s[:], at_f[:, :, 0], spread, col(ALLSAME), 0.0)))
                step(scan(*linked_scan(Gs[4], same_s[:], at_f[:, :, 1], spread, col(ALLSAME), 0.0)))
                v.wait_ge(al_loaded, 16 * (l + 1))
                step(tt(Gs[0], Gs[0], Gs[3], ALU.add))
                step(tt(Gs[0], Gs[0], Gs[5], ALU.add))
                step(stt(Gs[0], Gs[0], 0.2, Gs[0], ALU.mult, ALU.max))
                step(ts(Gs[5], same_s[:], -1.0, HUGE, ALU.add, ALU.mult))
                step(scan(*linked_scan(Gs[6], Gs[5], Gs[0], add, col(PENALL), -HUGE)))
                step(tt(Gs[6], Gs[6], last_s[:], ALU.mult))
                step(ts(Gs[5], last_s[:], -1.0, 1.0, ALU.mult, ALU.add))
                step(scan(*linked_scan(Gs[7], Gs[5], Gs[6], spread, col(NOLAST), 0.0, backward=True)))
                step(tt(at_l[:, :, 1], Gs[7], Gs[4], ALU.max))
                step(tt(Gs[5], Gs[0], at_l[:, :, 1], ALU.subtract), exp_in)
                v.wait_ge(exp_out, l + 1)
                step(scan(*linked_scan(at_l[:, :, 0], same_s[:], Gs[6], spread, col(ALLSAME), 0.0)), last_in)
                v.wait_ge(ex_turned, l + 1)
                step(copy(ex_t[:, 0:4 * TB], PS[:, 2048:2048 + 4 * TB]))
                step(copy(ex_t[:, 4 * TB:ET], PS[:, 2560:2560 + 3 * TB]))
                step(memset(nd3[:, :, 0:1], 0.0))
                step(memset(nd3[:, :, 1:2], -HUGE), last_fill)

            def attention_layer(k):
                l = k - 5
                v.wait_ge(last_ga, 16 * NT * (l + 1))
                step(tt(amax_n, nd3[:, :, 1], self_n, ALU.max))
                step(tt(exs_n, self_n, amax_n, ALU.subtract), self_in)
                v.wait_ge(self_out, l + 1)
                step(tt(rden_n, nd3[:, :, 0], exs_n, ALU.add))
                step(ts(rden_n, rden_n, 1e-16, None, ALU.add))
                step(recip(rden_n, rden_n))
                step(tt(T3, T3, exs_n.unsqueeze(2).broadcast_to([P, NT, D]), ALU.mult))
                for c in range(NCH):
                    g = chunk(G3, c)
                    v.wait_ge(node_rows[c], (k + 1) * CH * 16)
                    step(tt(g, g, chunk(T3, c), ALU.add))
                    step(tt(g, g, rden_n[:, c * CH:(c + 1) * CH].unsqueeze(2).broadcast_to([P, CH, D]), ALU.mult))
                    step(tt(g, g, vec_nodes(bias_vec[k], CH), ALU.add))
                    step(stt(chunk(H3, c), g, 0.01, g, ALU.mult, ALU.max))
                s0, nm, s1, sd = (acc[:, i * D:(i + 1) * D] for i in range(4))
                lastt = H3[:, NT - 1, :]
                step(ts(lastt, lastt, rowmask[:], None, ALU.mult))
                step(reduce(s0, H3.rearrange("p t f -> p f t"), AX.X, ALU.add), sum_in)
                v.wait_ge(sum_out, 2 * l + 1)
                step(ts(nm, PS[:, 0:D], -1.0 / N, None, ALU.mult))
                step(tt(H3, H3, nm.unsqueeze(1).broadcast_to([P, NT, D]), ALU.add))
                step(ts(lastt, lastt, rowmask[:], None, ALU.mult))
                step(tt(G[:], H[:, 0:NT * D], H[:, 0:NT * D], ALU.mult))
                step(reduce(s1, G3.rearrange("p t f -> p f t"), AX.X, ALU.add), sum_in)
                v.wait_ge(sum_out, 2 * l + 2)
                step(copy(s1, PS[:, 0:D]), var_ready)
                v.wait_ge(std_ready, vars_done(1))
                step(recip(sd, sd))
                step(tt(sd, sd, vec(V[f"L3_gnn_g{l + 1}"]), ALU.mult))
                step(tt(H3, H3, sd.unsqueeze(1).broadcast_to([P, NT, D]), ALU.mult))
                if k < K - 1:
                    step(tt(H3, H3, vec_nodes(V[f"L3_gnn_be{l + 1}"]), ALU.add), h_ready)
                else:
                    step(tt(H3, H3, vec_nodes(V[f"L3_gnn_be{l + 1}"]), ALU.add))
                    step(tt(X[:], X[:], H[:, 0:NT * D], ALU.add), out_ready)

            v.wait_ge(seg0_loaded, 16)
            for k in range(K):
                if k in (0, 1, 2, 5):
                    layer_input(k)
                if k != 1:
                    rows_product(k)
                if k in GAT:
                    attention(k)
                zero_acc(k)
                v.wait_ge(table_stored, 16 + k * 16)
                if k == 0:
                    step(memset(macc, 0.0))
                if k == 1:
                    product_pass()
                else:
                    edge_pass(k)
                if k == 0:
                    segment_facts()
                segments_out(k)
                if k == 0:
                    node_facts()
                if k == 1:
                    product_layer()
                elif k in SAGE:
                    mean_layer(k)
                else:
                    attention_layer(k)


CONSTS = 9
LOADS = 12 + 20 + 11 + 9 + 2
_NAMES = ["x", "src", "dst", "edge_attr_128", "edge_attr_3", "edge_weight", "L0_gnn_W_self", "L0_gnn_W_neigh",
          "L0_gnn_bias", "L1_gnn_W1", "L1_gnn_b1", "L1_gnn_W2", "L1_gnn_b2", "L1_gnn_W3", "L1_gnn_b3",
          "L2_gnn_W_agg", "L2_gnn_W_root", "L2_gnn_b"]
_NAMES += [f"L3_gnn_{n}{l}" for l in (1, 2, 3) for n in ("W", "as", "ad", "We", "ae", "b", "g", "be")]


def kernel(**inputs):
    import concourse.bacc as _bacc
    from concourse.bass_utils import run_bass_kernel_spmd as _run

    nc = _bacc.Bacc("TRN2", target_bir_lowering=False, num_devices=1)
    arrays, aps = {}, {}
    for name in _NAMES:
        x = np.ascontiguousarray(inputs[name])
        arrays[f"in_{name}"] = x
        aps[name] = nc.dram_tensor(f"in_{name}", x.shape, mybir.dt.from_np(x.dtype), kind="ExternalInput").ap()
    out = nc.dram_tensor("out_x", (N, D), F32, kind="ExternalOutput").ap()
    build(nc, aps, out)
    r = _run(nc, [arrays], core_ids=[0])
    return r.results[0]["out_x"]
```

```python
from contextlib import ExitStack

import numpy as np
import concourse.bass as bass
from concourse import mybir

ALU = mybir.AluOpType
ACT = mybir.ActivationFunctionType
F32 = mybir.dt.float32
I32 = mybir.dt.int32
BF16 = mybir.dt.bfloat16
AX = mybir.AxisListType

P = 128
N, E, D = 6250, 100000, 128
NT = -(-N // P)
NPAD = NT * P
NLAST = N - (NT - 1) * P
CH = 7
NCH = NT // CH
CW = CH * D
ET = 784
EPAD = ET * P
HT = 8
BT = 2 * HT
ITERS = ET // BT
BE = BT * P
HE = HT * P
BODY_HALVES = 2 * ITERS
TB = 112
NB = ET // TB
ACCW = 6400
SROWS = E - (P - 1) * ET
BIGPOS = float(1 << 20)
HUGE = 1.0e30
LN2 = 0.6931471805599453
R_MAX = 5.0
DELTA = R_MAX / (D - 1)
COEFF = -0.5 / (DELTA * DELTA)
EPS = 1e-5
MAGIC = 12582912.0
K = 8
SAGE = (0, 2, 3, 4)
GAT = (5, 6, 7)


def build(nc, a, out):
    ds = bass.ds
    with ExitStack() as ctx:
        def sb(name, shape, dt=F32):
            return ctx.enter_context(nc.sbuf_tensor(name, shape, dt))

        def sem(name):
            return ctx.enter_context(nc.semaphore(name))

        def sems(name, n):
            return [sem(f"{name}{i}") for i in range(n)]

        def dram(name, shape, dt=F32):
            return nc.dram_tensor(name, shape, dt, kind="Internal").ap()

        table = [dram("table0", (NPAD, D)), dram("table1", (NPAD, D))]
        seg_rows = dram("seg_rows", (NPAD, D))
        flats = dram("flats", (4, EPAD))
        flat_bf = dram("flat_bf", (10, EPAD), BF16)
        prod_rows = dram("prod_rows", (EPAD, D))
        first_of_tile = dram("first_of_tile", (ET,), I32)
        node_table = dram("node_table", (NPAD, 4))
        at_first = dram("at_first", (EPAD, 2))
        at_last = dram("at_last", (EPAD, 2))
        al_flat = dram("al_flat", (EPAD,))
        ex_flat = dram("ex_flat", (EPAD,))

        X = sb("X", [P, NT * D])
        H = sb("H", [P, ACCW])
        G = sb("G", [P, NT * D])
        T = sb("T", [P, NT * D])
        acc = sb("acc", [P, ACCW])
        rows = sb("rows", [P, BT, D])
        onehot = sb("onehot", [P, BT, D])
        idx_buf = sb("idx_buf", [P, BT], I32)
        meta_buf = sb("meta_buf", [P, BT * 3])
        iota_coli = sb("iota_coli", [P, 1], I32)
        src_t = sb("src_t", [P, ET], I32)
        srchi_t = sb("srchi_t", [P, ET])
        loc_t = sb("loc_t", [P, ET])
        als_bf = sb("als_bf", [P, 3 * NT], BF16)
        ex_t = sb("ex_t", [P, ET])
        als_t = sb("als_t", [P, ET])
        same_s = sb("same_s", [P, ET])
        last_s = sb("last_s", [P, ET])
        seg0_row = sb("seg0_row", [1, ET], I32)
        vecs = sb("vecs", [P, 20 * D])
        mats = sb("mats", [P, 14 * D])
        iota_row = sb("iota_row", [P, D])
        iota_col = sb("iota_col", [P, 1])
        iota_int = sb("iota_int", [P, D], I32)
        ident = sb("ident", [P, P])
        before = sb("before", [P, P])
        ones = sb("ones", [P, P])
        ones_bf = sb("ones_bf", [3, P], BF16)
        pick_keep = sb("pick_keep", [6, P], BF16)
        pick_start = sb("pick_start", [6, P], BF16)
        rowmask = sb("rowmask", [P, 1])
        node_info = sb("node_info", [P, NT * 4])
        cmap = sb("cmap", [P, NT], I32)
        firstpos = sb("firstpos", [P, NT], I32)
        lastpos = sb("lastpos", [P, NT], I32)
        rcount = sb("rcount", [P, NT])
        small = sb("small", [P, 8 * NT])
        nd = sb("nd", [P, NT * 2])
        cols = sb("cols", [P, 64])
        edge_cols = sb("edge_cols", [P, 2], I32)
        carry_cols = sb("carry_cols", [P, 2])
        carry_row = sb("carry_row", [1, 4 * P])
        carry_in = sb("carry_in", [P, 1])
        bias_cols = sb("bias_cols", [P, 4])
        ids_int = sb("ids_int", [P, NT], I32)
        seg0_blk = sb("seg0_blk", [P, NB], I32)
        PS = ctx.enter_context(nc.psum_tensor("PS", [P, 8 * 512], F32))

        def bank(b, w=512):
            return PS[:, b * 512:b * 512 + w]

        X3 = X[:].rearrange("p (t f) -> p t f", f=D)
        G3 = G[:].rearrange("p (t f) -> p t f", f=D)
        T3 = T[:].rearrange("p (t f) -> p t f", f=D)
        H3 = H[:, 0:NT * D].rearrange("p (t f) -> p t f", f=D)
        stage = onehot[:].rearrange("p a b -> p (a b)")
        stage_in, stage_mid = stage[:, 0:CW], stage[:, 1024:1024 + CW]
        stage_out = rows[:].rearrange("p a b -> p (a b)")[:, 0:CW]
        macc = H[0:3, :]
        meta_t = G[:, 0:3 * ET]

        def scan_tmp(buf, i):
            return buf[:, i * ET:(i + 1) * ET]

        def vec(i):
            return vecs[:, i * D:(i + 1) * D]

        def vec_nodes(i, tiles=NT):
            return vec(i).unsqueeze(1).broadcast_to([P, tiles, D])

        def mat(i):
            return mats[:, i * D:(i + 1) * D]

        VEC = ["L0_gnn_bias", "L1_gnn_b3", "L2_0", "L2_1", "L2_2"]
        for l in (1, 2, 3):
            VEC += [f"L3_gnn_as{l}", f"L3_gnn_ad{l}", f"L3_gnn_b{l}", f"L3_gnn_g{l}", f"L3_gnn_be{l}"]
        vsrc = {n: a[n] for n in VEC if not n.startswith("L2_")}
        for l in range(3):
            vsrc[f"L2_{l}"] = a["L2_gnn_b"][l, :]
        MAT = ["ws_raw", "wn_raw", "ws", "wn", "W1", "W2", "W3", "agg0", "agg1", "agg2",
               "root0", "root1", "root2"]
        msrc = {"ws_raw": a["L0_gnn_W_self"], "wn_raw": a["L0_gnn_W_neigh"], "W1": a["L1_gnn_W1"],
                "W2": a["L1_gnn_W2"], "W3": a["L1_gnn_W3"]}
        for l in range(3):
            msrc[f"agg{l}"] = a["L2_gnn_W_agg"][l, :, :]
            msrc[f"root{l}"] = a["L2_gnn_W_root"][l, :, :]
        gat_w = sb("gat_w", [P, 3 * D])
        gat_a = sb("gat_a", [P, 6])
        V = {n: i for i, n in enumerate(VEC)}
        M = {n: i for i, n in enumerate(MAT)}
        row_matrix = {0: mat(M["ws"]), 1: mat(M["W3"]), 2: mat(M["root0"]), 3: mat(M["root1"]), 4: mat(M["root2"]),
                      5: gat_w[:, 0:D], 6: gat_w[:, D:2 * D], 7: gat_w[:, 2 * D:3 * D]}
        seg_matrix = {0: mat(M["wn"]), 2: mat(M["agg0"]), 3: mat(M["agg1"]),
                      4: mat(M["agg2"]), 5: ident[:], 6: ident[:], 7: ident[:]}
        bias_vec = {0: V["L0_gnn_bias"], 1: V["L1_gnn_b3"], 2: V["L2_0"], 3: V["L2_1"], 4: V["L2_2"],
                    5: V["L3_gnn_b1"], 6: V["L3_gnn_b2"], 7: V["L3_gnn_b3"]}

        def wide(buf, i):
            return buf[:, i * BE:(i + 1) * BE]
        rbf, lnp = wide(H, 0), wide(H, 1)
        attr = wide(G, 1)
        msg0 = wide(G, 2)
        msgf = wide(T, 0)
        keep = wide(T, 1)
        prod = wide(T, 2)
        scan_rows = onehot[:].rearrange("p a b -> p (a b)")
        filt = wide(H, 2)

        def real(i):
            return not isinstance(i, int) or 0 <= i < ITERS

        def wait(eng, semaphore, count):
            if not isinstance(count, int) or count > 0:
                eng.wait_ge(semaphore, count)

        def half(buf, h):
            return buf[:, h * BE // 2:(h + 1) * BE // 2]

        def banks(h):
            return PS[:, h * 1024:(h + 1) * 1024]

        dist_row = sb("dist_row", [3, BE], BF16)
        cut_row = sb("cut_row", [6, BE], BF16)
        lo_row = cut_row[0:1, :]

        dst_i, src_i, ew = scan_tmp(T, 0).bitcast(I32), scan_tmp(T, 1).bitcast(I32), scan_tmp(T, 2)
        dst_f, src_f, seg_s = scan_tmp(T, 3), scan_tmp(T, 4), scan_tmp(T, 5)
        cut_s, w0, w1, w2 = scan_tmp(T, 6), scan_tmp(T, 7), scan_tmp(H, 0), scan_tmp(H, 1)
        first_s, ones_s = scan_tmp(H, 2), scan_tmp(acc, 2)
        bf = H[:, 3 * ET:8 * ET].bitcast(BF16).rearrange("p (q e) -> p q e", q=10)
        blocks = acc[0:TB, 0:4 * NB * P].rearrange("p (q b c) -> p q b c", q=4, c=P)
        pos_i = acc[:, 5600:5600 + ET].bitcast(I32)
        dst_t, last_t, srcf_t = scan_tmp(T, 0), scan_tmp(T, 1), scan_tmp(T, 2)
        we_bc = G[:, 3 * ET:3 * ET + 9 * D]
        ae_bc = G[:, 3 * ET + 9 * D:3 * ET + 12 * D]
        wprod = G[:, 3 * ET + 12 * D:3 * ET + 21 * D]
        HALF_PI, NEGC, ASUM, VV, AMEAN, ALLSAME, NOLAST, PENALL, EPSC, TOTAL = 0, 1, 2, 5, 14, 17, 18, 19, 20, 21
        AMN, EDGE, THIRTY = 22, 25, 40

        def col(i, n=1):
            return cols[:, i:i + n]

        Gs = [scan_tmp(G, i) for i in range(8)]
        Hs = [scan_tmp(H, i) for i in range(4)]
        turned = H[0:TB, 4 * ET:4 * ET + NB * P]
        at_f = G[:, ET:3 * ET].rearrange("p (j c) -> p j c", c=2)
        at_l = H[:, 0:2 * ET].rearrange("p (j c) -> p j c", c=2)
        hot_bf = onehot[:].rearrange("p a b -> p (a b)")[:, 0:BE // 2].bitcast(BF16)\
            .rearrange("p (h a b) -> p h a b", h=2, b=D)
        nd3 = nd[:].rearrange("p (t c) -> p t c", c=2)
        attr_pre = G[:, 0:3 * ET]
        attr_att = acc[:, 0:3 * ET]
        attr3 = attr_att.rearrange("p (j c) -> p j c", c=3)
        info3 = node_info[:].rearrange("p (t c) -> p t c", c=4)
        als_n, ald_n, self_n, amax_n, exs_n, rden_n = (small[:, i * NT:(i + 1) * NT] for i in range(6))
        stat0, stat1 = small[:, 6 * NT:7 * NT], small[:, 7 * NT:8 * NT]

        consts = sem("consts")
        pads_set = sem("pads_set")
        loads = sem("loads")
        dve = sem("dve")
        act = sem("act")
        pre_in = sem("pre_in")
        pre_out = sem("pre_out")
        cut_in = sem("cut_in")
        cut_out = sem("cut_out")
        zeros_ready = sem("zeros_ready")
        zeros_stored = sem("zeros_stored")
        flats_ready = sem("flats_ready")
        flats_stored = sem("flats_stored")
        blocks_loaded = sem("blocks_loaded")
        seg0_ready = sem("seg0_ready")
        seg0_stored = sem("seg0_stored")
        seg0_loaded = sem("seg0_loaded")
        loc_ready = sem("loc_ready")
        tiles_turned = sem("tiles_turned")
        tiles_copied = sem("tiles_copied")
        tiles_ready = sem("tiles_ready")
        info_turned = sem("info_turned")
        info_ready = sem("info_ready")
        info_scattered = sem("info_scattered")
        info_loaded = sem("info_loaded")
        info_cols = sem("info_cols")
        h_ready = sem("h_ready")
        h_chunks = sem("h_chunks")
        table_stored = sem("table_stored")
        p_staged = sem("p_staged")
        p_turned = sem("p_turned")
        p_copied = sem("p_copied")
        p_product = sem("p_product")
        p_done = sem("p_done")
        idx_loaded = sems("idx_loaded", 2)
        gathered = sems("gathered", 2)
        onehot_ready = sems("onehot_ready", 2)
        multiplied = sems("multiplied", 2)
        added = sems("added", 2)
        meta_staged = sems("meta_staged", 2)
        meta_added = sems("meta_added", 2)
        c_staged = sem("c_staged")
        c_product = sem("c_product")
        c_copied = sem("c_copied")
        c_stored = sem("c_stored")
        node_rows = sems("node_rows", NCH)
        dist_in = sems("dist_in", 2)
        cut_in_row = sems("cut_in_row", 2)
        attr_in = sems("attr_in", 2)
        dist_bc = sem("dist_bc")
        squared = sem("squared")
        rbf_ready = sem("rbf_ready")
        z_ready = sems("z_ready", 2)
        clamped = sems("clamped", 2)
        exp_done = sems("exp_done", 2)
        ln_done = sems("ln_done", 2)
        soft_ready = sems("soft_ready", 2)
        msg_ready = sem("msg_ready")
        msg_turned = sem("msg_turned")
        msgf_ready = sem("msgf_ready")
        keep_bc = sem("keep_bc")
        start_bc = sem("start_bc")
        keep_ready = sem("keep_ready")
        start_ready = sem("start_ready")
        scanned = sem("scanned")
        scan_turned = sem("scan_turned")
        scan_copied = sem("scan_copied")
        prod_stored = sems("prod_stored", 2)
        ln_in = sem("ln_in")
        ln_out = sem("ln_out")
        var_ready = sem("var_ready")
        std_ready = sem("std_ready")
        sum_in = sem("sum_in")
        squares = sem("squares")
        sum_out = sem("sum_out")
        attr_space = sem("attr_space")
        attr_again = sem("attr_again")
        lo_in = sems("lo_in", 2)
        lo_bc = sems("lo_bc", 2)
        lo_hot = sems("lo_hot", 2)
        al_rows = sems("al_rows", 2)
        al_mask = sems("al_mask", 2)
        al_pick = sems("al_pick", 2)
        al_done = sems("al_done", 2)
        turn_out = sem("turn_out")
        turn_blk = sem("turn_blk")
        al_stored = sem("al_stored")
        al_loaded = sem("al_loaded")
        first_in = sem("first_in")
        first_sc = sem("first_sc")
        first_ld = sem("first_ld")
        last_in = sem("last_in")
        last_st = sem("last_st")
        last_fill = sem("last_fill")
        last_ga = sem("last_ga")
        exp_in = sem("exp_in")
        exp_out = sem("exp_out")
        ex_stored = sem("ex_stored")
        ex_loaded = sem("ex_loaded")
        ex_turned = sem("ex_turned")
        self_in = sem("self_in")
        self_out = sem("self_out")
        carry_in_ready = sem("carry_in_ready")
        carry_rows = sem("carry_rows")
        carry_scanned = sem("carry_scanned")
        carry_cols_out = sem("carry_cols_out")
        out_ready = sem("out_ready")
        out_stored = sem("out_stored")

        by_chunks = {1: 0, 3: NCH, 4: 2 * NCH, 5: 3 * NCH, 6: 4 * NCH, 7: 5 * NCH}
        whole_inputs = {0: 1, 2: 2}
        table_parts = np.cumsum([1, NCH, 1] + 5 * [NCH]).tolist()
        turn = {k: k - (k > 1) for k in range(K)}

        def hold(eng):
            eng.nop(nofuse=True)

        def stepper(eng, own):
            count = {}

            def step(ins, s=own):
                count[s] = count.get(s, 0) + 1
                ins.then_inc(s, 1)
                eng.wait_ge(s, count[s])
            return step

        ctx.enter_context(nc.allow_non_contiguous_dma(reason="a few hundred single words at the start"))
        block = ctx.enter_context(nc.Block())

        @block.sync
        def _(sp):
            sp.wait_ge(pads_set, 1)
            sent = []

            def load(dst, src):
                sp.dma_start(dst, src).then_inc(loads, 16)
                sent.append(1)

            head_e = (P - 1) * ET
            for dst, name in ((dst_i, "dst"), (src_i, "src"), (ew, "edge_weight")):
                load(dst[0:P - 1, :], a[name][0:head_e].rearrange("(p j) -> p j", j=ET))
                load(dst[P - 1:P, 0:SROWS], a[name][head_e:E].unsqueeze(0))
            load(edge_cols[1:P, 0:1], a["dst"][ET - 1:ET + (P - 2) * ET:ET].unsqueeze(1))
            load(edge_cols[0:P - 1, 1:2], a["dst"][ET:ET + (P - 2) * ET + 1:ET].unsqueeze(1))
            attr_head = a["edge_attr_3"][0:head_e, :].rearrange("(p j) c -> p (j c)", j=ET)
            attr_rest = a["edge_attr_3"][head_e:E, :].rearrange("(o j) c -> o (j c)", o=1)
            load(attr_pre[0:P - 1, :], attr_head)
            load(attr_pre[P - 1:P, 0:3 * SROWS], attr_rest)
            load(X3[:, 0:NT - 1, :], a["x"][0:(NT - 1) * P, :].rearrange("(t p) f -> p t f", p=P))
            load(X3[0:NLAST, NT - 1, :], a["x"][(NT - 1) * P:N, :])
            for n, i in V.items():
                load(vec(i), vsrc[n].unsqueeze(0).broadcast_to([P, D]))
            for n in msrc:
                load(mat(M[n]), msrc[n])
            for l in range(3):
                load(gat_w[:, l * D:(l + 1) * D], a[f"L3_gnn_W{l + 1}"])
                load(we_bc[:, l * 3 * D:(l + 1) * 3 * D],
                     a[f"L3_gnn_We{l + 1}"].rearrange("(o c) f -> o (c f)", o=1).broadcast_to([P, 3 * D]))
                load(ae_bc[:, l * D:(l + 1) * D], a[f"L3_gnn_ae{l + 1}"].unsqueeze(0).broadcast_to([P, D]))
            load(bias_cols[:, 0:1], a["L1_gnn_b1"].unsqueeze(1))
            load(bias_cols[:, 1:2], a["L1_gnn_b2"].unsqueeze(1))
            assert len(sent) == LOADS

            sp.wait_ge(zeros_ready, 1)
            sp.dma_start(at_first.rearrange("(p j) c -> p (j c)", p=P), acc[:, 0:2 * ET]).then_inc(zeros_stored, 16)
            sp.dma_start(node_table.rearrange("(t p) c -> p t c", p=P), info3).then_inc(zeros_stored, 16)

            sp.wait_ge(flats_ready, 1)
            for q, t in enumerate((seg_s, dst_f, last_s[:], src_f)):
                sp.dma_start(flats[q, :].rearrange("(p j) -> p j", p=P), t).then_inc(flats_stored, 16)
            for q in range(10):
                sp.dma_start(flat_bf[q, :].rearrange("(p j) -> p j", p=P), bf[:, q, :]).then_inc(flats_stored, 16)
            sp.wait_ge(flats_stored, 16 * 14)
            sp.wait_ge(zeros_stored, 32)
            for q in range(4):
                sp.dma_start(blocks[:, q, :, :], flats[q, :].rearrange("(b t c) -> t b c", t=TB, c=P))\
                    .then_inc(blocks_loaded, 16)
            sp.wait_ge(seg0_ready, 1)
            sp.dma_start(first_of_tile.rearrange("(b t) -> t b", t=TB), seg0_blk[0:TB, :]).then_inc(seg0_stored, 16)
            sp.wait_ge(seg0_stored, 16)
            sp.dma_start(seg0_row[:], first_of_tile.unsqueeze(0)).then_inc(seg0_loaded, 16)

            def index_load(k, i, h):
                sp.wait_ge(gathered[h], i * (16 * HT) + k * (ITERS * 16 * HT))
                sp.dma_start(idx_buf[:, h * HT:(h + 1) * HT], src_t[:, ds(i * BT + h * HT, HT)])\
                    .then_inc(idx_loaded[h], 16)

            def distances(i, h):
                wait(sp, dist_bc, i * 2 + h - 1)
                sp.dma_start(half(dist_row, h), flat_bf[0:3, ds(i * BE + h * HE, HE)]).then_inc(dist_in[h], 16)

            def attributes(i, h):
                wait(sp, msg_ready, i * 2 + h - 1)
                e = i * BE + h * HE
                tiles = HT if not isinstance(i, int) else min(HT, (E - e) // P)
                sp.dma_start(half(attr, h)[:, 0:tiles * D].rearrange("p (t f) -> p t f", f=D),
                             a["edge_attr_128"][ds(e, tiles * P), :].rearrange("(t p) f -> p t f", p=P))\
                    .then_inc(attr_in[h], 16)
                if tiles < HT:
                    e += tiles * P
                    sp.dma_start(half(attr, h)[0:E - e, tiles * D:(tiles + 1) * D], a["edge_attr_128"][e:E, :])\
                        .then_inc(attr_in[h], 16)

            def store_products(i, h):
                if real(i):
                    sp.wait_ge(scan_copied, i * 2 + h + 1)
                    sp.dma_start(prod_rows[ds(i * BE + h * HE, HE), :].rearrange("(t p) f -> p t f", p=P),
                                 half(scan_rows, h).rearrange("p (t f) -> p t f", f=D)).then_inc(prod_stored[h], 16)

            def product_transfers(i):
                for h in range(2):
                    attributes(i, h)
                    index_load(1, i, h)
                    if real(i + 1):
                        distances(i + 1, h)
                    store_products(i - 2 + h, 1 - h)
                    wait(sp, start_bc, i * 2 + h - 1)
                    sp.dma_start(half(cut_row, h), flat_bf[3:9, ds(i * BE + h * HE, HE)]).then_inc(cut_in_row[h], 16)

            def store_chunk(k, c, rows3):
                sp.dma_start(table[k % 2][c * CH * P:(c + 1) * CH * P, :].rearrange("(t p) f -> p t f", p=P),
                             rows3[:, c * CH:(c + 1) * CH, :]).then_inc(table_stored, 16)

            for k in range(K):
                if k in GAT:
                    l = k - 5
                    for c in range(NCH):
                        sp.wait_ge(p_done, k * NCH + c + 1)
                        store_chunk(k, c, T3)
                    sp.wait_ge(attr_space, l + 1)
                    sp.dma_start(attr_att[0:P - 1, :], attr_head).then_inc(attr_again, 16)
                    sp.dma_start(attr_att[P - 1:P, 0:3 * SROWS], attr_rest).then_inc(attr_again, 16)
                    with sp.Fori(0, ITERS) as i:
                        for h in range(2):
                            sp.wait_ge(lo_bc[h], i + l * ITERS)
                            sp.dma_start(lo_row[:, h * 1024:(h + 1) * 1024], flat_bf[9:10, ds(i * BE + h * 1024, 1024)])\
                                .then_inc(lo_in[h], 16)
                    sp.wait_ge(turn_blk, l + 1)
                    sp.dma_start(al_flat.rearrange("(b t c) -> t b c", t=TB, c=P),
                                 turned.rearrange("p (b c) -> p b c", c=P)).then_inc(al_stored, 16)
                    sp.wait_ge(al_stored, 16 * (l + 1))
                    sp.dma_start(Gs[0], al_flat.rearrange("(p j) -> p j", p=P)).then_inc(al_loaded, 16)
                    sp.wait_ge(first_sc, 16 * NT * (l + 1))
                    sp.dma_start(G[:, ET:3 * ET], at_first.rearrange("(p j) c -> p (j c)", p=P)).then_inc(first_ld, 16)
                    sp.wait_ge(exp_out, l + 1)
                    sp.dma_start(ex_flat.rearrange("(p j) -> p j", p=P), Gs[6]).then_inc(ex_stored, 16)
                    sp.wait_ge(ex_stored, 16 * (l + 1))
                    sp.dma_start(turned.rearrange("p (b c) -> p b c", c=P),
                                 ex_flat.rearrange("(b t c) -> t b c", t=TB, c=P)).then_inc(ex_loaded, 16)
                    sp.wait_ge(last_in, l + 1)
                    sp.dma_start(at_last.rearrange("(p j) c -> p (j c)", p=P), H[:, 0:2 * ET]).then_inc(last_st, 16)
                elif k in by_chunks:
                    for c in range(NCH):
                        sp.wait_ge(h_chunks, by_chunks[k] + c + 1)
                        store_chunk(k, c, H3)
                else:
                    sp.wait_ge(h_ready, whole_inputs[k])
                    sp.dma_start(table[k % 2].rearrange("(t p) f -> p t f", p=P), H3).then_inc(table_stored, 16)
                if k == 0:
                    sp.wait_ge(tiles_ready, 1)
                if k == 1:
                    for h in range(2):
                        distances(0, h)
                    for i in range(2):
                        product_transfers(i)
                    with sp.Fori(2, ITERS - 1) as i:
                        product_transfers(i)
                    product_transfers(ITERS - 1)
                    for m in range(BODY_HALVES - 3, BODY_HALVES):
                        store_products(m // 2, m % 2)
                else:
                    with sp.Fori(0, ITERS) as i:
                        for h in range(2):
                            index_load(k, i, h)
                if k == 1:
                    continue
                with sp.Fori(0, NCH) as i:
                    sp.wait_ge(c_copied, i + 1 + turn[k] * NCH)
                    sp.dma_start(seg_rows[ds(i * (CH * P), CH * P), :].rearrange("(t p) f -> p t f", p=P),
                                 stage_out.rearrange("p (t f) -> p t f", f=D)).then_inc(c_stored, 16)
                if k == 0:
                    sp.wait_ge(info_scattered, 16 * NT)
                    sp.dma_start(info3, node_table.rearrange("(t p) c -> p t c", p=P)).then_inc(info_loaded, 16)
            for c in range(NCH):
                sp.wait_ge(out_ready, c + 1)
                last_tile = min((c + 1) * CH, NT - 1)
                sp.dma_start(out[c * CH * P:last_tile * P, :].rearrange("(t p) f -> p t f", p=P),
                             X3[:, c * CH:last_tile, :]).then_inc(out_stored, 16)
            sp.dma_start(out[(NT - 1) * P:N, :], X3[0:NLAST, NT - 1, :]).then_inc(out_stored, 16)
            sp.wait_ge(out_stored, 16 * (NCH + 1))

        @block.gpsimd
        def _(pool):
            step = stepper(pool, consts)
            step(pool.iota(iota_int[:], pattern=[[1, D]], base=0, channel_multiplier=0))
            step(pool.iota(iota_coli[:], pattern=[[0, 1]], base=0, channel_multiplier=1))
            step(pool.iota(ids_int[:], pattern=[[P, NT]], base=0, channel_multiplier=1))
            step(pool.iota(pos_i, pattern=[[P, ET]], base=0, channel_multiplier=1))
            step(pool.memset(ones[:], 1.0))
            step(pool.memset(ident[:], 0.0))
            step(pool.affine_select(out=ident[:], in_=ident[:], compare_op=ALU.not_equal, fill=1.0, base=0,
                                    pattern=[[-1, P]], channel_multiplier=1))
            step(pool.affine_select(out=before[:], in_=ones[:], compare_op=ALU.is_gt, fill=0.0, base=0,
                                    pattern=[[1, P]], channel_multiplier=-1))
            step(pool.affine_select(out=rowmask[:], in_=ones[:, 0:1], compare_op=ALU.is_gt, fill=0.0, base=NLAST,
                                    pattern=[[0, 1]], channel_multiplier=-1))

            def at(idx):
                return bass.IndirectOffsetOnAxis(idx, 0)

            for k in range(K):
                if k in GAT:
                    l = k - 5
                    pool.wait_ge(first_in, l + 1)
                    for t in range(NT):
                        pool.indirect_dma_start(at_first, at(firstpos[:, t:t + 1]), nd[:, 2 * t:2 * t + 2], None,
                                                bounds_check=EPAD - 1, oob_is_err=False).then_inc(first_sc, 16)
                pool.wait_ge(table_stored, 16 * table_parts[k])
                def gathers(i, h):
                    pool.wait_ge(idx_loaded[h], 16 * (i + 1) + k * (ITERS * 16))
                    if k == 1:
                        wait(pool, msg_ready, i * 2 + h - 1)
                    else:
                        wait(pool, multiplied[h], i + turn[k] * ITERS)
                    hold(pool)
                    for j in range(h * HT, (h + 1) * HT):
                        pool.indirect_dma_start(rows[:, j, :], None, table[k % 2], at(idx_buf[:, j:j + 1]))\
                            .then_inc(gathered[h], 16)

                for h in range(2):
                    gathers(0, h)
                with pool.Fori(1, ITERS) as i:
                    for h in range(2):
                        gathers(i, h)
                if k == 0:
                    pool.wait_ge(info_ready, 1)
                    for t in range(NT):
                        pool.indirect_dma_start(node_table, at(cmap[:, t:t + 1]), node_info[:, 4 * t:4 * t + 4], None,
                                                bounds_check=NPAD - 1, oob_is_err=False).then_inc(info_scattered, 16)
                    pool.wait_ge(info_cols, 1)
                if k in GAT:
                    pool.wait_ge(last_st, 16 * (l + 1))
                    pool.wait_ge(last_fill, l + 1)
                    for t in range(NT):
                        pool.indirect_dma_start(nd[:, 2 * t:2 * t + 2], None, at_last, at(lastpos[:, t:t + 1]),
                                                bounds_check=EPAD - 1, oob_is_err=False).then_inc(last_ga, 16)
                if k == 1:
                    for h in range(2):
                        pool.wait_ge(prod_stored[h], 16 * ITERS)
                    for t in range(NT):
                        pool.indirect_dma_start(acc[:, t * D:(t + 1) * D], None, prod_rows, at(lastpos[:, t:t + 1]),
                                                bounds_check=EPAD - 1, oob_is_err=False).then_inc(node_rows[t // CH], 16)
                    continue
                for t in range(NT):
                    if t == 0 or (t + 1) % CH == 0:
                        pool.wait_ge(c_stored, 16 * min(NCH, (t + 1) // CH + 1) + turn[k] * (NCH * 16))
                    pool.indirect_dma_start(G3[:, t, :], None, seg_rows, at(cmap[:, t:t + 1])).then_inc(node_rows[t // CH], 16)

        @block.scalar
        def _(s):
            step = stepper(s, act)
            s.wait_ge(cut_in, 1)
            step(nc.scalar.activation(w0, w0, ACT.Abs))
            nc.scalar.activation(w1, w0, ACT.Sin, bias=col(HALF_PI), scale=-2.0 * np.pi).then_inc(cut_out, 1)
            n_sqrt = 0

            def sqrt(scale, src, dst):
                nonlocal n_sqrt
                n_sqrt += 1
                s.wait_ge(var_ready, n_sqrt)
                nc.scalar.activation(dst, src, ACT.Sqrt, bias=col(EPSC), scale=scale).then_inc(std_ready, 1)

            def stage_turned(k, c):
                s.wait_ge(p_turned, c + 1 + k * NCH)
                wait(s, p_product, c + k * NCH)
                hold(s)
                nc.scalar.activation(stage_mid, PS[:, 0:CW], ACT.Copy).then_inc(p_copied, 1)

            def stage_chunks(k):
                s.wait_ge(c_product, turn[k] * NCH)
                for c in range(NCH):
                    if k == 5:
                        sqrt(1.0 / D, stat1[:, c * CH:(c + 1) * CH], stat1[:, c * CH:(c + 1) * CH])
                    s.wait_ge(h_chunks, by_chunks[k] + c + 1)
                    s.wait_ge(p_turned, c + k * NCH)
                    nc.scalar.activation(stage_in, H[:, c * CW:(c + 1) * CW], ACT.Copy).then_inc(p_staged, 1)
                    stage_turned(k, c)

            def stage_rows(k):
                s.wait_ge(h_ready, whole_inputs[k])
                with s.Fori(0, NCH) as i:
                    s.wait_ge(p_turned, i + k * NCH)
                    hold(s)
                    nc.scalar.activation(stage_in, H[:, ds(i * CW, CW)], ACT.Copy).then_inc(p_staged, 1)
                    stage_turned(k, i)

            def stage_products():
                for c in range(NCH):
                    s.wait_ge(node_rows[c], 2 * CH * 16)
                    s.wait_ge(p_turned, c + NCH)
                    nc.scalar.activation(stage_in, acc[:, c * CW:(c + 1) * CW], ACT.Copy).then_inc(p_staged, 1)
                    stage_turned(1, c)

            def stage_segments(k):
                for h in range(2):
                    s.wait_ge(added[h], (turn[k] + 1) * (ITERS * HT))
                with s.Fori(0, NCH) as i:
                    s.wait_ge(c_product, i + turn[k] * NCH)
                    hold(s)
                    nc.scalar.activation(stage_in, acc[:, ds(i * CW, CW)], ACT.Copy).then_inc(c_staged, 1)

            def product_slot(i, h):
                i0, m0 = i + 1, (i + 1) * 2 + h
                i1, h1 = (i + 1, 0) if h else (i, 1)
                m1 = i1 * 2 + h1
                if real(i0):
                    s.wait_ge(dist_bc, m0 + 1)
                    wait(s, z_ready[1], m0 - 1)
                    hold(s)
                    nc.scalar.activation(half(rbf, h), banks(h), ACT.Square, bias=col(NEGC)).then_inc(squared, 1)
                scan_copy(*((i, 0) if h else (i - 1, 1)))
                if real(i0):
                    s.wait_ge(squared, m0 + 1)
                    nc.scalar.activation(half(rbf, h), half(rbf, h), ACT.Exp, scale=COEFF).then_inc(rbf_ready, 1)
                if real(i1):
                    s.wait_ge(z_ready[1], m1 + 1)
                    s.wait_ge(soft_ready[0], m1 + 1)
                    logarithm(1, h1, m1)
                if real(i0):
                    s.wait_ge(z_ready[0], m0 + 1)
                    wait(s, soft_ready[1], m0 - 1)
                    logarithm(0, h, m0)

            def logarithm(n, h, m):
                hold(s)
                nc.scalar.activation(half(lnp, h), banks(h), ACT.Relu, bias=bias_cols[:, 2 + n:3 + n], scale=-1.0)\
                    .then_inc(clamped[n], 1)
                s.wait_ge(clamped[n], m + 1)
                nc.scalar.activation(half(lnp, h), half(lnp, h), ACT.Exp, bias=col(THIRTY), scale=-1.0)\
                    .then_inc(exp_done[n], 1)
                s.wait_ge(exp_done[n], m + 1)
                nc.scalar.activation(half(lnp, h), half(lnp, h), ACT.Ln, bias=1.0).then_inc(ln_done[n], 1)

            def scan_copy(i, h):
                if real(i):
                    s.wait_ge(scan_turned, i * 2 + h + 1)
                    wait(s, prod_stored[h], i * 16)
                    hold(s)
                    nc.scalar.activation(half(scan_rows, h), banks(2 + h), ACT.Copy).then_inc(scan_copied, 1)

            for k in range(K):
                if k in (0, 2):
                    sqrt(1.0 / D, stat1, stat1)
                if k == 1:
                    for c in range(NCH):
                        sqrt(1.0 / D, stat1[:, c * CH:(c + 1) * CH], stat1[:, c * CH:(c + 1) * CH])
                elif k in by_chunks:
                    stage_chunks(k)
                else:
                    stage_rows(k)
                if k == 0:
                    s.wait_ge(tiles_ready, 1)
                    with s.Fori(0, ITERS) as i:
                        for h in range(2):
                            s.wait_ge(multiplied[h], i + turn[0] * ITERS)
                            hold(s)
                            nc.scalar.activation(meta_buf[:, h * HT * 3:(h + 1) * HT * 3],
                                                 meta_t[:, ds(i * (BT * 3) + h * HT * 3, HT * 3)],
                                                 ACT.Copy).then_inc(meta_staged[h], 1)
                if k == 1:
                    s.preload_act_table_set("natural_log_exp_and_others")
                    s.wait_ge(table_stored, 16 * table_parts[1])
                    for i in (-1, 0):
                        for h in range(2):
                            product_slot(i, h)
                    with s.Fori(1, ITERS - 2) as i:
                        for h in range(2):
                            product_slot(i, h)
                    for i in (ITERS - 2, ITERS - 1):
                        for h in range(2):
                            product_slot(i, h)
                    scan_copy(ITERS - 1, 1)
                if k in GAT:
                    s.wait_ge(exp_in, k - 4)
                    nc.scalar.activation(Gs[6], Gs[5], ACT.Exp).then_inc(exp_out, 1)
                if k != 1:
                    stage_segments(k)
                else:
                    stage_products()
                    s.wait_ge(ln_in, 1)
                    step(nc.scalar.activation(G[:], G[:], ACT.Exp))
                    nc.scalar.activation(G[:], G[:], ACT.Ln, bias=1.0).then_inc(ln_out, 1)
                if k in GAT:
                    s.wait_ge(self_in, k - 4)
                    nc.scalar.activation(exs_n, exs_n, ACT.Exp).then_inc(self_out, 1)
                    for c in range(NCH):
                        s.wait_ge(sum_in, (2 * (k - 5) + 1) * NCH + c + 1)
                        nc.scalar.activation(G[:, c * CW:(c + 1) * CW], H[:, c * CW:(c + 1) * CW], ACT.Square)\
                            .then_inc(squares, 1)
                    sqrt(1.0 / N, acc[:, 2 * D:3 * D], acc[:, 3 * D:4 * D])

        @block.tensor
        def _(pe):
            mm, tr = nc.tensor.matmul, nc.tensor.transpose
            pe.wait_ge(consts, CONSTS)
            pe.wait_ge(loads, 16 * LOADS)
            pe.wait_ge(pre_in, 1)
            tr(PS[:, 0:D], mat(M["ws_raw"]), ident[:])
            tr(PS[:, D:2 * D], mat(M["wn_raw"]), ident[:])
            mm(PS[:, 512:513], mat(M["W2"]), ones[:, 0:1], start=True, stop=True)
            mm(PS[:, 1024:1025], before[:], col(TOTAL), start=True, stop=True)
            mm(PS[:, 1536:1539], ones[:], col(ASUM, 3), start=True, stop=True).then_inc(pre_out, 1)
            pe.wait_ge(blocks_loaded, 64)
            pe.wait_ge(loc_ready, 1)
            for q in range(4):
                base = 2048 + (q % 2) * 1024
                if q >= 2:
                    pe.wait_ge(tiles_copied, q - 1)
                for b in range(NB):
                    o = base + (b // 4) * 512 + (b % 4) * TB
                    last = tr(PS[:, o:o + TB], blocks[:, q, b, :], ident[0:TB, 0:TB])
                last.then_inc(tiles_turned, 1)

            def chunk_product(k, i):
                pe.wait_ge(p_staged, i + 1 + k * NCH)
                wait(pe, p_copied, i + k * NCH)
                for j in range(CH):
                    last = tr(PS[:, j * D:(j + 1) * D], stage_in[:, j * D:(j + 1) * D], ident[:])
                last.then_inc(p_turned, 1)
                pe.wait_ge(p_copied, i + 1 + k * NCH)
                wait(pe, p_done, i + k * NCH)
                for j in range(CH):
                    turned_rows = stage_mid[:, j * D:(j + 1) * D]
                    last = mm(PS[:, 1024 + j * D:1024 + (j + 1) * D], turned_rows, row_matrix[k], start=True, stop=True)
                    if k in GAT:
                        o = 2048 + (i * CH + j) * 2
                        last = mm(PS[:, o:o + 2], turned_rows, gat_a[:, 2 * (k - 5):2 * (k - 4)], start=True, stop=True)
                last.then_inc(p_product, 1)

            def rows_product(k):
                if k in GAT:
                    for i in range(NCH):
                        chunk_product(k, i)
                else:
                    with pe.Fori(0, NCH) as i:
                        chunk_product(k, i)

            def segment_product(k):
                with pe.Fori(0, NCH) as i:
                    pe.wait_ge(c_staged, i + 1 + turn[k] * NCH)
                    pe.wait_ge(c_copied, i + turn[k] * NCH)
                    for j in range(CH):
                        last = mm(PS[:, 1024 + j * D:1024 + (j + 1) * D], stage_in[:, j * D:(j + 1) * D],
                                  seg_matrix[k], start=True, stop=True)
                    last.then_inc(c_product, 1)

            def edge_pass(k):
                with pe.Fori(0, ITERS) as i:
                    for h in range(2):
                        pe.wait_ge(gathered[h], (i + 1) * (16 * HT) + k * (ITERS * 16 * HT))
                        pe.wait_ge(onehot_ready[h], i + 1 + turn[k] * ITERS)
                        pe.wait_ge(added[h], i * HT + turn[k] * (ITERS * HT))
                        if k == 0:
                            pe.wait_ge(meta_staged[h], i + 1)
                            pe.wait_ge(meta_added[h], i * HT)
                        for j in range(HT):
                            o, r = h * 1024 + j * D, h * HT + j
                            last = mm(PS[:, o:o + D], rows[:, r, :], onehot[:, r, :], start=True, stop=True)
                            if k == 0:
                                last = mm(PS[0:3, 2048 + o:2048 + o + D], meta_buf[:, 3 * r:3 * r + 3],
                                          onehot[:, r, :], start=True, stop=True)
                        last.then_inc(multiplied[h], 1)

            def filter_step(n, i, h):
                if real(i):
                    pe.wait_ge(soft_ready[0] if n else rbf_ready, i * 2 + h + 1)
                    for q in (2 * h, 2 * h + 1):
                        last = mm(bank(q), mat(M["W2" if n else "W1"]), rbf[:, q * 512:(q + 1) * 512],
                                  start=True, stop=True)
                    last.then_inc(z_ready[n], 1)

            def spread_distances(i, h):
                if real(i):
                    pe.wait_ge(dist_in[h], (i + 1) * 16)
                    wait(pe, soft_ready[1], i * 2 + h - 1)
                    for q in (2 * h, 2 * h + 1):
                        last = mm(bank(q), ones_bf[:], dist_row[:, q * 512:(q + 1) * 512], start=True, stop=True)
                    last.then_inc(dist_bc, 1)

            def turn_messages(i, h):
                if real(i):
                    pe.wait_ge(msg_ready, i * 2 + h + 1)
                    wait(pe, scan_copied, i * 2 + h - 1)
                    for j in range(h * HT, (h + 1) * HT):
                        last = tr(PS[:, 2048 + j * D:2048 + (j + 1) * D], msg0[:, j * D:(j + 1) * D], ident[:])
                    last.then_inc(msg_turned, 1)

            def spread_cutoffs(i, h, pick, after, done):
                if real(i):
                    pe.wait_ge(cut_in_row[h], (i + 1) * 16)
                    pe.wait_ge(after, i * 2 + h + 1)
                    for q in (2 * h, 2 * h + 1):
                        last = mm(bank(4 + q), pick[:], cut_row[:, q * 512:(q + 1) * 512], start=True, stop=True)
                    last.then_inc(done, 1)

            def turn_scans(i, h):
                if real(i):
                    pe.wait_ge(scanned, i * 2 + h + 1)
                    for j in range(h * HT, (h + 1) * HT):
                        last = tr(PS[:, 2048 + j * D:2048 + (j + 1) * D], prod[:, j * D:(j + 1) * D], ident[:])
                    last.then_inc(scan_turned, 1)

            def product_slot(i, h):
                filter_step(1, *((i + 1, 0) if h else (i, 1)))
                spread_cutoffs(i, h, pick_keep, msgf_ready, keep_bc)
                filter_step(0, i + 1, h)
                spread_cutoffs(i, h, pick_start, keep_ready, start_bc)
                turn_messages(*((i + 1, 0) if h else (i, 1)))
                spread_distances(*((i + 2, 0) if h else (i + 1, 1)))
                turn_scans(i, h)

            n_carry = 0

            def carries(n):
                nonlocal n_carry
                for _ in range(n):
                    n_carry += 1
                    pe.wait_ge(carry_in_ready, n_carry)
                    tr(PS[0:1, 3072:3072 + P], carry_cols[:, 0:1], ident[:])
                    tr(PS[0:1, 3072 + P:3072 + 2 * P], carry_cols[:, 1:2], ident[:]).then_inc(carry_rows, 1)
                    pe.wait_ge(carry_scanned, n_carry)
                    tr(PS[:, 3584:3585], carry_row[0:1, 3 * P:4 * P], ident[0:1, 0:1]).then_inc(carry_cols_out, 1)

            def attention(l):
                def spread(i, h):
                    pe.wait_ge(lo_in[h], (i + 1 + l * ITERS) * 16)
                    pe.wait_ge(lo_hot[h], i + l * ITERS)
                    for q in (2 * h, 2 * h + 1):
                        last = mm(bank(q), ones_bf[0:1, :], lo_row[:, q * 512:(q + 1) * 512], start=True, stop=True)
                    last.then_inc(lo_bc[h], 1)

                def candidates(i, h):
                    pe.wait_ge(lo_hot[h], i + 1 + l * ITERS)
                    pe.wait_ge(al_pick[h], i + l * ITERS)
                    for j in range(HT):
                        o = (4 + h) * 512 + j * NT
                        for part in range(3):
                            last = mm(PS[:, o:o + NT], hot_bf[:, h, j, :], als_bf[:, part * NT:(part + 1) * NT],
                                      start=(part == 0), stop=(part == 2))
                    last.then_inc(al_rows[h], 1)

                pe.wait_ge(first_in, l + 1)
                for h in range(2):
                    spread(0, h)
                with pe.Fori(0, ITERS - 1) as i:
                    for h in range(2):
                        candidates(i, h)
                        spread(i + 1, h)
                for h in range(2):
                    candidates(ITERS - 1, h)
                    pe.wait_ge(al_done[h], ITERS + l * ITERS)
                for b in range(NB):
                    last = tr(PS[0:TB, 3072 + b * P:3072 + (b + 1) * P], als_t[:, b * TB:(b + 1) * TB], ident[:])
                last.then_inc(turn_out, 1)
                pe.wait_ge(turn_blk, l + 1)
                carries(5)
                pe.wait_ge(ex_loaded, 16 * (l + 1))
                for b in range(NB):
                    o = 2048 + (b // 4) * 512 + (b % 4) * TB
                    last = tr(PS[:, o:o + TB], turned[:, b * P:(b + 1) * P], ident[0:TB, 0:TB])
                last.then_inc(ex_turned, 1)

            def statistics(l):
                for n in range(2):
                    for c in range(NCH):
                        if n == 0:
                            pe.wait_ge(sum_in, 2 * l * NCH + c + 1)
                        else:
                            pe.wait_ge(squares, l * NCH + c + 1)
                        for t in range(c * CH, (c + 1) * CH):
                            last = mm(PS[:, 0:D], ones[:], (G3 if n else H3)[:, t, :],
                                      start=(t == 0), stop=(t == NT - 1))
                    last.then_inc(sum_out, 1)

            for k in range(K):
                if k > 2:
                    pe.wait_ge(c_copied, turn[k] * NCH)
                if k != 1:
                    rows_product(k)
                if k == 1:
                    spread_distances(0, 0)
                    for i in (-1, 0):
                        for h in range(2):
                            product_slot(i, h)
                    with pe.Fori(1, ITERS - 2) as i:
                        for h in range(2):
                            product_slot(i, h)
                    for i in (ITERS - 2, ITERS - 1):
                        for h in range(2):
                            product_slot(i, h)
                    rows_product(1)
                    continue
                else:
                    if k in GAT:
                        attention(k - 5)
                    edge_pass(k)
                if k == 0:
                    for h in range(2):
                        pe.wait_ge(meta_added[h], ITERS * HT)
                    for t in range(NT):
                        last = tr(PS[:, 2560 + 3 * t:2563 + 3 * t], macc[:, t * P:(t + 1) * P], ident[0:3, 0:3])
                    last.then_inc(info_turned, 1)
                segment_product(k)
                if k in GAT:
                    statistics(k - 5)

        @block.vector
        def _(v):
            tt, ts, stt = nc.vector.tensor_tensor, nc.vector.tensor_scalar, nc.vector.scalar_tensor_tensor
            copy, memset, reduce = nc.vector.tensor_copy, nc.vector.memset, nc.vector.tensor_reduce
            scan, recip = nc.vector.tensor_tensor_scan, nc.vector.reciprocal
            step = stepper(v, dve)

            step(memset(dst_i, N))
            step(memset(src_i, 0))
            step(memset(ew, R_MAX))
            step(memset(edge_cols[:], -1))
            step(memset(X3[:, NT - 1, :], 0.0))
            memset(attr_pre, 0.0).then_inc(pads_set, 1)
            step(memset(acc[:, 0:2 * ET], 0.0))
            step(memset(col(HALF_PI), float(np.pi / 2)))
            step(memset(col(EPSC), EPS))
            step(memset(ones_bf[:], 1.0))
            step(memset(ones_s, 1.0))
            step(memset(col(THIRTY), 30.0))
            step(memset(pick_start[:], 1.0))
            step(memset(pick_start[0:3, :], 0.0))
            step(memset(pick_keep[:], 0.0))
            step(memset(pick_keep[0:3, :], 1.0))
            step(memset(info3[:, :, 0:1], 0.0))
            step(memset(info3[:, :, 1:3], BIGPOS))
            memset(info3[:, :, 3:4], 0.0).then_inc(zeros_ready, 1)
            v.wait_ge(consts, CONSTS)
            step(copy(iota_row[:], iota_int[:]))
            step(copy(iota_col[:], iota_coli[:]))
            step(ts(col(NEGC), iota_col[:], -DELTA, None, ALU.mult))
            v.wait_ge(loads, 16 * LOADS)
            step(copy(dst_f, dst_i))
            step(copy(src_f, src_i))
            step(copy(col(EDGE, 2), edge_cols[:]))
            step(tt(first_s[:, 1:ET], dst_f[:, 1:ET], dst_f[:, 0:ET - 1], ALU.not_equal))
            step(tt(first_s[:, 0:1], dst_f[:, 0:1], col(EDGE), ALU.not_equal))
            step(copy(last_s[:, 0:ET - 1], first_s[:, 1:ET]))
            step(tt(last_s[:, ET - 1:ET], dst_f[:, ET - 1:ET], col(EDGE + 1), ALU.not_equal))
            step(ts(same_s[:], first_s, -1.0, 1.0, ALU.mult, ALU.add))
            step(reduce(col(ALLSAME), same_s[:], AX.X, ALU.min))
            step(ts(col(PENALL), col(ALLSAME), -1.0, HUGE, ALU.add, ALU.mult))
            step(reduce(col(NOLAST), last_s[:], AX.X, ALU.max))
            step(ts(col(NOLAST), col(NOLAST), -1.0, 1.0, ALU.mult, ALU.add))
            step(scan(seg_s, ones_s, first_s, 0.0, ALU.mult, ALU.add))
            step(copy(col(TOTAL), seg_s[:, ET - 1:ET]))
            reduce(col(ASUM, 3), attr_pre.rearrange("p (j c) -> p c j", c=3), AX.X, ALU.add).then_inc(pre_in, 1)
            step(ts(w0, ew, 0.1, MAGIC, ALU.mult, ALU.add))
            step(ts(w0, w0, -MAGIC, None, ALU.add))
            stt(w0, ew, 0.1, w0, ALU.mult, ALU.subtract).then_inc(cut_in, 1)
            def in_parts(parts, x):
                step(copy(parts[0], x))
                step(tt(x, x, parts[0], ALU.subtract))
                step(copy(parts[1], x))
                step(tt(x, x, parts[1], ALU.subtract))
                step(copy(parts[2], x))

            step(ts(w2.bitcast(I32), src_i, P - 1, None, ALU.bitwise_and))
            step(copy(bf[:, 9, :], w2.bitcast(I32)))
            v.wait_ge(cut_out, 1)
            step(ts(cut_s, w1, 0.5, 0.5, ALU.mult, ALU.add))
            step(ts(w2, ew, R_MAX, None, ALU.is_lt))
            step(tt(cut_s, cut_s, w2, ALU.mult))
            step(tt(w2, cut_s, same_s[:], ALU.mult))
            step(tt(cut_s, cut_s, first_s, ALU.mult))
            in_parts([bf[:, q, :] for q in (0, 1, 2)], ew)
            in_parts([bf[:, q, :] for q in (3, 4, 5)], w2)
            in_parts([bf[:, q, :] for q in (6, 7, 8)], cut_s)
            for l in range(3):
                step(tt(wprod[:, 3 * l * D:3 * (l + 1) * D].rearrange("p (c f) -> p c f", c=3),
                        we_bc[:, 3 * l * D:3 * (l + 1) * D].rearrange("p (c f) -> p c f", c=3),
                        ae_bc[:, l * D:(l + 1) * D].unsqueeze(1).broadcast_to([P, 3, D]), ALU.mult))
            step(reduce(col(VV, 9), wprod.rearrange("p (c f) -> p c f", f=D), AX.X, ALU.add))
            for l in range(3):
                for q, w in enumerate((f"L3_gnn_as{l + 1}", f"L3_gnn_ad{l + 1}")):
                    step(tt(wprod[:, (2 * l + q) * D:(2 * l + q + 1) * D], gat_w[:, l * D:(l + 1) * D], vec(V[w]), ALU.mult))
            step(reduce(gat_a[:], wprod[:, 0:6 * D].rearrange("p (c f) -> p c f", f=D), AX.X, ALU.add))
            v.wait_ge(pre_out, 1)
            step(ts(col(AMN, 3), PS[:, 1536:1539], 1.0 / E, None, ALU.mult))
            for l in range(3):
                step(tt(col(EDGE + 2, 3), col(AMN, 3), col(VV + 3 * l, 3), ALU.mult))
                step(reduce(col(AMEAN + l), col(EDGE + 2, 3), AX.X, ALU.add))
            step(copy(mats[:, M["ws"] * D:(M["wn"] + 1) * D], PS[:, 0:2 * D]))
            step(stt(bias_cols[:, 1:2], PS[:, 512:513], -LN2, bias_cols[:, 1:2], ALU.mult, ALU.add))
            step(ts(bias_cols[:, 2:4], bias_cols[:, 0:2], -1.0, 30.0, ALU.mult, ALU.add))
            step(copy(col(TOTAL), PS[:, 1024:1025]))
            step(ts(seg_s, seg_s, col(TOTAL), None, ALU.add), flats_ready)
            v.wait_ge(blocks_loaded, 64)
            step(copy(small[0:TB, 0:NB], blocks[:, 0, :, 0]))
            copy(seg0_blk[0:TB, :], small[0:TB, 0:NB]).then_inc(seg0_ready, 1)
            tt(blocks[:, 0, :, :], blocks[:, 0, :, :], small[0:TB, 0:NB].unsqueeze(2).broadcast_to([TB, NB, P]),
               ALU.subtract).then_inc(loc_ready, 1)
            for q, dst in enumerate((loc_t[:], dst_t, last_t, srcf_t)):
                base = 2048 + (q % 2) * 1024
                v.wait_ge(tiles_turned, q + 1)
                step(copy(dst[:, 0:4 * TB], PS[:, base:base + 4 * TB]))
                step(copy(dst[:, 4 * TB:ET], PS[:, base + 512:base + 512 + 3 * TB]), tiles_copied)
            step(copy(src_t[:], srcf_t))
            step(ts(srcf_t.bitcast(I32), src_t[:], 7, None, ALU.arith_shift_right))
            step(copy(srchi_t[:], srcf_t.bitcast(I32)))
            meta3 = meta_t.rearrange("p (e c) -> p e c", c=3)
            step(tt(meta3[:, :, 0], dst_t, last_t, ALU.mult))
            step(copy(srcf_t, pos_i))
            step(tt(meta3[:, :, 1], srcf_t, last_t, ALU.mult))
            step(memset(meta3[:, :, 2:3], 1.0), tiles_ready)

            def layer_input(k):
                step(reduce(stat0, X3, AX.X, ALU.add))
                step(ts(stat0, stat0, -1.0 / D, None, ALU.mult))
                step(tt(H3, X3, stat0.unsqueeze(2).broadcast_to([P, NT, D]), ALU.add))
                sq = acc[:, 0:NT * D]
                step(tt(sq, H[:, 0:NT * D], H[:, 0:NT * D], ALU.mult))
                reduce(stat1, sq.rearrange("p (t f) -> p t f", f=D), AX.X, ALU.add).then_inc(var_ready, 1)
                v.wait_ge(std_ready, vars_done(1))
                step(recip(stat1, stat1))
                step(stt(H3, H3, 0.0, stat1.unsqueeze(2).broadcast_to([P, NT, D]), ALU.max, ALU.mult), h_ready)

            def normalize(x, scratch, mean, var, h):
                tiles = [P, CH, D]
                step(reduce(mean, x, AX.X, ALU.add))
                step(ts(mean, mean, -1.0 / D, None, ALU.mult))
                step(tt(h, x, mean.unsqueeze(2).broadcast_to(tiles), ALU.add))
                step(tt(scratch, h, h, ALU.mult))
                reduce(var, scratch, AX.X, ALU.add).then_inc(var_ready, 1)
                v.wait_ge(std_ready, vars_done(1))
                step(recip(var, var))
                step(stt(h, h, 0.0, var.unsqueeze(2).broadcast_to(tiles), ALU.max, ALU.mult), h_chunks)

            def chunk_product(k, c):
                v.wait_ge(p_product, c + 1 + k * NCH)
                copy(T[:, c * CW:(c + 1) * CW], PS[:, 1024:1024 + CW]).then_inc(p_done, 1)

            n_vars = 0

            def vars_done(n):
                nonlocal n_vars
                n_vars += n
                return n_vars

            def rows_product(k):
                with v.Fori(0, NCH) as i:
                    v.wait_ge(p_product, i + 1 + k * NCH)
                    hold(v)
                    copy(T[:, ds(i * CW, CW)], PS[:, 1024:1024 + CW]).then_inc(p_done, 1)
                v.wait_ge(p_done, NCH + k * NCH)

            def zero_acc(k):
                step(memset(acc[:], 1.0 if k == 1 else 0.0))

            def make_onehot(k, i, h, loc):
                if k in GAT:
                    hold(v)
                    for j in range(HT):
                        e = i * BT + (h * HT + j)
                        last = ts(onehot[:, h * HT + j, :], iota_row[:], loc[:, ds(e, 1)], ex_t[:, ds(e, 1)],
                                  ALU.is_equal, ALU.mult)
                    last.then_inc(onehot_ready[h], 1)
                else:
                    tt(onehot[:, h * HT:(h + 1) * HT, :], iota_row[:].unsqueeze(1).broadcast_to([P, HT, D]),
                       loc[:, ds(i * BT + h * HT, HT)].unsqueeze(2).broadcast_to([P, HT, D]), ALU.is_equal)\
                        .then_inc(onehot_ready[h], 1)

            def add_windows(i, h, sums, after, first):
                for j in range(HT):
                    for windows, dst, done, before_pass in sums:
                        at = dst[:, ds(first[j], D)]
                        if j in after:
                            v.wait_ge(*after[j])
                        if j == 0:
                            v.wait_ge(done[1 - h], (i + h) * HT + before_pass)
                        else:
                            v.wait_ge(done[h], i * HT + j + before_pass)
                        tt(at, at, windows[:, j * D:(j + 1) * D], ALU.add).then_inc(done[h], 1)

            seg_regs = [v.alloc_register(f"segment{j}") for j in range(HT)]

            def tile_segments(i, h):
                v.load(seg_regs, seg0_row[0:1, ds(i * BT + h * HT, HT)])
                return [v.snap(r, min_val=0, max_val=ACCW - D) for r in seg_regs]

            def edge_pass(k):
                def add_half(i, h):
                    first = tile_segments(i, h)
                    ready = {0: (multiplied[h], i + 1 + turn[k] * ITERS)}
                    sums = [(PS[:, h * 1024:(h + 1) * 1024], acc, added, turn[k] * ITERS * HT)]
                    if k == 0:
                        sums.append((PS[0:3, 2048 + h * 1024:2048 + (h + 1) * 1024], macc, meta_added, 0))
                    add_windows(i, h, sums, ready, first)

                for h in range(2):
                    make_onehot(k, 0, h, loc_t)
                with v.Fori(0, ITERS - 1) as i:
                    for h in range(2):
                        add_half(i, h)
                        v.wait_ge(multiplied[h], i + 1 + turn[k] * ITERS)
                        make_onehot(k, i + 1, h, loc_t)
                for h in range(2):
                    add_half(ITERS - 1, h)

            def messages(i, h):
                if real(i):
                    v.wait_ge(attr_in[h], (i + 1) * 16 + (16 if isinstance(i, int) and i == ITERS - 1 and h else 0))
                    v.wait_ge(gathered[h], (i + 1) * (16 * HT) + 1 * (ITERS * 16 * HT))
                    wait(v, msg_turned, i * 2 + h - 1)
                    hold(v)
                    tt(half(msg0, h), half(attr, h), rows[:, h * HT:(h + 1) * HT, :].rearrange("p a b -> p (a b)"),
                       ALU.mult).then_inc(msg_ready, 1)

            def softplus(n, i, h):
                if real(i):
                    v.wait_ge(ln_done[n], i * 2 + h + 1)
                    stt(half(filt if n else rbf, h), banks(h), bias_cols[:, n:n + 1], half(lnp, h), ALU.add, ALU.max)\
                        .then_inc(soft_ready[n], 1)

            def feature_messages(i, h):
                v.wait_ge(msg_turned, i * 2 + h + 1)
                v.wait_ge(soft_ready[1], i * 2 + h + 1)
                wait(v, scanned, i * 2 + h - 1)
                hold(v)
                stt(half(msgf, h), half(filt, h), -LN2, banks(2 + h), ALU.add, ALU.mult).then_inc(msgf_ready, 1)

            def cutoffs(i, h, out, spread, done):
                v.wait_ge(spread, i * 2 + h + 1)
                tt(half(out, h), half(msgf, h), banks(2 + h), ALU.mult).then_inc(done, 1)

            def running_products(i, h):
                v.wait_ge(start_ready, i * 2 + h + 1)
                wait(v, scanned, i * 2 + h)
                wait(v, scan_turned, i * 2 + h - 1)
                hold(v)
                e = (h * HE - 1) % BE
                scan(half(prod, h), half(keep, h), half(msgf, h), prod[:, e:e + 1], ALU.mult, ALU.add)\
                    .then_inc(scanned, 1)

            def product_slot(i, h):
                before = (i + 1, 0) if h else (i, 1)
                softplus(0, *before)
                if real(i):
                    feature_messages(i, h)
                messages(*before)
                if real(i):
                    cutoffs(i, h, keep, keep_bc, keep_ready)
                    cutoffs(i, h, msgf, start_bc, start_ready)
                softplus(1, *before)
                if real(i):
                    running_products(i, h)

            def product_pass():
                step(memset(prod, 0.0))
                for i in (-1, 0):
                    for h in range(2):
                        product_slot(i, h)
                with v.Fori(1, ITERS - 2) as i:
                    for h in range(2):
                        product_slot(i, h)
                for i in (ITERS - 2, ITERS - 1):
                    for h in range(2):
                        product_slot(i, h)

            def segments_out(k):
                with v.Fori(0, NCH) as i:
                    v.wait_ge(c_product, i + 1 + turn[k] * NCH)
                    v.wait_ge(c_stored, i * 16 + turn[k] * (NCH * 16))
                    copy(stage_out, PS[:, 1024:1024 + CW]).then_inc(c_copied, 1)

            def segment_facts():
                v.wait_ge(info_turned, 1)
                facts = PS[:, 2560:2560 + 3 * NT].rearrange("p (t c) -> p t c", c=3)
                step(copy(info3[:, :, 2:4], facts[:, :, 1:3]))
                step(copy(info3[:, :, 0], ids_int[:]))
                step(stt(info3[:, :, 1], info3[:, :, 2], 1.0, info3[:, :, 3], ALU.add, ALU.subtract))
                step(ts(stat0, info3[:, :, 3], 0.0, BIGPOS, ALU.is_equal, ALU.mult))
                step(tt(stat0, stat0, facts[:, :, 0], ALU.add))
                step(copy(cmap[:], stat0), info_ready)

            def node_facts():
                v.wait_ge(info_loaded, 16)
                step(copy(firstpos[:], info3[:, :, 1]))
                step(copy(lastpos[:], info3[:, :, 2]))
                step(ts(rcount[:], info3[:, :, 3], 1.0, None, ALU.max))
                step(recip(rcount[:], rcount[:]))
                step(copy(cmap[:], info3[:, :, 0]), info_cols)

            def chunk(buf3, c):
                return buf3[:, c * CH:(c + 1) * CH, :]

            def mean_layer(k):
                for c in range(NCH):
                    g = chunk(G3, c)
                    v.wait_ge(node_rows[c], (k + 1) * CH * 16)
                    step(tt(g, g, rcount[:, c * CH:(c + 1) * CH].unsqueeze(2).broadcast_to([P, CH, D]), ALU.mult))
                    step(tt(g, g, chunk(T3, c), ALU.add))
                    step(tt(g, g, vec_nodes(bias_vec[k], CH), ALU.add))
                    x = chunk(X3, c)
                    if k == 0:
                        step(stt(x, g, 0.0, x, ALU.max, ALU.add))
                    elif k == 4:
                        step(tt(x, g, x, ALU.add))
                    else:
                        step(ts(chunk(H3, c), g, 0.0, None, ALU.max), h_chunks)
                    if k in (0, 4):
                        w = slice(c * CH, (c + 1) * CH)
                        normalize(x, g, stat0[:, w], stat1[:, w], chunk(H3, c))
                    if k > 0 and c > 0:
                        chunk_product(k + 1, c - 1)
                if k > 0:
                    chunk_product(k + 1, NCH - 1)
                    v.wait_ge(p_done, NCH + (k + 1) * NCH)

            def product_layer():
                step(tt(T3, T3, vec_nodes(bias_vec[1]), ALU.add))
                ts(G[:], T[:], 30.0, None, ALU.min).then_inc(ln_in, 1)
                v.wait_ge(ln_out, 1)
                step(tt(T[:], T[:], G[:], ALU.max))
                step(stt(X[:], T[:], -LN2, X[:], ALU.add, ALU.add))

            n_carry = 0

            def linked_scan(dst, d0, d1, ops, whole, start, backward=False):
                nonlocal n_carry
                n_carry += 1
                r = (lambda x: x[:, ::-1]) if backward else (lambda x: x)
                end = dst[:, 0:1] if backward else dst[:, ET - 1:ET]
                step(scan(r(dst), r(d0), r(d1), start, *ops))
                step(copy(carry_cols[:, 0:1], end))
                copy(carry_cols[:, 1:2], whole).then_inc(carry_in_ready, 1)
                v.wait_ge(carry_rows, n_carry)
                step(copy(carry_row[:, 0:2 * P], PS[0:1, 3072:3072 + 2 * P]))
                f, w, o, z = (carry_row[:, i * P:(i + 1) * P] for i in range(4))
                step(scan(r(o), r(w), r(f), start, *ops))
                step(memset(z[:, P - 1:P] if backward else z[:, 0:1], start))
                if backward:
                    step(copy(z[:, 0:P - 1], o[:, 1:P]), carry_scanned)
                else:
                    step(copy(z[:, 1:P], o[:, 0:P - 1]), carry_scanned)
                v.wait_ge(carry_cols_out, n_carry)
                step(copy(carry_in[:], PS[:, 3584:3585]))
                return r(dst), r(d0), r(d1), carry_in[:], *ops

            def attention(k):
                l = k - 5
                step(memset(attr_att, 0.0), attr_space)
                v.wait_ge(p_product, (k + 1) * NCH)
                node_scalars = PS[:, 2048:2048 + 2 * NT].rearrange("p (t c) -> p t c", c=2)
                step(copy(als_n, node_scalars[:, :, 0]))
                step(copy(ald_n, node_scalars[:, :, 1]))
                step(tt(self_n, als_n, ald_n, ALU.add))
                step(ts(self_n, self_n, col(AMEAN + l), None, ALU.add))
                step(stt(self_n, self_n, 0.2, self_n, ALU.mult, ALU.max))
                step(copy(stat0, als_n))
                in_parts([als_bf[:, q * NT:(q + 1) * NT] for q in range(3)], stat0)
                step(copy(nd3[:, :, 0], ald_n))
                step(copy(nd3[:, :, 1], self_n), first_in)
                def make_lo(i, h):
                    v.wait_ge(lo_bc[h], i + 1 + l * ITERS)
                    v.wait_ge(al_rows[h], i + l * ITERS)
                    hold(v)
                    ts(hot_bf[:, h, :, :].rearrange("p a b -> p (a b)"), PS[:, h * 1024:(h + 1) * 1024], iota_col[:],
                       None, ALU.is_equal).then_inc(lo_hot[h], 1)

                def pick(i, h):
                    at = l * ITERS + i
                    mask = Hs[h][:, 0:HT * NT].rearrange("p (t c) -> p t c", c=NT)
                    cand = PS[:, (4 + h) * 512:(4 + h) * 512 + HT * NT].rearrange("p (t c) -> p t c", c=NT)
                    v.wait_ge(al_done[h], at)
                    tt(mask, iota_row[:, 0:NT].unsqueeze(1).broadcast_to([P, HT, NT]),
                       srchi_t[:, ds(i * BT + h * HT, HT)].unsqueeze(2).broadcast_to([P, HT, NT]), ALU.is_equal)\
                        .then_inc(al_mask[h], 1)
                    v.wait_ge(al_mask[h], at + 1)
                    v.wait_ge(al_rows[h], at + 1)
                    hold(v)
                    tt(mask, mask, cand, ALU.mult).then_inc(al_pick[h], 1)
                    v.wait_ge(al_pick[h], at + 1)
                    hold(v)
                    reduce(als_t[:, ds(i * BT + h * HT, HT)], mask, AX.X, ALU.add).then_inc(al_done[h], 1)

                make_lo(0, 0)
                with v.Fori(0, ITERS - 1) as i:
                    make_lo(i, 1)
                    pick(i, 0)
                    make_lo(i + 1, 0)
                    pick(i, 1)
                make_lo(ITERS - 1, 1)
                pick(ITERS - 1, 0)
                pick(ITERS - 1, 1)
                v.wait_ge(turn_out, l + 1)
                step(copy(turned, PS[0:TB, 3072:3072 + NB * P]), turn_blk)
                v.wait_ge(attr_again, 32 * (l + 1))
                step(ts(Gs[5], attr3[:, :, 0], col(VV + 3 * l), None, ALU.mult))
                for c in (1, 2):
                    step(stt(Gs[5], attr3[:, :, c], col(VV + 3 * l + c), Gs[5], ALU.mult, ALU.add))
                v.wait_ge(first_ld, 16 * (l + 1))
                add, spread = (ALU.add, ALU.max), (ALU.mult, ALU.add)
                step(scan(*linked_scan(Gs[3], same_s[:], at_f[:, :, 0], spread, col(ALLSAME), 0.0)))
                step(scan(*linked_scan(Gs[4], same_s[:], at_f[:, :, 1], spread, col(ALLSAME), 0.0)))
                v.wait_ge(al_loaded, 16 * (l + 1))
                step(tt(Gs[0], Gs[0], Gs[3], ALU.add))
                step(tt(Gs[0], Gs[0], Gs[5], ALU.add))
                step(stt(Gs[0], Gs[0], 0.2, Gs[0], ALU.mult, ALU.max))
                step(ts(Gs[5], same_s[:], -1.0, HUGE, ALU.add, ALU.mult))
                step(scan(*linked_scan(Gs[6], Gs[5], Gs[0], add, col(PENALL), -HUGE)))
                step(tt(Gs[6], Gs[6], last_s[:], ALU.mult))
                step(ts(Gs[5], last_s[:], -1.0, 1.0, ALU.mult, ALU.add))
                step(scan(*linked_scan(Gs[7], Gs[5], Gs[6], spread, col(NOLAST), 0.0, backward=True)))
                step(tt(at_l[:, :, 1], Gs[7], Gs[4], ALU.max))
                step(tt(Gs[5], Gs[0], at_l[:, :, 1], ALU.subtract), exp_in)
                v.wait_ge(exp_out, l + 1)
                step(scan(*linked_scan(at_l[:, :, 0], same_s[:], Gs[6], spread, col(ALLSAME), 0.0)), last_in)
                v.wait_ge(ex_turned, l + 1)
                step(copy(ex_t[:, 0:4 * TB], PS[:, 2048:2048 + 4 * TB]))
                step(copy(ex_t[:, 4 * TB:ET], PS[:, 2560:2560 + 3 * TB]))
                step(memset(nd3[:, :, 0:1], 0.0))
                step(memset(nd3[:, :, 1:2], -HUGE), last_fill)

            def attention_layer(k):
                l = k - 5
                v.wait_ge(last_ga, 16 * NT * (l + 1))
                step(tt(amax_n, nd3[:, :, 1], self_n, ALU.max))
                step(tt(exs_n, self_n, amax_n, ALU.subtract), self_in)
                v.wait_ge(self_out, l + 1)
                step(tt(rden_n, nd3[:, :, 0], exs_n, ALU.add))
                step(ts(rden_n, rden_n, 1e-16, None, ALU.add))
                step(recip(rden_n, rden_n))
                step(tt(T3, T3, exs_n.unsqueeze(2).broadcast_to([P, NT, D]), ALU.mult))
                for c in range(NCH):
                    g = chunk(G3, c)
                    v.wait_ge(node_rows[c], (k + 1) * CH * 16)
                    step(tt(g, g, chunk(T3, c), ALU.add))
                    step(tt(g, g, rden_n[:, c * CH:(c + 1) * CH].unsqueeze(2).broadcast_to([P, CH, D]), ALU.mult))
                    step(tt(g, g, vec_nodes(bias_vec[k], CH), ALU.add))
                    lastt = H3[:, NT - 1, :]
                    if c < NCH - 1:
                        step(stt(chunk(H3, c), g, 0.01, g, ALU.mult, ALU.max), sum_in)
                    else:
                        step(stt(chunk(H3, c), g, 0.01, g, ALU.mult, ALU.max))
                        step(ts(lastt, lastt, rowmask[:], None, ALU.mult), sum_in)
                nm, s1, sd = (acc[:, i * D:(i + 1) * D] for i in (1, 2, 3))
                v.wait_ge(sum_out, 2 * l + 1)
                step(ts(nm, PS[:, 0:D], -1.0 / N, None, ALU.mult))
                for c in range(NCH):
                    h = chunk(H3, c)
                    if c < NCH - 1:
                        step(tt(h, h, nm.unsqueeze(1).broadcast_to([P, CH, D]), ALU.add), sum_in)
                    else:
                        step(tt(h, h, nm.unsqueeze(1).broadcast_to([P, CH, D]), ALU.add))
                        step(ts(lastt, lastt, rowmask[:], None, ALU.mult), sum_in)
                v.wait_ge(sum_out, 2 * l + 2)
                step(copy(s1, PS[:, 0:D]), var_ready)
                v.wait_ge(std_ready, vars_done(1))
                step(recip(sd, sd))
                step(tt(sd, sd, vec(V[f"L3_gnn_g{l + 1}"]), ALU.mult))
                for c in range(NCH):
                    h, x = chunk(H3, c), chunk(X3, c)
                    step(tt(h, h, sd.unsqueeze(1).broadcast_to([P, CH, D]), ALU.mult))
                    if k < K - 1:
                        step(tt(h, h, vec_nodes(V[f"L3_gnn_be{l + 1}"], CH), ALU.add), h_chunks)
                        if c > 0:
                            chunk_product(k + 1, c - 1)
                    else:
                        step(tt(h, h, vec_nodes(V[f"L3_gnn_be{l + 1}"], CH), ALU.add))
                        step(tt(x, x, h, ALU.add), out_ready)
                if k < K - 1:
                    chunk_product(k + 1, NCH - 1)
                    v.wait_ge(p_done, NCH + (k + 1) * NCH)

            v.wait_ge(seg0_loaded, 16)
            for k in range(K):
                if k in (0, 2):
                    layer_input(k)
                if k not in by_chunks:
                    rows_product(k)
                if k in GAT:
                    attention(k)
                zero_acc(k)
                v.wait_ge(table_stored, 16 * table_parts[k])
                if k == 0:
                    step(memset(macc, 0.0))
                if k == 1:
                    product_pass()
                    rows_product(1)
                    product_layer()
                    continue
                else:
                    edge_pass(k)
                if k == 0:
                    segment_facts()
                segments_out(k)
                if k == 0:
                    node_facts()
                if k in SAGE:
                    mean_layer(k)
                else:
                    attention_layer(k)


CONSTS = 9
LOADS = 12 + 20 + 11 + 9 + 2
_NAMES = ["x", "src", "dst", "edge_attr_128", "edge_attr_3", "edge_weight", "L0_gnn_W_self", "L0_gnn_W_neigh",
          "L0_gnn_bias", "L1_gnn_W1", "L1_gnn_b1", "L1_gnn_W2", "L1_gnn_b2", "L1_gnn_W3", "L1_gnn_b3",
          "L2_gnn_W_agg", "L2_gnn_W_root", "L2_gnn_b"]
_NAMES += [f"L3_gnn_{n}{l}" for l in (1, 2, 3) for n in ("W", "as", "ad", "We", "ae", "b", "g", "be")]


def kernel(**inputs):
    import concourse.bacc as _bacc
    from concourse.bass_utils import run_bass_kernel_spmd as _run

    nc = _bacc.Bacc("TRN2", target_bir_lowering=False, num_devices=1)
    arrays, aps = {}, {}
    for name in _NAMES:
        x = np.ascontiguousarray(inputs[name])
        arrays[f"in_{name}"] = x
        aps[name] = nc.dram_tensor(f"in_{name}", x.shape, mybir.dt.from_np(x.dtype), kind="ExternalInput").ap()
    out = nc.dram_tensor("out_x", (N, D), F32, kind="ExternalOutput").ap()
    build(nc, aps, out)
    r = _run(nc, [arrays], core_ids=[0])
    return r.results[0]["out_x"]
```
